# Optimizing a Trainium2 kernel written in Bass

```python
import numpy as np
import jax
import jax.numpy as jnp

def _softmax(x, axis=-1):
    return jax.nn.softmax(x, axis=axis)

def _gelu(x):
    return jax.nn.gelu(x, approximate=True)

def _silu(x):
    return jax.nn.silu(x)

def _sigmoid(x):
    return jax.nn.sigmoid(x)

def _layernorm(x, axis=-1, eps=1e-05):
    m = jnp.mean(x, axis=axis, keepdims=True)
    v = jnp.var(x, axis=axis, keepdims=True)
    return (x - m) / jnp.sqrt(v + eps)

def _scatter_add(tgt, idx, src, axis=0):
    return tgt.at[idx].add(src)

def _segment_sum(src, seg, n):
    return jax.ops.segment_sum(src, seg, n)
kernel_name = 'mk_adaln_ffn_d1_seqx_r4_edb92c'

def setup_inputs(seed: int=0):
    np.random.seed(seed)
    _w = jnp.asarray

    def _rec_inputs():
        import jax
        import jax.numpy as jnp
        _rk = jax.random.key(seed)
        x = 7.22e-05 + 1 * jax.random.normal(jax.random.fold_in(_rk, 1), (2, 1024, 256), jnp.float32)
        _lenS = 1024 - jax.random.randint(jax.random.fold_in(_rk, 7), (2,), 0, max(1, 1024 // 4) + 1, jnp.int32)
        _lenS2 = 1024 - jax.random.randint(jax.random.fold_in(_rk, 8), (2,), 0, max(1, 1024 // 4) + 1, jnp.int32)
        itok_BxS_0_999 = jax.random.randint(jax.random.fold_in(_rk, 11), (2, 1024), 0, 250, jnp.int32)
        itok_BxS_0_4 = jax.random.randint(jax.random.fold_in(_rk, 12), (2, 1024), 0, 5, jnp.int32)
        cond_512 = 0.00199304 + 1.00034 * jax.random.normal(jax.random.fold_in(_rk, 14), (2, 128), jnp.float32)
        cond_64 = 0.0990542 + 1.04422 * jax.random.normal(jax.random.fold_in(_rk, 15), (2, 64), jnp.float32)
        fside_Bx32_0 = -0.136436 + 0.990155 * jax.random.normal(jax.random.fold_in(_rk, 16), (2, 32), jnp.float32)
        _validS = jnp.arange(1024)[None, :] < _lenS[:, None]
        _validS2 = jnp.arange(1024)[None, :] < _lenS2[:, None]
        _causal = jnp.tril(jnp.ones((1024, 1024), dtype=bool))
        mask_BxS_ik0 = jnp.where(jnp.broadcast_to(_validS[:, :], (2, 1024)), 0, 1).astype(jnp.int32)
        return (x, itok_BxS_0_999, itok_BxS_0_4, cond_512, cond_64, fside_Bx32_0, mask_BxS_ik0)
    x, itok_BxS_0_999, itok_BxS_0_4, cond_512, cond_64, fside_Bx32_0, mask_BxS_ik0 = _rec_inputs()

    def _L0_cond_setup():
        import jax, jax.numpy as jnp
        import numpy as np
        EPS = 1e-05

        def _ln(x, g, b):
            m = jnp.mean(x, axis=-1, keepdims=True)
            v = jnp.mean((x - m) ** 2, axis=-1, keepdims=True)
            return (x - m) * jax.lax.rsqrt(v + EPS) * g + b

        def _mlp_ln(s, W1, b1, W2, b2, g, b):
            h = jax.nn.silu(s @ W1 + b1) @ W2 + b2
            return _ln(h, g, b)
        key = jax.random.key(seed)
        B, S, D = (4, 512, 256)
        MEM, NOI, RES = (128, 64, 32)
        ks = jax.random.split(key, 40)
        ki = iter(range(40))

        def nrm(shape, scale=0.02):
            return jax.random.normal(ks[next(ki)], shape, jnp.float32) * scale

        def gamma(shape):
            return jnp.ones(shape, jnp.float32) + nrm(shape)
        inp = {'x': jax.random.normal(ks[next(ki)], (B, S, D), jnp.float32), 'pathway_ids': jax.random.randint(ks[next(ki)], (B, S), 0, 250), 'compartment_ids': jax.random.randint(ks[next(ki)], (B, S), 0, 5), 'time_steps': jax.random.randint(ks[next(ki)], (B, S), 0, 5), 'scale_type': jax.random.randint(ks[next(ki)], (B, S), 0, 3), 'memory_state': jax.random.normal(ks[next(ki)], (B, MEM), jnp.float32), 'noise_state': jax.random.normal(ks[next(ki)], (B, NOI), jnp.float32), 'resource_state': jax.random.normal(ks[next(ki)], (B, RES), jnp.float32), 'pw_g': gamma((250, D)), 'pw_b': nrm((250, D)), 'cp_g': gamma((5, D)), 'cp_b': nrm((5, D)), 'tm_g': gamma((5, D)), 'tm_b': nrm((5, D)), 'ms_g': gamma((3, D)), 'ms_b': nrm((3, D)), 'mem_W1': nrm((MEM, D)), 'mem_b1': jnp.zeros((D,)), 'mem_W2': nrm((D, D)), 'mem_b2': jnp.zeros((D,)), 'mem_g': gamma((D,)), 'mem_be': jnp.zeros((D,)), 'noi_W1': nrm((NOI, D)), 'noi_b1': jnp.zeros((D,)), 'noi_W2': nrm((D, D)), 'noi_b2': jnp.zeros((D,)), 'noi_g': gamma((D,)), 'noi_be': jnp.zeros((D,)), 'res_W1': nrm((RES, D)), 'res_b1': jnp.zeros((D,)), 'res_W2': nrm((D, D)), 'res_b2': jnp.zeros((D,)), 'res_g': gamma((D,)), 'res_be': jnp.zeros((D,)), 'int_W1': nrm((6 * D, D)), 'int_b1': jnp.zeros((D,)), 'int_W2': nrm((D, D)), 'int_b2': jnp.zeros((D,)), 'int_g': gamma((D,)), 'int_be': jnp.zeros((D,)), 'aw': jnp.ones((6,), jnp.float32) / 6.0}
        return inp
    _L0_cond_all = _L0_cond_setup()
    _L0_cond_in = {k: v for k, v in _L0_cond_all.items() if k in ('pw_g', 'pw_b', 'cp_g', 'cp_b', 'tm_g', 'tm_b', 'ms_g', 'ms_b', 'mem_W1', 'mem_b1', 'mem_W2', 'mem_b2', 'mem_g', 'mem_be', 'noi_W1', 'noi_b1', 'noi_W2', 'noi_b2', 'noi_g', 'noi_be', 'res_W1', 'res_b1', 'res_W2', 'res_b2', 'res_g', 'res_be', 'int_W1', 'int_b1', 'int_W2', 'int_b2', 'int_g', 'int_be', 'aw')}
    del _L0_cond_all

    def _L0_ffn_setup():
        import jax, jax.numpy as jnp
        import numpy as np
        E, K, H, I = (8, 2, 256, 896)
        key = jax.random.key(seed)
        k0, k1, k2, k3, k4 = jax.random.split(key, 5)
        scale = 0.02
        return {'hidden_states': jax.random.normal(k0, (2, 256, H), dtype=jnp.float32), 'w_gate': jax.random.normal(k1, (E, H), dtype=jnp.float32) * scale, 'w1': jax.random.normal(k2, (E, I, H), dtype=jnp.float32) * scale, 'w3': jax.random.normal(k3, (E, I, H), dtype=jnp.float32) * scale, 'w2': jax.random.normal(k4, (E, H, I), dtype=jnp.float32) * scale}
    _L0_ffn_all = _L0_ffn_setup()
    _L0_ffn_in = {k: v for k, v in _L0_ffn_all.items() if k in ('w_gate', 'w1', 'w3', 'w2')}
    del _L0_ffn_all
    return {'x': x, 'itok_BxS_0_999': itok_BxS_0_999, 'itok_BxS_0_4': itok_BxS_0_4, 'cond_512': cond_512, 'cond_64': cond_64, 'fside_Bx32_0': fside_Bx32_0, 'mask_BxS_ik0': mask_BxS_ik0, 'L0_cond_pw_g': _L0_cond_in['pw_g'], 'L0_cond_pw_b': _L0_cond_in['pw_b'], 'L0_cond_cp_g': _L0_cond_in['cp_g'], 'L0_cond_cp_b': _L0_cond_in['cp_b'], 'L0_cond_tm_g': _L0_cond_in['tm_g'], 'L0_cond_tm_b': _L0_cond_in['tm_b'], 'L0_cond_ms_g': _L0_cond_in['ms_g'], 'L0_cond_ms_b': _L0_cond_in['ms_b'], 'L0_cond_mem_W1': _L0_cond_in['mem_W1'], 'L0_cond_mem_b1': _L0_cond_in['mem_b1'], 'L0_cond_mem_W2': _L0_cond_in['mem_W2'], 'L0_cond_mem_b2': _L0_cond_in['mem_b2'], 'L0_cond_mem_g': _L0_cond_in['mem_g'], 'L0_cond_mem_be': _L0_cond_in['mem_be'], 'L0_cond_noi_W1': _L0_cond_in['noi_W1'], 'L0_cond_noi_b1': _L0_cond_in['noi_b1'], 'L0_cond_noi_W2': _L0_cond_in['noi_W2'], 'L0_cond_noi_b2': _L0_cond_in['noi_b2'], 'L0_cond_noi_g': _L0_cond_in['noi_g'], 'L0_cond_noi_be': _L0_cond_in['noi_be'], 'L0_cond_res_W1': _L0_cond_in['res_W1'], 'L0_cond_res_b1': _L0_cond_in['res_b1'], 'L0_cond_res_W2': _L0_cond_in['res_W2'], 'L0_cond_res_b2': _L0_cond_in['res_b2'], 'L0_cond_res_g': _L0_cond_in['res_g'], 'L0_cond_res_be': _L0_cond_in['res_be'], 'L0_cond_int_W1': _L0_cond_in['int_W1'], 'L0_cond_int_b1': _L0_cond_in['int_b1'], 'L0_cond_int_W2': _L0_cond_in['int_W2'], 'L0_cond_int_b2': _L0_cond_in['int_b2'], 'L0_cond_int_g': _L0_cond_in['int_g'], 'L0_cond_int_be': _L0_cond_in['int_be'], 'L0_cond_aw': _L0_cond_in['aw'], 'L0_ffn_w_gate': _L0_ffn_in['w_gate'], 'L0_ffn_w1': _L0_ffn_in['w1'], 'L0_ffn_w3': _L0_ffn_in['w3'], 'L0_ffn_w2': _L0_ffn_in['w2']}

def reference(x, itok_BxS_0_999, itok_BxS_0_4, cond_512, cond_64, fside_Bx32_0, mask_BxS_ik0, L0_cond_pw_g, L0_cond_pw_b, L0_cond_cp_g, L0_cond_cp_b, L0_cond_tm_g, L0_cond_tm_b, L0_cond_ms_g, L0_cond_ms_b, L0_cond_mem_W1, L0_cond_mem_b1, L0_cond_mem_W2, L0_cond_mem_b2, L0_cond_mem_g, L0_cond_mem_be, L0_cond_noi_W1, L0_cond_noi_b1, L0_cond_noi_W2, L0_cond_noi_b2, L0_cond_noi_g, L0_cond_noi_be, L0_cond_res_W1, L0_cond_res_b1, L0_cond_res_W2, L0_cond_res_b2, L0_cond_res_g, L0_cond_res_be, L0_cond_int_W1, L0_cond_int_b1, L0_cond_int_W2, L0_cond_int_b2, L0_cond_int_g, L0_cond_int_be, L0_cond_aw, L0_ffn_w_gate, L0_ffn_w1, L0_ffn_w3, L0_ffn_w2):
    import jax
    import jax.numpy as jnp

    def _L0_cond_ref(x, pathway_ids, compartment_ids, time_steps, scale_type, memory_state, noise_state, resource_state, pw_g, pw_b, cp_g, cp_b, tm_g, tm_b, ms_g, ms_b, mem_W1, mem_b1, mem_W2, mem_b2, mem_g, mem_be, noi_W1, noi_b1, noi_W2, noi_b2, noi_g, noi_be, res_W1, res_b1, res_W2, res_b2, res_g, res_be, int_W1, int_b1, int_W2, int_b2, int_g, int_be, aw):
        import jax, jax.numpy as jnp
        import numpy as np
        EPS = 1e-05

        def _ln(x, g, b):
            m = jnp.mean(x, axis=-1, keepdims=True)
            v = jnp.mean((x - m) ** 2, axis=-1, keepdims=True)
            return (x - m) * jax.lax.rsqrt(v + EPS) * g + b

        def _mlp_ln(s, W1, b1, W2, b2, g, b):
            h = jax.nn.silu(s @ W1 + b1) @ W2 + b2
            return _ln(h, g, b)
        h = _ln(x, pw_g[pathway_ids], pw_b[pathway_ids])
        h = _ln(h, cp_g[compartment_ids], cp_b[compartment_ids])
        t = _ln(x, tm_g[time_steps], tm_b[time_steps])
        m = x + _mlp_ln(memory_state, mem_W1, mem_b1, mem_W2, mem_b2, mem_g, mem_be)[:, None, :]
        n = x + _mlp_ln(noise_state, noi_W1, noi_b1, noi_W2, noi_b2, noi_g, noi_be)[:, None, :]
        r = x + _mlp_ln(resource_state, res_W1, res_b1, res_W2, res_b2, res_g, res_be)[:, None, :]
        s = _ln(x, ms_g[scale_type], ms_b[scale_type])
        w = jax.nn.softmax(aw)
        cat = jnp.concatenate([w[0] * h, w[1] * t, w[2] * m, w[3] * n, w[4] * r, w[5] * s], axis=-1)
        return _mlp_ln(cat, int_W1, int_b1, int_W2, int_b2, int_g, int_be)

    def _L0_ffn_ref(hidden_states, w_gate, w1, w3, w2):
        import jax, jax.numpy as jnp
        import numpy as np
        E, K, H, I = (8, 2, 256, 896)
        B, S, Hd = hidden_states.shape
        x = hidden_states.reshape(-1, Hd)
        logits = jnp.einsum('th,eh->te', x, w_gate)
        probs = jax.nn.softmax(logits, axis=-1)
        topw, topi = jax.lax.top_k(probs, K)
        topw = topw / jnp.sum(topw, axis=-1, keepdims=True)
        comb = jnp.sum(jax.nn.one_hot(topi, E, dtype=x.dtype) * topw[..., None], axis=1)
        g = jnp.einsum('th,eih->eti', x, w1)
        u = jnp.einsum('th,eih->eti', x, w3)
        h = jax.nn.silu(g) * u
        out = jnp.einsum('eti,ehi->eth', h, w2)
        y = jnp.einsum('te,eth->th', comb, out)
        return y.reshape(B, S, Hd)
    x = x + _L0_ffn_ref(_L0_cond_ref(x, itok_BxS_0_999, itok_BxS_0_4, itok_BxS_0_4, mask_BxS_ik0, cond_512, cond_64, fside_Bx32_0, L0_cond_pw_g, L0_cond_pw_b, L0_cond_cp_g, L0_cond_cp_b, L0_cond_tm_g, L0_cond_tm_b, L0_cond_ms_g, L0_cond_ms_b, L0_cond_mem_W1, L0_cond_mem_b1, L0_cond_mem_W2, L0_cond_mem_b2, L0_cond_mem_g, L0_cond_mem_be, L0_cond_noi_W1, L0_cond_noi_b1, L0_cond_noi_W2, L0_cond_noi_b2, L0_cond_noi_g, L0_cond_noi_be, L0_cond_res_W1, L0_cond_res_b1, L0_cond_res_W2, L0_cond_res_b2, L0_cond_res_g, L0_cond_res_be, L0_cond_int_W1, L0_cond_int_b1, L0_cond_int_W2, L0_cond_int_b2, L0_cond_int_g, L0_cond_int_be, L0_cond_aw), L0_ffn_w_gate, L0_ffn_w1, L0_ffn_w3, L0_ffn_w2)
    return x

_drawn_inputs = setup_inputs


def setup_inputs(seed=0):
    import zlib

    import numpy as np

    out = dict(_drawn_inputs(seed))
    spreads = {'L0_cond_mem_b1': (0.0, 0.8),
     'L0_cond_mem_b2': (0.0, 0.8),
     'L0_cond_mem_be': (0.0, 0.8),
     'L0_cond_noi_b1': (0.0, 0.8),
     'L0_cond_noi_b2': (0.0, 0.8),
     'L0_cond_noi_be': (0.0, 0.8),
     'L0_cond_res_b1': (0.0, 0.8),
     'L0_cond_res_b2': (0.0, 0.8),
     'L0_cond_res_be': (0.0, 0.8),
     'L0_cond_int_b1': (0.0, 0.8),
     'L0_cond_int_b2': (0.0, 0.1),
     'L0_cond_int_be': (0.0, 0.8),
     'L0_cond_aw': (0.1666666716337204, 0.6)}
    factors = {'cond_512': 8.0,
     'cond_64': 8.0,
     'fside_Bx32_0': 8.0,
     'L0_cond_pw_g': 8.0,
     'L0_cond_pw_b': 8.0,
     'L0_cond_cp_g': 8.0,
     'L0_cond_cp_b': 8.0,
     'L0_cond_tm_g': 8.0,
     'L0_cond_tm_b': 8.0,
     'L0_cond_ms_g': 8.0,
     'L0_cond_ms_b': 8.0,
     'L0_cond_mem_W1': 8.0,
     'L0_cond_mem_W2': 8.0,
     'L0_cond_mem_g': 8.0,
     'L0_cond_noi_W1': 8.0,
     'L0_cond_noi_W2': 8.0,
     'L0_cond_noi_g': 8.0,
     'L0_cond_res_W1': 8.0,
     'L0_cond_res_W2': 8.0,
     'L0_cond_res_g': 8.0,
     'L0_cond_int_W1': 6.77,
     'L0_cond_int_W2': 5.898,
     'L0_cond_int_g': 8.0,
     'L0_ffn_w1': 2.675}
    for name, (base, spread) in spreads.items():
        noise = np.random.default_rng([zlib.crc32(name.encode()), seed]).standard_normal(out[name].shape)
        drawn = base * np.exp(spread * noise) if base else spread * noise
        out[name] = jnp.asarray(drawn.astype(out[name].dtype))
    for name, factor in factors.items():
        out[name] = (out[name] * factor).astype(out[name].dtype)
    return out
```

```python
from contextlib import ExitStack

import numpy as np
import concourse.bass as bass
from concourse import mybir

ALU = mybir.AluOpType
ACT = mybir.ActivationFunctionType
AX = mybir.AxisListType
F32 = mybir.dt.float32
BF16 = mybir.dt.bfloat16
I32 = mybir.dt.int32
U32 = mybir.dt.uint32

P = 128
B, S, D = 2, 1024, 256
T = B * S
NTOK = T // P
DC = D // P
E, I, K = 8, 896, 2
IC = I // P
NCOMP, NSCALE = 5, 3
ROWS = NCOMP + NSCALE + B
PARTS = 3
KR = 32 * (PARTS - 1) + ROWS
NPW = 250
EPS = 1e-5

REGION = T + P
NT = (K * T + E * (P - 1)) // P
ROW = D + 2
WEXP = 2 * DC * I + IC * D
HALF = ((0, 4), (4, IC))
EARLY = 6
PIECE = EARLY * WEXP // NTOK


class Tile:

    def __init__(self, pair, parity):
        self.pair, self.parity = pair, parity

    def plus(self, d):
        q = self.parity + d
        return Tile(self.pair + q // 2, q % 2)

    def at(self, scale=1, offset=0):
        return self.pair * (2 * scale) + (self.parity * scale + offset)

    def inside(self, n):
        return not isinstance(self.pair, int) or 0 <= self.at() < n

    def is_first(self, n=1):
        return isinstance(self.pair, int) and self.at() < n


def pipeline(engine, body, first, last, head, tail):
    lo, hi = first + head, last - tail
    for n in range(first, lo):
        body(Tile(n // 2, n % 2))
    with engine.Fori(lo // 2, lo // 2 + (hi - lo) // 2) as pair:
        body(Tile(pair, 0).plus(lo % 2))
        body(Tile(pair, 0).plus(lo % 2 + 1))
    for n in range(hi, last):
        body(Tile(n // 2, n % 2))


def side_by_side(*chains):
    chains = list(chains)
    while chains:
        for chain in tuple(chains):
            if next(chain, done_) is done_:
                chains.remove(chain)


done_ = object()


def adaln_moe(nc, a, out, routed):
    with ExitStack() as ctx:
        def sb(name, shape, dt=F32):
            return ctx.enter_context(nc.sbuf_tensor(name, shape, dt))

        def sem(name):
            return ctx.enter_context(nc.semaphore(name))

        ident = sb("ident", [P, P])
        before = sb("before", [P, P], BF16)
        ones = sb("ones", [P, P], BF16)
        before_f = sb("before_f", [P, P])
        small = sb("small", [P, 2 * E + 2 + NTOK])
        iota_e = small[:, 0:E]
        region_e = small[:, E:2 * E]
        e_base = small[:, 2 * E:2 * E + 1]
        row_id = small[:, 2 * E + 1:2 * E + 2]
        token_id = small[:, 2 * E + 2:2 * E + 2 + NTOK]
        pad_rows = sb("pad_rows", [P, ROW])
        ln_gb = sb("ln_gb", [P, 2, DC])
        wgate = sb("wgate", [P, DC, E])
        pw_ids = sb("pw_ids", [P, NTOK], I32)
        pw_idx = [sb(f"pw_idx{p}", [P, 1], I32) for p in range(2)]
        minus_half = sb("minus_half", [P, NTOK])
        gates = sb("gates", [KR, 4 * D], BF16)
        shifts = sb("shifts", [KR, D], BF16)

        w_all = sb("w_all", [P, E * WEXP])
        at = [EARLY * WEXP]

        def place(n, dt=F32):
            v = w_all[:, at[0]:at[0] + n]
            at[0] += n
            return v if dt == F32 else v.bitcast(dt)

        x_all = place(NTOK * D).rearrange("p (t d) -> p t d", d=D)
        onehot = place(T // 2, BF16)
        w_in = place(12 * D).rearrange("p (c d) -> p c d", d=D)
        w_out = place(DC * D).rearrange("p (c d) -> p c d", d=D)
        gate_s = place(3 * D)
        s1 = place(D)
        s1_t = place(D).rearrange("p (c t) -> p c t", t=P)
        y_t = place(D).rearrange("p (c t) -> p c t", t=P)
        assert at[0] <= E * WEXP
        at[0] = PIECE * NTOK // 2
        ids = place(T, I32)
        c_w1 = place(3 * D).rearrange("p (c d) -> p c d", d=D)
        c_w2 = place(6 * D).rearrange("p (c d) -> p c d", d=D)
        g_tab = place(4 * D)
        t_rest = place(4 * D)
        t_part = place(4 * D)
        t_bf = place(2 * D, BF16)
        tab_t = place(12 * KR).rearrange("p (c k) -> p c k", k=KR)
        c_vec = place(9 * D).rearrange("p (v d) -> p v d", v=3)[0:B]
        c_h = place(3 * D).rearrange("p (c d) -> p c d", c=3)[0:B]
        b1_row = place(D)[0:1]
        b1_sel = place(KR)[0:1]
        assert at[0] <= EARLY * WEXP

        aw = sb("aw", [P, 6])
        aw_s = sb("aw_s", [P, 4])
        cond = sb("cond", [P, 3 * B])
        c_b1 = sb("c_b1", [P, 6 * B])
        c_sh = sb("c_sh", [P, 6 * B])
        c_st = sb("c_st", [B, 3, 8])
        c_ve = sb("c_ve", [B, 8])
        st6 = sb("st6", [P, NTOK, 6])
        mv_x = sb("mv_x", [P, NTOK, 2])
        var_x = sb("var_x", [P, NTOK])
        rstd_x = sb("rstd_x", [P, NTOK])
        nmr_x = sb("nmr_x", [P, NTOK])

        x_t = sb("x_t", [P, 2, DC, P])
        pw = sb("pw", [P, 2, 2 * D])
        xn = sb("xn", [P, 2, D])
        an0 = sb("an0", [P, D])
        an = sb("an", [P, 2, D])
        st_a = sb("st_a", [P, 10])
        r_a = sb("r_a", [P, 1])
        cat = sb("cat", [P, 2, 6, P])
        st_y = sb("st_y", [P, 10])
        r_y = sb("r_y", [P, 1])
        yn = sb("yn", [P, 2, D])
        y_rows = sb("y_rows", [P, 2, K, ROW])
        lg = sb("lg", [P, E])
        top = sb("top", [P, 8])
        top_i = sb("top_i", [P, 8], U32)
        oh = sb("oh", [P, K, E])
        oh_sum = sb("oh_sum", [P, 2, E], BF16)
        seen = sb("seen", [P, 2, E], BF16)
        gap = sb("gap", [P, 1])
        nm_a = sb("nm_a", [P, 1])
        nm_y = sb("nm_y", [P, 1])
        euler = sb("euler", [P, 1])
        q_ = sb("q_", [P, 1])
        den = sb("den", [P, 1])
        pos = sb("pos", [P, E])
        pos_k = sb("pos_k", [P, K, E])
        slot_f = sb("slot_f", [P, K])
        slot = [sb(f"slot{p}", [P, K], I32) for p in range(2)]


        cnt = sb("cnt", [1, E])
        cnt_i = sb("cnt_i", [1, E], I32)
        ntile = sb("ntile", [1, E])
        t_end = sb("t_end", [1, E])
        tail_i = sb("tail_i", [1, E], I32)
        t_num = sb("t_num", [1, NT])
        t_exp = sb("t_exp", [1, NT])
        t_loc = sb("t_loc", [1, NT])
        t_tmp = sb("t_tmp", [1, NT])
        tile_exp = sb("tile_exp", [1, NT], I32)
        tile_row = sb("tile_row", [1, NT], I32)

        xs = sb("xs", [P, 2, ROW])
        xs_t = sb("xs_t", [P, 2, DC, P])
        n1 = (HALF[1][1] - HALF[1][0]) * P
        used = cat[:].rearrange("p b c t -> p (b c t)")
        sg = [pw[:, 0, :], used[:, 0:n1]]
        hh = [pw[:, 1, :], used[:, n1:2 * n1]]
        ht = [xn[:].rearrange("p b (c t) -> p (b c) t", t=P), used[:, 2 * n1:3 * n1].rearrange("p (c t) -> p c t", t=P)]
        yo = sb("yo", [P, 2, D])
        weight = sb("weight", [P, 2])
        tok = [sb(f"tok{p}", [P, 1], I32) for p in range(2)]

        bank = [ctx.enter_context(nc.psum_tensor(f"bank{n}", [P, 512], F32)) for n in range(8)]

        s_row = sem("s_row")
        s_const = sem("s_const")
        s_x = sem("s_x")
        s_ids = sem("s_ids")
        s_win = sem("s_win")
        s_cond = sem("s_cond")
        s_out0 = sem("s_out0")
        s_early = sem("s_early")
        s_late = [sem(f"s_late{e}") for e in range(EARLY, E)]
        experts_ready = sem("experts_ready")
        s_xt = [sem(f"s_xt{p}") for p in range(2)]
        s_pw = [sem(f"s_pw{p}") for p in range(2)]
        pro_v = sem("pro_v")
        pro_a = sem("pro_a")
        pro_p = sem("pro_p")
        pro_t = sem("pro_t")
        xn_done = sem("xn_done")
        a_step = sem("a_step")
        ra_done = sem("ra_done")
        an_done = sem("an_done")
        flip_done = sem("flip_done")
        gate_mm = sem("gate_mm")
        gate_done = sem("gate_done")
        cat_done = sem("cat_done")
        in_done = sem("in_done")
        silu_done = sem("silu_done")
        s1t_mm = sem("s1t_mm")
        s1t_done = sem("s1t_done")
        out_mm = sem("out_mm")
        ly_step = sem("ly_step")
        ry_done = sem("ry_done")
        nma_done = sem("nma_done")
        nmy_done = sem("nmy_done")
        yn_done = sem("yn_done")
        row_step = sem("row_step")
        id_step = sem("id_step")
        yt_mm = sem("yt_mm")
        yt_done = sem("yt_done")
        logit_mm = sem("logit_mm")
        top_step = sem("top_step")
        q_done = sem("q_done")
        rank_mm = sem("rank_mm")
        slot_step = sem("slot_step")
        s_scat = [sem(f"s_scat{p}") for p in range(2)]
        plan_step = sem("plan_step")
        s_tail = sem("s_tail")
        s_xs = [sem(f"s_xs{p}") for p in range(2)]
        flip_x = sem("flip_x")
        xst_done = sem("xst_done")
        g_mm = [sem(f"g_mm{h}") for h in range(2)]
        u_mm = [sem(f"u_mm{h}") for h in range(2)]
        sg_done = [sem(f"sg_done{h}") for h in range(2)]
        h_done = [sem(f"h_done{h}") for h in range(2)]
        ht_mm = [sem(f"ht_mm{h}") for h in range(2)]
        ht_done = [sem(f"ht_done{h}") for h in range(2)]
        y_mm = sem("y_mm")
        meta_step = sem("meta_step")
        yo_done = sem("yo_done")
        s_add = sem("s_add")
        idx_done = sem("idx_done")
        s_pwid = sem("s_pwid")
        relay_s, relay_p, relay_v = sem("relay_s"), sem("relay_p"), sem("relay_v")

        NCONST = 9
        TOPN, SLOTN, LYN, AN_ = 8, 7, 3, 5

        block = ctx.enter_context(nc.Block())

        @block.sync
        def _(sp):
            sp.dma_start(x_all, a["x"].rearrange("(t p) d -> p t d", p=P)).then_inc(s_x, 16)
            for dst, src in ((small[:], a["small"]), (pad_rows[:], a["pad_rows"])):
                sp.dma_start(dst, src).then_inc(s_row, 16)
            sp.dma_start(ids[0:KR, :], a["ids"]).then_inc(s_ids, 16)
            sp.dma_start(g_tab[0:KR, :], a["g_tab"]).then_inc(s_ids, 16)
            for dst, src in ((cond[:], a["cond"]), (c_b1[:], a["c_b1"]), (c_w1, a["c_w1"]),
                             (c_w2, a["c_w2"]), (c_vec, a["c_vec"])):
                sp.dma_start(dst, src).then_inc(s_cond, 16)
            for dst, src in ((aw[:], a["aw"]), (ident[:], a["ident"]), (before_f[:], a["before"]),
                             (ln_gb[:], a["ln_gb"]), (wgate[:], a["wgate"]), (tab_t, a["tab_t"]),
                             (b1_row, a["b1_row"]), (b1_sel, a["b1_sel"]), (t_num[:], a["tile_num"])):
                sp.dma_start(dst, src).then_inc(s_const, 16)
            sp.dma_start(w_in, a["w_in"]).then_inc(s_win, 16)
            sp.dma_start(w_out, a["w_out"]).then_inc(s_win, 16)

            def load_tile(t):
                if not t.is_first(2):
                    sp.wait_ge(in_done, t.at(1, -1))
                    sp.sem_inc(relay_s, 1)
                sp.dma_start(x_t[:, t.parity], a["x_t"][bass.ds(t.at(P), P), :]).then_inc(s_xt[t.parity], 16)
                cols = bass.ds(t.at(PIECE), PIECE)
                sp.dma_start(w_all[:, cols], a["w_exp"][:, cols]).then_inc(s_early, 16)

            pipeline(sp, load_tile, 0, NTOK, 2, 0)

            sp.dma_start(out[0:T, :], a["x"]).then_inc(s_out0, 16)
            sp.wait_ge(s_row, 32)
            sp.dma_start(out[T:T + P, :], pad_rows[:, 0:D]).then_inc(s_out0, 16)
            sp.dma_start(routed[E * REGION:E * REGION + P, :], pad_rows[:]).then_inc(s_tail, 16)
            sp.wait_ge(plan_step, PLAN)
            for e in range(E):
                row = sp.value_load(tail_i[0:1, e:e + 1], min_val=0, max_val=E * REGION - P)
                sp.dma_start(routed[bass.ds(row, P), :], pad_rows[:]).then_inc(s_tail, 16)
            sp.wait_ge(s_tail, 16 * (E + 1))
            for p in range(2):
                sp.wait_ge(s_scat[p], 16 * K * NTOK // 2)

            def load_xs(t):
                row = sp.value_load(tile_row[0:1, bass.ds(t.at(), 1)], min_val=0, max_val=E * REGION)
                if not t.is_first(2):
                    sp.wait_ge(flip_x, t.at(1, -1))
                    sp.wait_ge(meta_step, t.at(2, -2))
                    sp.sem_inc(relay_s, 1)
                sp.dma_start(xs[:, t.parity, :], routed[bass.ds(row, P), :]).then_inc(s_xs[t.parity], 16)

            load_xs(Tile(0, 0))
            load_xs(Tile(0, 1))
            for n in range(E - EARLY):
                cols = slice((EARLY + n) * WEXP, (EARLY + n + 1) * WEXP)
                sp.dma_start(w_all[:, cols], a["w_exp"][:, cols]).then_inc(s_late[n], 16)
            for n in range(E - EARLY):
                sp.wait_ge(s_late[n], 16)
                sp.sem_inc(experts_ready, 1)
            pipeline(sp, load_xs, 2, NT, 0, 1)
            sp.wait_ge(s_add, 16 * NT)

        @block.gpsimd
        def _(pool):
            nc.gpsimd.memset(minus_half[:], -0.5).then_inc(pro_p, 1)
            nc.gpsimd.memset(euler[:], float(np.e)).then_inc(pro_p, 1)
            pool.dma_start(pw_ids[:], a["pw_ids"]).then_inc(s_pwid, 16)

            def gather_pw(t):
                if not t.is_first(2):
                    pool.wait_ge(a_step, t.at(AN_, -AN_))
                    pool.sem_inc(relay_p, 1)
                nc.gpsimd.tensor_copy(pw_idx[t.parity][:], pw_ids[:, bass.ds(t.at(), 1)]).then_inc(idx_done, 1)
                pool.wait_ge(idx_done, t.at(1, 1))
                pool.sem_inc(relay_p, 1)
                nc.gpsimd.indirect_dma_start(
                    pw[:, t.parity, :], None, a["pw_tab"],
                    bass.IndirectOffsetOnAxis(ap=pw_idx[t.parity][:, 0:1], axis=0)).then_inc(s_pw[t.parity], 16)

            def power(o, base, exponent, s):
                nc.gpsimd.tensor_tensor(o, base, exponent, ALU.pow).then_inc(s, 1)

            pool.wait_ge(s_pwid, 16)
            gather_pw(Tile(0, 0))
            gather_pw(Tile(0, 1))
            pool.wait_ge(pro_p, 2)
            pool.wait_ge(pro_v, VARX)
            power(rstd_x[:], var_x[:], minus_half[:], pro_p)
            pool.wait_ge(pro_v, CVE)
            power(c_ve[:, 3:6], c_ve[:, 0:3], minus_half[0:B, 0:3], pro_p)

            def root_a(i):
                pool.wait_ge(a_step, i.at(AN_, AN_))
                power(r_a[:], st_a[:, 8:9], minus_half[:, 0:1], ra_done)

            def root_y(i):
                pool.wait_ge(ly_step, i.at(LYN, LYN))
                power(r_y[:], st_y[:, 8:9], minus_half[:, 0:1], ry_done)

            def exp_gap(i):
                pool.wait_ge(top_step, i.at(TOPN, TOPN))
                power(q_[:], euler[:], gap[:], q_done)

            def scatter(i):
                pool.wait_ge(slot_step, i.at(SLOTN, SLOTN))
                pool.wait_ge(row_step, i.at(1, 1))
                pool.wait_ge(id_step, i.at(1, 1))
                pool.sem_inc(relay_p, 1)
                for k in range(K):
                    nc.gpsimd.indirect_dma_start(
                        routed, bass.IndirectOffsetOnAxis(ap=slot[i.parity][:, k:k + 1], axis=0),
                        y_rows[:, i.parity, k, :], None).then_inc(s_scat[i.parity], 16)

            root_a(Tile(0, 0))
            def step(n):
                for lag, work in ((2, gather_pw), (1, root_a), (-4, scatter), (-2, root_y), (-3, exp_gap)):
                    if n.plus(lag).inside(NTOK):
                        work(n.plus(lag))

            pipeline(pool, step, 0, NTOK + 4, HEAD, TAIL)

            def add_tile(t):
                if not t.is_first(1):
                    pool.wait_ge(s_add, t.at(16))
                pool.wait_ge(yo_done, t.at(1, 1))
                pool.sem_inc(relay_p, 1)
                nc.gpsimd.indirect_dma_start(
                    out, bass.IndirectOffsetOnAxis(ap=tok[t.parity][:, 0:1], axis=0),
                    yo[:, t.parity, :], None, compute_op=ALU.add).then_inc(s_add, 16)

            pool.wait_ge(s_out0, 32)
            pipeline(pool, add_tile, 0, NT, 1, 0)

        @block.scalar
        def _(act):
            act.wait_ge(pro_v, CSH)
            nc.scalar.activation(c_sh[:], c_sh[:], ACT.Silu).then_inc(pro_a, 1)
            act.wait_ge(pro_v, AWS)
            nc.scalar.activation(aw[:], aw[:], ACT.Exp).then_inc(pro_a, 1)
            act.wait_ge(pro_v, NMX)

            def norm_x(i):
                if not i.is_first(2):
                    act.wait_ge(flip_done, i.at(1, -1))
                    act.wait_ge(a_step, i.at(AN_, -AN_))
                c = bass.ds(i.at(), 1)
                nc.scalar.activation(xn[:, i.parity, :], x_all[:, c, :].rearrange("p o d -> p (o d)"), ACT.Identity,
                                     bias=nmr_x[:, c], scale=rstd_x[:, c]).then_inc(xn_done, 1)

            def norm_a(i):
                act.wait_ge(nma_done, i.at(1, 1))
                if not i.is_first(2):
                    act.wait_ge(flip_done, i.at(1, -1))
                nc.scalar.activation(an[:, i.parity, :], an0[:], ACT.Identity, bias=nm_a[:], scale=r_a[:]).then_inc(an_done, 1)

            def copy_s1(i):
                act.wait_ge(s1t_mm, i.at(1, 1))
                nc.scalar.copy(s1_t.rearrange("p c t -> p (c t)"), bank[4][:, 0:D]).then_inc(s1t_done, 1)

            def copy_gates(i):
                act.wait_ge(gate_mm, i.at(1, 1))
                if not i.is_first():
                    act.wait_ge(cat_done, i.at(2))
                nc.scalar.copy(gate_s[:, 0:2 * D], bank[1][:, :]).then_inc(gate_done, 1)
                nc.scalar.copy(gate_s[:, 2 * D:3 * D], bank[2][:, 0:D]).then_inc(gate_done, 1)

            def affine_y(i):
                act.wait_ge(yt_mm, i.at(1, 1))
                if not i.is_first():
                    act.wait_ge(logit_mm, i.at())
                for f in range(DC):
                    nc.scalar.activation(y_t[:, f, :], bank[6][:, f * P:(f + 1) * P], ACT.Identity,
                                         bias=ln_gb[:, 1, f:f + 1], scale=ln_gb[:, 0, f:f + 1]).then_inc(yt_done, 1)

            def silu_1(i):
                act.wait_ge(in_done, i.at(1, 1))
                if not i.is_first():
                    act.wait_ge(s1t_mm, i.at())
                nc.scalar.activation(s1, bank[3][:, 0:D], ACT.Silu).then_inc(silu_done, 1)

            def norm_y(i):
                act.wait_ge(nmy_done, i.at(1, 1))
                if not i.is_first(2):
                    act.wait_ge(yt_mm, i.at(1, -1))
                nc.scalar.activation(yn[:, i.parity, :], bank[5][:, 0:D], ACT.Identity, bias=nm_y[:], scale=r_y[:]).then_inc(yn_done, 1)

            def copy_rows(i):
                act.wait_ge(yn_done, i.at(1, 1))
                if not i.is_first(2):
                    act.wait_ge(s_scat[i.parity], i.pair * (16 * K))
                for k in range(K):
                    last = nc.scalar.copy(y_rows[:, i.parity, k, 0:D], yn[:, i.parity, :])
                last.then_inc(row_step, 1)

            norm_x(Tile(0, 0))
            norm_x(Tile(0, 1))
            norm_a(Tile(0, 0))

            def step(n):
                for lag, work in ((-2, copy_s1), (-3, affine_y), (0, copy_gates), (2, norm_x), (1, norm_a),
                                  (-3, copy_rows), (-1, silu_1), (-2, norm_y)):
                    if n.plus(lag).inside(NTOK):
                        work(n.plus(lag))

            pipeline(act, step, 0, NTOK + 4, HEAD, TAIL)

            def silu(t, h):
                n = (HALF[h][1] - HALF[h][0]) * P
                act.wait_ge(g_mm[h], t.at(1, 1))
                if not t.is_first():
                    act.wait_ge(h_done[h], t.at())
                nc.scalar.activation(sg[h], bank[2 * h][:, 0:n], ACT.Silu).then_inc(sg_done[h], 1)

            def copy_ht(t, h):
                n = (HALF[h][1] - HALF[h][0]) * P
                act.wait_ge(ht_mm[h], t.at(1, 1))
                if not t.is_first():
                    act.wait_ge(y_mm, t.at())
                nc.scalar.copy(ht[h].rearrange("p c t -> p (c t)"), bank[4 + h][:, 0:n]).then_inc(ht_done[h], 1)

            def expert_step(t):
                silu(t, 0)
                if not t.is_first():
                    copy_ht(t.plus(-1), 1)
                silu(t, 1)
                copy_ht(t, 0)

            pipeline(act, expert_step, 0, NT, 3, 0)
            copy_ht(Tile((NT - 1) // 2, (NT - 1) % 2), 1)

        @block.vector
        def _(dve):
            done = [0]

            def did(ins):
                done[0] += 1
                ins.then_inc(pro_v, 1)

            def after(n=None):
                dve.wait_ge(pro_v, done[0] if n is None else n)

            dve.wait_ge(s_x, 16)
            for t in range(NTOK):
                did(nc.vector.bn_stats(st6[:, t, :], x_all[:, t, :]))
            after()
            for t in range(NTOK):
                did(nc.vector.bn_aggr(mv_x[:, t, :], st6[:, t, :]))
            after()
            did(nc.vector.tensor_scalar(var_x[:], mv_x[:, :, 1], EPS, None, ALU.add))
            assert done[0] == VARX, done[0]
            did(nc.vector.memset(gates[:].bitcast(I32), 0))
            did(nc.vector.memset(shifts[:].bitcast(I32), 0))
            did(nc.vector.memset(seen[:, 0, :], 0.0))
            did(nc.vector.memset(ones[:], 1.0))
            dve.wait_ge(s_row, 32)
            dve.wait_ge(s_ids, 32)
            did(nc.vector.tensor_scalar(onehot[0:KR, :], ids[0:KR, :], row_id[0:KR, :], None, ALU.is_equal))

            def split(table, width, stacked):
                def rows(v, n):
                    return v[32 * n:32 * n + ROWS, 0:width]
                after()
                did(nc.vector.tensor_copy(rows(stacked, 0), rows(table, 0)))
                did(nc.vector.tensor_copy(t_bf[0:KR, 0:width], table[0:KR, 0:width]))
                after()
                did(nc.vector.tensor_tensor(t_rest[0:KR, 0:width], table[0:KR, 0:width], t_bf[0:KR, 0:width], ALU.subtract))
                after()
                did(nc.vector.tensor_copy(rows(stacked, 1), rows(t_rest, 1)))
                did(nc.vector.tensor_copy(t_bf[0:KR, 0:width], t_rest[0:KR, 0:width]))
                after()
                did(nc.vector.tensor_tensor(t_part[0:KR, 0:width], t_rest[0:KR, 0:width], t_bf[0:KR, 0:width], ALU.subtract))
                after()
                did(nc.vector.tensor_copy(rows(stacked, 2), rows(t_part, 2)))

            split(g_tab, 4 * D, gates)
            dve.wait_ge(pro_p, 3)
            did(nc.vector.scalar_tensor_tensor(nmr_x[:], mv_x[:, :, 0], -1.0, rstd_x[:], ALU.mult, ALU.mult))
            assert done[0] == NMX, done[0]
            dve.wait_ge(s_cond, 16 * 5)
            dve.wait_ge(pro_t, 1)
            did(nc.vector.tensor_tensor(c_sh[:], bank[0][:, 0:6 * B], c_b1[:], ALU.add))
            assert done[0] == CSH, done[0]
            dve.wait_ge(s_const, 16 * NCONST)
            did(nc.vector.tensor_reduce(aw_s[:, 0:1], aw[:], AX.X, ALU.max))
            did(nc.vector.tensor_copy(before[:], before_f[:]))
            after()
            did(nc.vector.tensor_scalar(aw[:], aw[:], aw_s[:, 0:1], None, ALU.subtract))
            assert done[0] == AWS, done[0]
            dve.wait_ge(pro_t, 2)
            did(nc.vector.tensor_tensor(c_h[:, 0:2, :].rearrange("b c d -> b (c d)"), bank[1][0:B, :], c_vec[:, 0, 0:2 * D], ALU.add))
            did(nc.vector.tensor_tensor(c_h[:, 2, :], bank[2][0:B, 0:D], c_vec[:, 0, 2 * D:3 * D], ALU.add))
            after()
            for c in range(3):
                did(nc.vector.bn_stats(c_st[:, c, 0:6], c_h[:, c, :]))
            after()
            for c in range(3):
                did(nc.vector.bn_aggr(c_st[:, c, 6:8], c_st[:, c, 0:6]))
            after()
            did(nc.vector.tensor_scalar(c_ve[:, 0:3], c_st[:, :, 7], EPS, None, ALU.add))
            assert done[0] == CVE, done[0]
            dve.wait_ge(pro_a, 2)
            did(nc.vector.tensor_reduce(aw_s[:, 1:2], aw[:], AX.X, ALU.add))
            after()
            did(nc.vector.reciprocal(aw_s[:, 2:3], aw_s[:, 1:2]))
            after()
            did(nc.vector.tensor_scalar(aw[:], aw[:], aw_s[:, 2:3], None, ALU.mult))
            after()
            dve.wait_ge(s_win, 32)
            for c in range(6):
                w2 = w_in[:, 2 * c:2 * c + 2, :]
                did(nc.vector.tensor_scalar(w2, w2, aw[:, c:c + 1], None, ALU.mult))
            dve.wait_ge(pro_p, 4)
            for c in range(3):
                did(nc.vector.tensor_scalar(c_h[:, c, :], c_h[:, c, :], c_st[:, c, 6:7], c_ve[:, 3 + c:4 + c], ALU.subtract, ALU.mult))
            after()
            ch = c_h.rearrange("b c d -> b (c d)")
            did(nc.vector.tensor_tensor(ch, ch, c_vec[:, 1, :], ALU.mult))
            after()
            did(nc.vector.tensor_tensor(ch, ch, c_vec[:, 2, :], ALU.add))
            assert done[0] == CLN, done[0]
            dve.wait_ge(pro_t, 3)
            for n in range(PARTS):
                o = 32 * n + ROWS - B
                did(nc.vector.tensor_copy(tab_t[:, 4:10, o:o + B], bank[3][:, 0:6 * B].rearrange("p (c b) -> p c b", b=B)))
            assert done[0] == CTT, done[0]

            def affine_a(i):
                def w(n):
                    dve.wait_ge(a_step, i.at(AN_, n))
                p = i.parity
                dve.wait_ge(xn_done, i.at(1, 1))
                dve.wait_ge(s_pw[p], i.pair * 16 + 16)
                if not i.is_first():
                    dve.wait_ge(an_done, i.at())
                nc.vector.tensor_tensor(an0[:], xn[:, p, :], pw[:, p, 0:D], ALU.mult).then_inc(a_step, 1)
                yield
                w(1)
                nc.vector.tensor_tensor(an0[:], an0[:], pw[:, p, D:2 * D], ALU.add).then_inc(a_step, 1)
                yield
                w(2)
                nc.vector.bn_stats(st_a[:, 0:6], an0[:]).then_inc(a_step, 1)
                yield
                w(3)
                dve.sem_inc(relay_v, 1)
                nc.vector.bn_aggr(st_a[:, 6:8], st_a[:, 0:6]).then_inc(a_step, 1)
                yield
                w(4)
                nc.vector.tensor_scalar(st_a[:, 8:9], st_a[:, 7:8], EPS, None, ALU.add).then_inc(a_step, 1)

            def bias_a(i):
                dve.wait_ge(ra_done, i.at(1, 1))
                nc.vector.tensor_scalar(nm_a[:], st_a[:, 6:7], -1.0, r_a[:], ALU.mult, ALU.mult).then_inc(nma_done, 1)

            side_by_side(affine_a(Tile(0, 0)))
            bias_a(Tile(0, 0))
            dve.wait_ge(pro_t, 4)
            did(nc.vector.tensor_copy(g_tab[0:KR, 0:D], bank[4][0:KR, 0:D]))
            split(g_tab, D, shifts)
            for c in (6, 8):
                after()
                did(nc.vector.tensor_tensor(w_in[:, 4:6, :], w_in[:, 4:6, :], w_in[:, c:c + 2, :], ALU.add))
            assert done[0] == NMR, done[0]

            def gain(i):
                dve.wait_ge(flip_done, i.at(1, 1))
                dve.wait_ge(gate_done, i.at(2, 2))
                if not i.is_first(2):
                    dve.wait_ge(in_done, i.at(1, -1))
                c = cat[:, i.parity].rearrange("p c t -> p (c t)")
                nc.vector.tensor_tensor(c[:, 0:2 * D], gate_s[:, 0:2 * D], bank[0][:, :], ALU.mult).then_inc(cat_done, 1)
                nc.vector.tensor_tensor(c[:, 2 * D:3 * D], gate_s[:, 2 * D:3 * D], bank[0][:, D:2 * D], ALU.mult).then_inc(cat_done, 1)

            def stats_y(i):
                def w(n):
                    dve.wait_ge(ly_step, i.at(LYN, n))
                dve.wait_ge(out_mm, i.at(1, 1))
                dve.sem_inc(relay_v, 1)
                nc.vector.bn_stats(st_y[:, 0:6], bank[5][:, 0:D]).then_inc(ly_step, 1)
                yield
                w(1)
                dve.sem_inc(relay_v, 1)
                nc.vector.bn_aggr(st_y[:, 6:8], st_y[:, 0:6]).then_inc(ly_step, 1)
                yield
                w(2)
                nc.vector.tensor_scalar(st_y[:, 8:9], st_y[:, 7:8], EPS, None, ALU.add).then_inc(ly_step, 1)

            def bias_y(i):
                dve.wait_ge(ry_done, i.at(1, 1))
                if not i.is_first():
                    dve.wait_ge(yn_done, i.at())
                nc.vector.tensor_scalar(nm_y[:], st_y[:, 6:7], -1.0, r_y[:], ALU.mult, ALU.mult).then_inc(nmy_done, 1)

            def number_rows(i):
                if not i.is_first(2):
                    dve.wait_ge(s_scat[i.parity], i.pair * (16 * K))
                nc.vector.tensor_copy(y_rows[:, i.parity, :, D + 1],
                                      token_id[:, bass.ds(i.at(), 1)].broadcast_to([P, K])).then_inc(id_step, 1)

            def route(i):
                def w(n):
                    dve.wait_ge(top_step, i.at(TOPN, n))
                def s(ins):
                    ins.then_inc(top_step, 1)
                p = i.parity
                dve.wait_ge(logit_mm, i.at(1, 1))
                s(nc.vector.tensor_copy(lg[:], bank[7][:, 0:E]))
                yield
                w(1)
                dve.sem_inc(relay_v, 1)
                s(nc.vector.max(top[:], lg[:]))
                yield
                w(2)
                dve.sem_inc(relay_v, 1)
                s(nc.vector.max_index(top_i[:], top[:], lg[:]))
                s(nc.vector.tensor_tensor(gap[:], top[:, 1:2], top[:, 0:1], ALU.subtract))
                yield
                w(3)
                for k in range(K):
                    s(nc.vector.tensor_scalar(oh[:, k, :], iota_e, top_i[:, k:k + 1], None, ALU.is_equal))
                yield
                w(6)
                if not i.is_first(2):
                    dve.wait_ge(rank_mm, i.at(1, -1))
                s(nc.vector.tensor_tensor(oh_sum[:, p, :], oh[:, 0, :], oh[:, 1, :], ALU.add))
                yield
                w(7)
                if not i.is_first():
                    dve.wait_ge(rank_mm, i.at())
                s(nc.vector.tensor_tensor(seen[:, 1 - p, :], seen[:, p, :], oh_sum[:, p, :], ALU.add))

            def slots(i):
                def w(n):
                    dve.wait_ge(slot_step, i.at(SLOTN, n))
                def s(ins):
                    ins.then_inc(slot_step, 1)
                p = i.parity
                dve.wait_ge(rank_mm, i.at(1, 1))
                dve.wait_ge(q_done, i.at(1, 1))
                s(nc.vector.tensor_scalar(den[:], q_[:], 1.0, None, ALU.add))
                s(nc.vector.tensor_tensor(pos[:], bank[7][:, 0:E], region_e, ALU.add))
                yield
                w(1)
                s(nc.vector.reciprocal(y_rows[:, p, 0, D:D + 1], den[:]))
                w(2)
                for k in range(K):
                    s(nc.vector.tensor_tensor_reduce(out=pos_k[:, k, :], in0=pos[:], in1=oh[:, k, :], scale=1.0, scalar=0.0,
                                                     op0=ALU.mult, op1=ALU.add, accum_out=slot_f[:, k:k + 1]))
                yield
                w(3)
                s(nc.vector.tensor_tensor(y_rows[:, p, 1, D:D + 1], q_[:], y_rows[:, p, 0, D:D + 1], ALU.mult))
                yield
                w(5)
                s(nc.vector.tensor_copy(slot[p][:], slot_f[:]))

            def step(n):
                def alive(*work):
                    return [f(n.plus(lag)) for lag, f in work if n.plus(lag).inside(NTOK)]
                side_by_side(*alive((1, affine_a), (-4, slots)))
                alive((0, gain), (1, bias_a), (-3, number_rows))
                side_by_side(*alive((-2, stats_y), (-3, route)))
                alive((-2, bias_y))

            pipeline(dve, step, 0, NTOK + 4, HEAD, TAIL)

            planned = [0]

            def plan(ins):
                planned[0] += 1
                ins.then_inc(plan_step, 1)
                dve.wait_ge(plan_step, planned[0])

            dve.wait_ge(rank_mm, NTOK + 1)
            plan(nc.vector.tensor_copy(cnt[:], bank[7][0:1, 0:E]))
            plan(nc.vector.tensor_scalar(cnt_i[:], cnt[:], float(P - 1), None, ALU.add))
            plan(nc.vector.tensor_scalar(cnt_i[:], cnt_i[:], 7, None, ALU.logical_shift_right))
            plan(nc.vector.tensor_copy(ntile[:], cnt_i[:]))
            plan(nc.vector.tensor_tensor_scan(t_end[:], ones[0:1, 0:E], ntile[:], 0.0, ALU.mult, ALU.add))
            plan(nc.vector.tensor_tensor(tail_i[:], cnt[:], region_e[0:1, :], ALU.add))
            plan(nc.vector.memset(t_exp[:], 0.0))
            plan(nc.vector.tensor_copy(t_loc[:], t_num[:]))
            for e in range(E):
                plan(nc.vector.tensor_scalar(t_tmp[:], t_num[:], t_end[:, e:e + 1], None, ALU.is_ge))
                plan(nc.vector.tensor_tensor(t_exp[:], t_exp[:], t_tmp[:], ALU.add))
                plan(nc.vector.tensor_scalar(t_tmp[:], t_tmp[:], ntile[:, e:e + 1], None, ALU.mult))
                plan(nc.vector.tensor_tensor(t_loc[:], t_loc[:], t_tmp[:], ALU.subtract))
            plan(nc.vector.tensor_scalar(t_loc[:], t_loc[:], float(P), None, ALU.mult))
            plan(nc.vector.tensor_scalar(t_tmp[:], t_exp[:], float(REGION), None, ALU.mult))
            plan(nc.vector.tensor_tensor(t_loc[:], t_loc[:], t_tmp[:], ALU.add))
            plan(nc.vector.tensor_scalar(t_loc[:], t_loc[:], float(E * REGION), None, ALU.min))
            plan(nc.vector.tensor_copy(tile_row[:], t_loc[:]))
            plan(nc.vector.tensor_scalar(tile_exp[:], t_exp[:], float(E - 1), None, ALU.min))
            assert planned[0] == PLAN, planned[0]

            def affine_xs(t):
                dve.wait_ge(flip_x, t.at(1, 1))
                if not t.is_first(2):
                    dve.wait_ge(u_mm[1], t.at(1, -1))
                for f in range(DC):
                    nc.vector.tensor_scalar(xs_t[:, t.parity, f, :], bank[7][:, f * P:(f + 1) * P], ln_gb[:, 0, f:f + 1],
                                            ln_gb[:, 1, f:f + 1], ALU.mult, ALU.add).then_inc(xst_done, 1)

            def hidden(t, h):
                n = (HALF[h][1] - HALF[h][0]) * P
                dve.wait_ge(u_mm[h], t.at(1, 1))
                dve.wait_ge(sg_done[h], t.at(1, 1))
                if not t.is_first():
                    dve.wait_ge(ht_mm[h], t.at())
                nc.vector.tensor_tensor(hh[h], sg[h], bank[2 * h + 1][:, 0:n], ALU.mult).then_inc(h_done[h], 1)

            def meta(t):
                p = t.parity
                if not t.is_first(2):
                    dve.wait_ge(s_add, t.at(16, -16))
                nc.vector.tensor_copy(tok[p][:], xs[:, p, D + 1:D + 2]).then_inc(meta_step, 1)
                nc.vector.tensor_copy(weight[:, p:p + 1], xs[:, p, D:D + 1]).then_inc(meta_step, 1)

            def weigh(t):
                p = t.parity
                dve.wait_ge(y_mm, t.at(1, 1))
                dve.wait_ge(meta_step, t.at(2, 2))
                nc.vector.tensor_scalar(yo[:, p, :], bank[6][:, 0:D], weight[:, p:p + 1], None, ALU.mult).then_inc(yo_done, 1)

            def expert_step(t):
                hidden(t, 0)
                if not (isinstance(t.pair, int) and t.at() == NT - 1):
                    affine_xs(t.plus(1))
                meta(t)
                hidden(t, 1)
                if not t.is_first():
                    weigh(t.plus(-1))

            affine_xs(Tile(0, 0))
            pipeline(dve, expert_step, 0, NT, 3, 2)
            weigh(Tile((NT - 1) // 2, (NT - 1) % 2))

        @block.tensor
        def _(pe):
            mm = nc.tensor.matmul
            pe.wait_ge(s_cond, 16 * 5)
            for c in range(3):
                for f in range(DC):
                    o = (c * DC + f) * B
                    last = mm(bank[0][:, o:o + B], c_w1[:, c, f * P:(f + 1) * P], cond[:, c * B:(c + 1) * B],
                              start=True, stop=True)
            last.then_inc(pro_t, 1)
            pe.wait_ge(pro_a, 1)
            for c in range(3):
                for f in range(DC):
                    o = (c * DC + f) * B
                    last = mm(bank[1 + c // 2][0:B, (c % 2) * D:(c % 2 + 1) * D], c_sh[:, o:o + B],
                              c_w2[:, c * DC + f, :], start=(f == 0), stop=(f == DC - 1))
            last.then_inc(pro_t, 1)
            pe.wait_ge(pro_v, CLN)
            pe.wait_ge(s_const, 16 * NCONST)
            for c in range(3):
                for f in range(DC):
                    o = (c * DC + f) * B
                    last = nc.tensor.transpose(bank[3][:, o:o + B], c_h[:, c, f * P:(f + 1) * P], ident[0:B, 0:B])
            last.then_inc(pro_t, 1)
            pe.wait_ge(pro_v, CTT)
            for c in range(12):
                mm(bank[4][0:KR, 0:D], tab_t[:, c, :], w_in[:, c, :], start=(c == 0), stop=False)
            mm(bank[4][0:KR, 0:D], b1_sel[:], b1_row[:], start=False, stop=True).then_inc(pro_t, 1)
            def flip(i):
                p = i.parity
                pe.wait_ge(an_done, i.at(1, 1))
                pe.wait_ge(xn_done, i.at(1, 1))
                if not i.is_first():
                    pe.wait_ge(cat_done, i.at(2))
                    pe.wait_ge(gate_done, i.at(2))
                for n, src in enumerate((an, an, xn, xn)):
                    f = n % DC
                    last = nc.tensor.transpose(bank[0][:, n * P:(n + 1) * P], src[:, p, f * P:(f + 1) * P], ident[:])
                last.then_inc(flip_done, 1)
                cols = onehot[0:KR, bass.ds(i.at(P), P)]
                for n in range(6):
                    b, o = (bank[1], n) if n < 4 else (bank[2], n - 4)
                    last = mm(b[:, o * P:(o + 1) * P], gates[:, n * P:(n + 1) * P], cols, start=True, stop=True)
                last.then_inc(gate_mm, 1)

            def integrate(i):
                p = i.parity
                pe.wait_ge(cat_done, i.at(2, 2))
                if i.is_first():
                    pe.wait_ge(pro_v, NMR)
                if not i.is_first():
                    pe.wait_ge(silu_done, i.at())
                pe.wait_ge(s_xt[p], i.pair * 16 + 16)
                o = bank[3][:, 0:D]
                mm(o, onehot[0:KR, bass.ds(i.at(P), P)], shifts[:], start=True, stop=False)
                for n, c in enumerate((0, 1, 2, 3, 10, 11)):
                    mm(o, cat[:, p, n, :], w_in[:, c, :], start=False, stop=False)
                for f in range(DC):
                    last = mm(o, x_t[:, p, f, :], w_in[:, 4 + f, :], start=False, stop=(f == DC - 1))
                last.then_inc(in_done, 1)

            def flip_s(i):
                pe.wait_ge(silu_done, i.at(1, 1))
                if not i.is_first():
                    pe.wait_ge(s1t_done, i.at())
                for f in range(DC):
                    last = nc.tensor.transpose(bank[4][:, f * P:(f + 1) * P], s1[:, f * P:(f + 1) * P], ident[:])
                last.then_inc(s1t_mm, 1)

            def flip_y(i):
                pe.wait_ge(yn_done, i.at(1, 1))
                if not i.is_first():
                    pe.wait_ge(yt_done, i.at(2))
                for f in range(DC):
                    last = nc.tensor.transpose(bank[6][:, f * P:(f + 1) * P], yn[:, i.parity, f * P:(f + 1) * P], ident[:])
                last.then_inc(yt_mm, 1)

            def project(i):
                pe.wait_ge(s1t_done, i.at(1, 1))
                if not i.is_first():
                    pe.wait_ge(yn_done, i.at())
                o = bank[5][:, 0:D]
                mm(o, onehot[0:KR, bass.ds(i.at(P), P)], gates[:, 3 * D:4 * D], start=True, stop=False)
                for f in range(DC):
                    last = mm(o, s1_t[:, f, :], w_out[:, f, :], start=False, stop=(f == DC - 1))
                last.then_inc(out_mm, 1)

            def logits(i):
                pe.wait_ge(yt_done, i.at(2, 2))
                if not i.is_first():
                    pe.wait_ge(slot_step, i.at(SLOTN))
                for f in range(DC):
                    last = mm(bank[7][:, 0:E], y_t[:, f, :], wgate[:, f, :], start=(f == 0), stop=(f == DC - 1))
                last.then_inc(logit_mm, 1)

            def rank(i):
                p = i.parity
                pe.wait_ge(top_step, i.at(TOPN, TOPN))
                mm(bank[7][:, 0:E], before[:], oh_sum[:, p, :], start=True, stop=False)
                mm(bank[7][:, 0:E], ones[:], seen[:, p, :], start=False, stop=True).then_inc(rank_mm, 1)

            def step(n):
                for lag, work in ((-4, rank), (0, flip), (-2, flip_s), (-3, flip_y), (-2, project),
                                  (-3, logits), (-1, integrate)):
                    if n.plus(lag).inside(NTOK):
                        work(n.plus(lag))

            pipeline(pe, step, 0, NTOK + 4, HEAD, TAIL)
            pe.wait_ge(slot_step, SLOTN * NTOK)
            mm(bank[7][:, 0:E], ones[:], seen[:, NTOK % 2, :], start=True, stop=True).then_inc(rank_mm, 1)

            pe.wait_ge(plan_step, PLAN)
            pe.wait_ge(s_early, 16 * NTOK)
            pe.sem_inc(experts_ready, EARLY)

            def expert_of(t):
                return pe.value_load(tile_exp[0:1, bass.ds(t.at(), 1)], min_val=0, max_val=E - 1)

            def weights(e, start, width):
                return w_all[:, bass.ds(e * WEXP + start, width)]

            def flip_in(t):
                pe.wait_ge(s_xs[t.parity], t.pair * 16 + 16)
                if not t.is_first():
                    pe.wait_ge(xst_done, t.at(2))
                for f in range(DC):
                    last = nc.tensor.transpose(bank[7][:, f * P:(f + 1) * P], xs[:, t.parity, f * P:(f + 1) * P], ident[:])
                last.then_inc(flip_x, 1)

            def gate_up(t, e, h):
                c0, c1 = HALF[h]
                n = (c1 - c0) * P
                if h == 0:
                    pe.wait_ge(xst_done, t.at(2, 2))
                for m, (s_free, s_full) in enumerate(((sg_done[h], g_mm[h]), (h_done[h], u_mm[h]))):
                    if not t.is_first():
                        pe.wait_ge(s_free, t.at())
                    for f in range(DC):
                        last = mm(bank[2 * h + m][:, 0:n], xs_t[:, t.parity, f, :],
                                  weights(e, (f * 2 + m) * I + c0 * P, n), start=(f == 0), stop=(f == DC - 1))
                    last.then_inc(s_full, 1)

            def flip_h(t, h):
                c0, c1 = HALF[h]
                pe.wait_ge(h_done[h], t.at(1, 1))
                if not t.is_first():
                    pe.wait_ge(ht_done[h], t.at())
                for c in range(c1 - c0):
                    last = nc.tensor.transpose(bank[4 + h][:, c * P:(c + 1) * P], hh[h][:, c * P:(c + 1) * P], ident[:])
                last.then_inc(ht_mm[h], 1)

            def down(t, e, h):
                c0, c1 = HALF[h]
                pe.wait_ge(ht_done[h], t.at(1, 1))
                if h == 0 and not t.is_first():
                    pe.wait_ge(yo_done, t.at())
                for c in range(c0, c1):
                    last = mm(bank[6][:, 0:D], ht[h][:, c - c0, :], weights(e, 2 * DC * I + c * D, D),
                              start=(c == 0), stop=(c == IC - 1))
                if h == 1:
                    last.then_inc(y_mm, 1)

            def expert_step(t):
                before_t = t.plus(-1)
                e = expert_of(t)
                pe.wait_ge(experts_ready, e + 1)
                gate_up(t, e, 0)
                if not t.is_first():
                    e_b = expert_of(before_t)
                    flip_h(before_t, 1)
                    down(before_t, e_b, 0)
                if not (isinstance(t.pair, int) and t.at() == NT - 1):
                    flip_in(t.plus(1))
                gate_up(t, e, 1)
                if not t.is_first():
                    down(before_t, e_b, 1)
                flip_h(t, 0)

            flip_in(Tile(0, 0))
            pipeline(pe, expert_step, 0, NT, 3, 2)
            t = Tile((NT - 1) // 2, (NT - 1) % 2)
            e = expert_of(t)
            flip_h(t, 1)
            down(t, e, 0)
            down(t, e, 1)


VARX = 2 * NTOK + 1
NMX = VARX + 5 + 7 + 1
CSH = NMX + 1
AWS = CSH + 3
CVE = AWS + 2 + 6 + 1
CLN = CVE + 3 + 6 + 5
CTT = CLN + 3
NMR = CTT + 1 + 7 + 2
HEAD, TAIL = 6, 6
PLAN = 8 + 4 * E + 6


def kernel(**v):
    import numpy as _np
    import concourse.bacc as _bacc
    from concourse.bass_utils import run_bass_kernel_spmd as _run

    v = {k: _np.asarray(x) for k, x in v.items()}
    f = _np.float32

    def part(w):
        return w.reshape(-1, P, w.shape[-1]).transpose(1, 0, 2)

    h = {}
    x = v["x"].reshape(T, D)
    h["x"] = x
    h["x_t"] = x.reshape(NTOK, P, DC, P).transpose(0, 3, 2, 1).reshape(NTOK * P, DC * P)
    h["pw_tab"] = _np.concatenate([v["L0_cond_pw_g"], v["L0_cond_pw_b"]], axis=1)
    h["pw_ids"] = v["itok_BxS_0_999"].reshape(NTOK, P).T
    comp, scale = v["itok_BxS_0_4"].reshape(T), v["mask_BxS_ik0"].reshape(T)
    ids = _np.full((KR, T), -1, _np.int32)
    g_tab = _np.zeros((KR, 4 * D), f)
    row_id = _np.zeros((P, 1), f)
    tab_t = _np.zeros((P, 12, KR), f)
    b1_sel = _np.zeros((1, KR), f)
    for n in range(PARTS):
        o = 32 * n
        ids[o:o + NCOMP] = comp
        ids[o + NCOMP:o + NCOMP + NSCALE] = scale
        ids[o + ROWS - B:o + ROWS] = _np.repeat(_np.arange(B, dtype=_np.int32), S)
        g_tab[o:o + NCOMP, 0:D] = v["L0_cond_cp_g"]
        g_tab[o:o + NCOMP, D:2 * D] = v["L0_cond_tm_g"]
        g_tab[o + NCOMP:o + NCOMP + NSCALE, 2 * D:3 * D] = v["L0_cond_ms_g"]
        g_tab[o + ROWS - B:o + ROWS, 3 * D:4 * D] = v["L0_cond_int_b2"]
        row_id[o:o + ROWS, 0] = [*range(NCOMP), *range(NSCALE), *range(B)]
        tab_t[:, 0:2, o:o + NCOMP] = part(v["L0_cond_cp_b"].T)
        tab_t[:, 2:4, o:o + NCOMP] = part(v["L0_cond_tm_b"].T)
        tab_t[:, 10:12, o + NCOMP:o + NCOMP + NSCALE] = part(v["L0_cond_ms_b"].T)
        b1_sel[0, o + ROWS - B:o + ROWS] = 1
    h["ids"], h["g_tab"], h["tab_t"], h["b1_sel"] = ids, g_tab, tab_t, b1_sel
    h["b1_row"] = v["L0_cond_int_b1"].reshape(1, D)
    h["w_in"] = part(v["L0_cond_int_W1"])
    h["w_out"] = part(v["L0_cond_int_W2"])
    nets = ("mem", "noi", "res")
    cond, c_w1 = _np.zeros((P, 3, B), f), _np.zeros((P, 3, D), f)
    for c, (s, n) in enumerate(zip(("cond_512", "cond_64", "fside_Bx32_0"), nets)):
        w = v[f"L0_cond_{n}_W1"]
        cond[:w.shape[0], c] = v[s].T
        c_w1[:w.shape[0], c] = w
    h["cond"], h["c_w1"] = cond.reshape(P, 3 * B), c_w1
    h["c_w2"] = _np.concatenate([part(v[f"L0_cond_{n}_W2"]) for n in nets], axis=1)
    b1 = _np.stack([v[f"L0_cond_{n}_b1"] for n in nets]).reshape(3 * DC, P).T
    h["c_b1"] = _np.repeat(b1, B, axis=1)
    vec = _np.stack([_np.concatenate([v[f"L0_cond_{n}_{k}"] for n in nets]) for k in ("b2", "g", "be")])
    h["c_vec"] = _np.broadcast_to(vec, (B, 3, 3 * D))
    h["aw"] = _np.broadcast_to(v["L0_cond_aw"], (P, 6))
    h["ln_gb"] = _np.stack([v[f"L0_cond_int_{k}"].reshape(DC, P).T for k in ("g", "be")], axis=1)
    h["wgate"] = part(v["L0_ffn_w_gate"].T)
    h["ident"] = _np.eye(P, dtype=f)
    h["before"] = _np.triu(_np.ones((P, P), f), 1)
    iota = _np.broadcast_to(_np.arange(E, dtype=f), (P, E))
    tokens = _np.arange(T, dtype=f).reshape(NTOK, P).T
    h["small"] = _np.concatenate([iota, iota * REGION, _np.ones((P, 1), f), row_id, tokens], axis=1)
    h["tile_num"] = _np.arange(NT, dtype=f).reshape(1, NT)
    pad = _np.zeros((P, ROW), f)
    pad[:, D + 1] = _np.arange(T, T + P)
    h["pad_rows"] = pad
    w1, w3, w2 = v["L0_ffn_w1"], v["L0_ffn_w3"], v["L0_ffn_w2"]
    gu = _np.stack([w1, w3], axis=1).reshape(E, 2, I, DC, P).transpose(0, 4, 3, 1, 2).reshape(E, P, 2 * DC * I)
    dn = w2.reshape(E, D, IC, P).transpose(0, 3, 2, 1).reshape(E, P, IC * D)
    h["w_exp"] = _np.concatenate([gu, dn], axis=2).transpose(1, 0, 2).reshape(P, E * WEXP)

    nc = _bacc.Bacc("TRN2", target_bir_lowering=False, num_devices=1)
    arrays, aps = {}, {}
    for name, w in h.items():
        w = _np.ascontiguousarray(w)
        arrays[f"in_{name}"] = w
        aps[name] = nc.dram_tensor(f"in_{name}", w.shape, mybir.dt.from_np(w.dtype), kind="ExternalInput").ap()
    out = nc.dram_tensor("out_rows", (T + P, D), F32, kind="ExternalOutput").ap()
    routed = nc.dram_tensor("routed_rows", (E * REGION + P, ROW), F32, kind="Internal").ap()
    adaln_moe(nc, aps, out, routed)
    r = _run(nc, [arrays], core_ids=[0])
    return r.results[0]["out_rows"][0:T].reshape(B, S, D)
```

```python
from contextlib import ExitStack

import numpy as np
import concourse.bass as bass
from concourse import mybir

ALU = mybir.AluOpType
ACT = mybir.ActivationFunctionType
AX = mybir.AxisListType
F32 = mybir.dt.float32
BF16 = mybir.dt.bfloat16
F16 = mybir.dt.float16
I32 = mybir.dt.int32
U32 = mybir.dt.uint32

P = 128
B, S, D = 2, 1024, 256
T = B * S
NTOK = T // P
DC = D // P
E, I, K = 8, 896, 2
IC = I // P
NCOMP, NSCALE = 5, 3
ROWS = NCOMP + NSCALE + B
PARTS = 3
KR = 32 * (PARTS - 1) + ROWS
NPW = 250
EPS = 1e-5

REGION = T + P
NT = (K * T + (E - K) * (P - 1) + K * P) // P
ROW = D + 2
WEXP = 2 * DC * I + IC * D
HALF = ((0, 4), (4, IC))
EARLY = 6
PIECE = EARLY * WEXP // NTOK
UNITS = WEXP // I
SHIFT = 2
SPLIT_A = 3


class Tile:

    def __init__(self, pair, parity):
        self.pair, self.parity = pair, parity

    def plus(self, d):
        q = self.parity + d
        return Tile(self.pair + q // 2, q % 2)

    def at(self, scale=1, offset=0):
        return self.pair * (2 * scale) + (self.parity * scale + offset)

    def inside(self, n):
        return not isinstance(self.pair, int) or 0 <= self.at() < n

    def is_first(self, n=1):
        return isinstance(self.pair, int) and self.at() < n


def pipeline(engine, body, first, last, head, tail):
    lo, hi = first + head, last - tail
    for n in range(first, lo):
        body(Tile(n // 2, n % 2))
    with engine.Fori(lo // 2, lo // 2 + (hi - lo) // 2) as pair:
        body(Tile(pair, 0).plus(lo % 2))
        body(Tile(pair, 0).plus(lo % 2 + 1))
    for n in range(hi, last):
        body(Tile(n // 2, n % 2))


def side_by_side(*chains):
    chains = list(chains)
    while chains:
        for chain in tuple(chains):
            if next(chain, done_) is done_:
                chains.remove(chain)


done_ = object()


def adaln_moe(nc, a, out, routed):
    with ExitStack() as ctx:
        def sb(name, shape, dt=F32):
            return ctx.enter_context(nc.sbuf_tensor(name, shape, dt))

        def sem(name):
            return ctx.enter_context(nc.semaphore(name))

        ident = sb("ident", [P, P])
        before = sb("before", [P, P], BF16)
        ones = sb("ones", [P, P], BF16)
        ident_h = sb("ident_h", [P, P], F16)
        ident_l = sb("ident_l", [P, P], BF16)
        small = sb("small", [P, 2 * E + 2 + NTOK])
        iota_e = small[:, 0:E]
        region_e = small[:, E:2 * E]
        e_base = small[:, 2 * E:2 * E + 1]
        row_id = small[:, 2 * E + 1:2 * E + 2]
        token_id = small[:, 2 * E + 2:2 * E + 2 + NTOK]
        pad_rows = sb("pad_rows", [P, ROW])
        ln_gb = sb("ln_gb", [P, 2, DC])
        wgate = sb("wgate", [P, DC, E])
        pw_ids = sb("pw_ids", [P, NTOK], I32)
        pw_idx = [sb(f"pw_idx{p}", [P, 1], I32) for p in range(2)]
        minus_half = sb("minus_half", [P, NTOK])
        gates = sb("gates", [KR, 4 * D], BF16)
        shifts = sb("shifts", [KR, D], BF16)

        w_all = sb("w_all", [P, E * WEXP + SHIFT * I])
        w_hi, w_lo = w_all[:].bitcast(F16), w_all[:].bitcast(BF16)
        at = [EARLY * WEXP + SHIFT * I]

        def place(n, dt=F32):
            v = w_all[:, at[0]:at[0] + n]
            at[0] += n
            return v if dt == F32 else v.bitcast(dt)

        x_all = place(NTOK * D).rearrange("p (t d) -> p t d", d=D)
        onehot = place(T // 2, BF16)
        w_in = place(12 * D).rearrange("p (c d) -> p c d", d=D)
        w_out = place(DC * D).rearrange("p (c d) -> p c d", d=D)
        gate_s = place(3 * D)
        s1 = place(D)
        s1_t = place(D).rearrange("p (c t) -> p c t", t=P)
        y_t = place(D).rearrange("p (c t) -> p c t", t=P)
        assert at[0] <= E * WEXP + SHIFT * I
        at[0] = PIECE * NTOK // 2 + SHIFT * I
        before_f = place(P)
        ids = place(T, I32)
        c_w1 = place(3 * D).rearrange("p (c d) -> p c d", d=D)
        c_w2 = place(6 * D).rearrange("p (c d) -> p c d", d=D)
        g_tab = place(4 * D)
        t_rest = place(4 * D)
        t_part = place(4 * D)
        t_bf = place(2 * D, BF16)
        tab_t = place(12 * KR).rearrange("p (c k) -> p c k", k=KR)
        c_vec = place(9 * D).rearrange("p (v d) -> p v d", v=3)[0:B]
        c_h = place(3 * D).rearrange("p (c d) -> p c d", c=3)[0:B]
        b1_row = place(D)[0:1]
        b1_sel = place(KR)[0:1]
        assert at[0] <= EARLY * WEXP + SHIFT * I

        aw = sb("aw", [P, 6])
        aw_s = sb("aw_s", [P, 4])
        cond = sb("cond", [P, 3 * B])
        c_b1 = sb("c_b1", [P, 6 * B])
        c_sh = sb("c_sh", [P, 6 * B])
        c_st = sb("c_st", [B, 3, 8])
        c_ve = sb("c_ve", [B, 8])
        st6 = sb("st6", [P, NTOK, 6])
        mv_x = sb("mv_x", [P, NTOK, 2])
        var_x = sb("var_x", [P, NTOK])
        rstd_x = sb("rstd_x", [P, NTOK])
        nmr_x = sb("nmr_x", [P, NTOK])

        both = sb("both", [P, 13 * D + 2 * 6 * P + 2 * K * ROW])
        used = [0]

        def share(n):
            used[0] += n
            return both[:, used[0] - n:used[0]]

        x_t = share(2 * D).rearrange("p (b c t) -> p b c t", b=2, t=P)
        pw = share(4 * D).rearrange("p (b d) -> p b d", b=2)
        xn = share(2 * D).rearrange("p (b d) -> p b d", b=2)
        an0 = share(D)
        an = share(2 * D).rearrange("p (b d) -> p b d", b=2)
        cat = share(2 * 6 * P).rearrange("p (b c t) -> p b c t", b=2, t=P)
        yn = share(2 * D).rearrange("p (b d) -> p b d", b=2)
        y_rows = share(2 * K * ROW).rearrange("p (b k r) -> p b k r", b=2, k=K)
        st_a = sb("st_a", [P, 10])
        r_a = sb("r_a", [P, 1])
        st_y = sb("st_y", [P, 10])
        r_y = sb("r_y", [P, 1])
        lg = sb("lg", [P, E])
        top = sb("top", [P, 8])
        top_i = sb("top_i", [P, 8], U32)
        oh = sb("oh", [P, K, E])
        oh_sum = sb("oh_sum", [P, 2, E], BF16)
        seen = sb("seen", [P, 2, E], BF16)
        gap = sb("gap", [P, 1])
        nm_a = sb("nm_a", [P, 1])
        nm_y = sb("nm_y", [P, 1])
        euler = sb("euler", [P, 1])
        q_ = sb("q_", [P, 1])
        den = sb("den", [P, 1])
        pos = sb("pos", [P, E])
        pos_k = sb("pos_k", [P, K, E])
        slot_f = sb("slot_f", [P, K])
        slot = [sb(f"slot{p}", [P, K], I32) for p in range(2)]


        cnt = sb("cnt", [1, E])
        cnt_i = sb("cnt_i", [1, E], I32)
        ntile = sb("ntile", [1, E])
        t_end = sb("t_end", [1, E])
        tail_i = sb("tail_i", [1, E], I32)
        t_num = sb("t_num", [1, NT])
        t_exp = sb("t_exp", [1, NT])
        t_loc = sb("t_loc", [1, NT])
        t_tmp = sb("t_tmp", [1, NT])
        tile_exp = sb("tile_exp", [1, NT], I32)
        tile_row = sb("tile_row", [1, NT], I32)

        used[0] = 0
        xs = share(2 * ROW).rearrange("p (b r) -> p b r", b=2)
        xf = share(D)
        xsp = share(2 * D).rearrange("p (b d) -> p b d", b=2)
        width = [(c1 - c0) * P for c0, c1 in HALF]
        sg = [share(n) for n in width]
        hh = [share(n) for n in width]
        hsp = [share(n) for n in width]
        ht = [share(n) for n in width]
        yo = share(2 * D).rearrange("p (b d) -> p b d", b=2)
        weight = sb("weight", [P, 2])
        tok = [sb(f"tok{p}", [P, 1], I32) for p in range(2)]

        bank = [ctx.enter_context(nc.psum_tensor(f"bank{n}", [P, 512], F32)) for n in range(8)]

        s_row = sem("s_row")
        s_const = sem("s_const")
        s_x = sem("s_x")
        s_ids = sem("s_ids")
        s_win = sem("s_win")
        s_cond = sem("s_cond")
        s_out0 = sem("s_out0")
        s_early = [sem(f"s_early{p}") for p in range(2)]
        s_late = [sem(f"s_late{e}") for e in range(EARLY, E)]
        split_hi = sem("split_hi")
        split_lo = sem("split_lo")
        s_xt = [sem(f"s_xt{p}") for p in range(2)]
        s_pw = [sem(f"s_pw{p}") for p in range(2)]
        pro_v = sem("pro_v")
        pro_a = sem("pro_a")
        pro_p = sem("pro_p")
        pro_t = sem("pro_t")
        xn_done = sem("xn_done")
        a_step = sem("a_step")
        ra_done = sem("ra_done")
        an_done = sem("an_done")
        flip_done = sem("flip_done")
        gate_mm = sem("gate_mm")
        gate_done = sem("gate_done")
        cat_done = sem("cat_done")
        in_done = sem("in_done")
        silu_done = sem("silu_done")
        s1t_mm = sem("s1t_mm")
        s1t_done = sem("s1t_done")
        out_mm = sem("out_mm")
        ly_step = sem("ly_step")
        ry_done = sem("ry_done")
        nma_done = sem("nma_done")
        nmy_done = sem("nmy_done")
        yn_done = sem("yn_done")
        row_step = sem("row_step")
        id_step = sem("id_step")
        yt_mm = sem("yt_mm")
        yt_done = sem("yt_done")
        logit_mm = sem("logit_mm")
        top_step = sem("top_step")
        q_done = sem("q_done")
        rank_mm = sem("rank_mm")
        slot_step = sem("slot_step")
        s_scat = [sem(f"s_scat{p}") for p in range(2)]
        plan_step = sem("plan_step")
        s_tail = sem("s_tail")
        s_xs = [sem(f"s_xs{p}") for p in range(2)]
        flip_x = sem("flip_x")
        xst_done = sem("xst_done")
        xhi_done = sem("xhi_done")
        xlo_done = sem("xlo_done")
        g_mm = [sem(f"g_mm{h}") for h in range(2)]
        u_mm = [sem(f"u_mm{h}") for h in range(2)]
        sg_done = [sem(f"sg_done{h}") for h in range(2)]
        h_done = [sem(f"h_done{h}") for h in range(2)]
        hi_done = [sem(f"hi_done{h}") for h in range(2)]
        lo_done = [sem(f"lo_done{h}") for h in range(2)]
        ht_mm = [sem(f"ht_mm{h}") for h in range(2)]
        ht_done = [sem(f"ht_done{h}") for h in range(2)]
        y_mm = sem("y_mm")
        meta_step = sem("meta_step")
        yo_done = sem("yo_done")
        s_add = sem("s_add")
        idx_done = sem("idx_done")
        s_pwid = sem("s_pwid")
        relay_s, relay_p, relay_v = sem("relay_s"), sem("relay_p"), sem("relay_v")

        def units_beside(t):
            if not t.is_first(E - SPLIT_A):
                return []
            first = (SPLIT_A + t.at()) * UNITS
            return [Tile(u // 2, u % 2) for u in range(first, first + UNITS)]

        NCONST = 9
        TOPN, SLOTN, LYN, AN_ = 8, 7, 3, 5

        block = ctx.enter_context(nc.Block())

        @block.sync
        def _(sp):
            sp.dma_start(x_all, a["x"].rearrange("(t p) d -> p t d", p=P)).then_inc(s_x, 16)
            for dst, src in ((small[:], a["small"]), (pad_rows[:], a["pad_rows"])):
                sp.dma_start(dst, src).then_inc(s_row, 16)
            sp.dma_start(ids[0:KR, :], a["ids"]).then_inc(s_ids, 16)
            sp.dma_start(g_tab[0:KR, :], a["g_tab"]).then_inc(s_ids, 16)
            for dst, src in ((cond[:], a["cond"]), (c_b1[:], a["c_b1"]), (c_w1, a["c_w1"]),
                             (c_w2, a["c_w2"]), (c_vec, a["c_vec"])):
                sp.dma_start(dst, src).then_inc(s_cond, 16)
            for dst, src in ((aw[:], a["aw"]), (ident[:], a["ident"]), (before_f[:], a["before"]),
                             (ln_gb[:], a["ln_gb"]), (wgate[:], a["wgate"]), (tab_t, a["tab_t"]),
                             (b1_row, a["b1_row"]), (b1_sel, a["b1_sel"]), (t_num[:], a["tile_num"])):
                sp.dma_start(dst, src).then_inc(s_const, 16)
            sp.dma_start(w_in, a["w_in"]).then_inc(s_win, 16)
            sp.dma_start(w_out, a["w_out"]).then_inc(s_win, 16)

            def load_tile(t):
                if not t.is_first(2):
                    sp.wait_ge(in_done, t.at(1, -1))
                    sp.sem_inc(relay_s, 1)
                sp.dma_start(x_t[:, t.parity], a["x_t"][bass.ds(t.at(P), P), :]).then_inc(s_xt[t.parity], 16)
                if not t.is_first(2):
                    sp.wait_ge(s_early[t.parity], t.pair * 16)
                    sp.sem_inc(relay_s, 1)
                sp.dma_start(w_all[:, bass.ds(t.at(PIECE, SHIFT * I), PIECE)],
                             a["w_exp"][:, bass.ds(t.at(PIECE), PIECE)]).then_inc(s_early[t.parity], 16)

            pipeline(sp, load_tile, 0, NTOK, 2, 0)

            sp.dma_start(out[0:T, :], a["x"]).then_inc(s_out0, 16)
            sp.wait_ge(s_row, 32)
            sp.dma_start(out[T:T + P, :], pad_rows[:, 0:D]).then_inc(s_out0, 16)
            sp.dma_start(routed[E * REGION:E * REGION + P, :], pad_rows[:]).then_inc(s_tail, 16)
            sp.wait_ge(plan_step, PLAN)
            for e in range(E):
                row = sp.value_load(tail_i[0:1, e:e + 1], min_val=0, max_val=E * REGION - P)
                sp.dma_start(routed[bass.ds(row, P), :], pad_rows[:]).then_inc(s_tail, 16)
            sp.wait_ge(s_tail, 16 * (E + 1))
            for p in range(2):
                sp.wait_ge(s_scat[p], 16 * K * NTOK // 2)

            def load_xs(t):
                row = sp.value_load(tile_row[0:1, bass.ds(t.at(), 1)], min_val=0, max_val=E * REGION)
                if not t.is_first(2):
                    sp.wait_ge(flip_x, t.at(1, -1))
                    sp.wait_ge(meta_step, t.at(2, -2))
                    sp.sem_inc(relay_s, 1)
                sp.dma_start(xs[:, t.parity, :], routed[bass.ds(row, P), :]).then_inc(s_xs[t.parity], 16)

            load_xs(Tile(0, 0))
            load_xs(Tile(0, 1))
            for n in range(E - EARLY):
                c = (EARLY + n) * WEXP
                sp.dma_start(w_all[:, c + SHIFT * I:c + SHIFT * I + WEXP], a["w_exp"][:, c:c + WEXP]).then_inc(s_late[n], 16)
            pipeline(sp, load_xs, 2, NT, 0, 1)
            sp.wait_ge(s_add, 16 * NT)

        @block.gpsimd
        def _(pool):
            nc.gpsimd.memset(minus_half[:], -0.5).then_inc(pro_p, 1)
            nc.gpsimd.memset(euler[:], float(np.e)).then_inc(pro_p, 1)
            pool.dma_start(pw_ids[:], a["pw_ids"]).then_inc(s_pwid, 16)

            def gather_pw(t):
                if not t.is_first(2):
                    pool.wait_ge(a_step, t.at(AN_, -AN_))
                    pool.sem_inc(relay_p, 1)
                nc.gpsimd.tensor_copy(pw_idx[t.parity][:], pw_ids[:, bass.ds(t.at(), 1)]).then_inc(idx_done, 1)
                pool.wait_ge(idx_done, t.at(1, 1))
                pool.sem_inc(relay_p, 1)
                nc.gpsimd.indirect_dma_start(
                    pw[:, t.parity, :], None, a["pw_tab"],
                    bass.IndirectOffsetOnAxis(ap=pw_idx[t.parity][:, 0:1], axis=0)).then_inc(s_pw[t.parity], 16)

            def power(o, base, exponent, s):
                nc.gpsimd.tensor_tensor(o, base, exponent, ALU.pow).then_inc(s, 1)

            pool.wait_ge(s_pwid, 16)
            gather_pw(Tile(0, 0))
            gather_pw(Tile(0, 1))
            pool.wait_ge(pro_p, 2)
            pool.wait_ge(pro_v, VARX)
            power(rstd_x[:], var_x[:], minus_half[:], pro_p)
            pool.wait_ge(pro_v, CVE)
            power(c_ve[:, 3:6], c_ve[:, 0:3], minus_half[0:B, 0:3], pro_p)

            def root_a(i):
                pool.wait_ge(a_step, i.at(AN_, AN_))
                power(r_a[:], st_a[:, 8:9], minus_half[:, 0:1], ra_done)

            def root_y(i):
                pool.wait_ge(ly_step, i.at(LYN, LYN))
                power(r_y[:], st_y[:, 8:9], minus_half[:, 0:1], ry_done)

            def exp_gap(i):
                pool.wait_ge(top_step, i.at(TOPN, TOPN))
                power(q_[:], euler[:], gap[:], q_done)

            def scatter(i):
                pool.wait_ge(slot_step, i.at(SLOTN, SLOTN))
                pool.wait_ge(row_step, i.at(1, 1))
                pool.wait_ge(id_step, i.at(1, 1))
                pool.sem_inc(relay_p, 1)
                for k in range(K):
                    nc.gpsimd.indirect_dma_start(
                        routed, bass.IndirectOffsetOnAxis(ap=slot[i.parity][:, k:k + 1], axis=0),
                        y_rows[:, i.parity, k, :], None).then_inc(s_scat[i.parity], 16)

            root_a(Tile(0, 0))
            def step(n):
                for lag, work in ((2, gather_pw), (1, root_a), (-4, scatter), (-2, root_y), (-3, exp_gap)):
                    if n.plus(lag).inside(NTOK):
                        work(n.plus(lag))

            pipeline(pool, step, 0, NTOK + 4, HEAD, TAIL)

            def add_tile(t):
                if not t.is_first(1):
                    pool.wait_ge(s_add, t.at(16))
                pool.wait_ge(yo_done, t.at(1, 1))
                pool.sem_inc(relay_p, 1)
                nc.gpsimd.indirect_dma_start(
                    out, bass.IndirectOffsetOnAxis(ap=tok[t.parity][:, 0:1], axis=0),
                    yo[:, t.parity, :], None, compute_op=ALU.add).then_inc(s_add, 16)

            pool.wait_ge(s_out0, 32)
            pipeline(pool, add_tile, 0, NT, 1, 0)

        @block.scalar
        def _(act):
            act.wait_ge(pro_v, CSH)
            nc.scalar.activation(c_sh[:], c_sh[:], ACT.Silu).then_inc(pro_a, 1)
            act.wait_ge(pro_v, AWS)
            nc.scalar.activation(aw[:], aw[:], ACT.Exp).then_inc(pro_a, 1)
            act.wait_ge(pro_v, NMX)

            def norm_x(i):
                if not i.is_first(2):
                    act.wait_ge(flip_done, i.at(1, -1))
                    act.wait_ge(a_step, i.at(AN_, -AN_))
                c = bass.ds(i.at(), 1)
                nc.scalar.activation(xn[:, i.parity, :], x_all[:, c, :].rearrange("p o d -> p (o d)"), ACT.Identity,
                                     bias=nmr_x[:, c], scale=rstd_x[:, c]).then_inc(xn_done, 1)

            def norm_a(i):
                act.wait_ge(nma_done, i.at(1, 1))
                if not i.is_first(2):
                    act.wait_ge(flip_done, i.at(1, -1))
                nc.scalar.activation(an[:, i.parity, :], an0, ACT.Identity, bias=nm_a[:], scale=r_a[:]).then_inc(an_done, 1)

            def copy_s1(i):
                act.wait_ge(s1t_mm, i.at(1, 1))
                nc.scalar.copy(s1_t.rearrange("p c t -> p (c t)"), bank[4][:, 0:D]).then_inc(s1t_done, 1)

            def copy_gates(i):
                act.wait_ge(gate_mm, i.at(1, 1))
                if not i.is_first():
                    act.wait_ge(cat_done, i.at(2))
                nc.scalar.copy(gate_s[:, 0:2 * D], bank[1][:, :]).then_inc(gate_done, 1)
                nc.scalar.copy(gate_s[:, 2 * D:3 * D], bank[2][:, 0:D]).then_inc(gate_done, 1)

            def affine_y(i):
                act.wait_ge(yt_mm, i.at(1, 1))
                if not i.is_first():
                    act.wait_ge(logit_mm, i.at())
                for f in range(DC):
                    nc.scalar.activation(y_t[:, f, :], bank[6][:, f * P:(f + 1) * P], ACT.Identity,
                                         bias=ln_gb[:, 1, f:f + 1], scale=ln_gb[:, 0, f:f + 1]).then_inc(yt_done, 1)

            def silu_1(i):
                act.wait_ge(in_done, i.at(1, 1))
                if not i.is_first():
                    act.wait_ge(s1t_mm, i.at())
                nc.scalar.activation(s1, bank[3][:, 0:D], ACT.Silu).then_inc(silu_done, 1)

            def norm_y(i):
                act.wait_ge(nmy_done, i.at(1, 1))
                if not i.is_first(2):
                    act.wait_ge(yt_mm, i.at(1, -1))
                nc.scalar.activation(yn[:, i.parity, :], bank[5][:, 0:D], ACT.Identity, bias=nm_y[:], scale=r_y[:]).then_inc(yn_done, 1)

            def copy_rows(i):
                act.wait_ge(yn_done, i.at(1, 1))
                if not i.is_first(2):
                    act.wait_ge(s_scat[i.parity], i.pair * (16 * K))
                for k in range(K):
                    last = nc.scalar.copy(y_rows[:, i.parity, k, 0:D], yn[:, i.parity, :])
                last.then_inc(row_step, 1)

            norm_x(Tile(0, 0))
            norm_x(Tile(0, 1))
            norm_a(Tile(0, 0))

            def round_unit(u):
                if isinstance(u.pair, int) and u.at() >= EARLY * UNITS:
                    act.wait_ge(s_late[u.at() // UNITS - EARLY], 16)
                elif isinstance(u.pair, int) and u.at() >= NTOK:
                    for p in range(2):
                        act.wait_ge(s_early[p], 16 * NTOK // 2)
                else:
                    act.wait_ge(s_early[u.parity], u.pair * 16 + 16)
                if not u.is_first(SHIFT):
                    act.wait_ge(split_lo, u.at(1, 1 - SHIFT))
                nc.scalar.copy(w_hi[:, bass.ds(u.at(2 * I), I)],
                               w_all[:, bass.ds(u.at(I, SHIFT * I), I)]).then_inc(split_hi, 1)

            def step(n):
                for lag, work in ((-2, copy_s1), (-3, affine_y), (0, copy_gates), (2, norm_x), (-2, round_unit),
                                  (1, norm_a), (-3, copy_rows), (-1, silu_1), (-2, norm_y)):
                    if n.plus(lag).inside(SPLIT_A * UNITS if work is round_unit else NTOK):
                        work(n.plus(lag))

            pipeline(act, step, 0, NTOK + 4, HEAD, TAIL)

            def silu(t, h):
                n = (HALF[h][1] - HALF[h][0]) * P
                act.wait_ge(g_mm[h], t.at(1, 1))
                if not t.is_first():
                    act.wait_ge(h_done[h], t.at())
                nc.scalar.activation(sg[h], bank[2 * h][:, 0:n], ACT.Silu).then_inc(sg_done[h], 1)

            def round_h(t, h):
                n = width[h]
                act.wait_ge(h_done[h], t.at(1, 1))
                if not t.is_first():
                    act.wait_ge(ht_mm[h], t.at())
                nc.scalar.copy(hsp[h].bitcast(F16)[:, 0:n], hh[h]).then_inc(hi_done[h], 1)

            def affine_xs(t):
                act.wait_ge(flip_x, t.at(1, 1))
                if not t.is_first():
                    act.wait_ge(xlo_done, t.at())
                for f in range(DC):
                    cols = slice(f * P, (f + 1) * P)
                    nc.scalar.activation(xf[:, cols], bank[7][:, cols], ACT.Identity, bias=ln_gb[:, 1, f:f + 1],
                                         scale=ln_gb[:, 0, f:f + 1]).then_inc(xst_done, 1)

            def round_xs(t):
                act.wait_ge(xst_done, t.at(2, 2))
                if not t.is_first(2):
                    act.wait_ge(u_mm[1], t.at(1, -1))
                nc.scalar.copy(xsp[:, t.parity].bitcast(F16)[:, 0:D], xf).then_inc(xhi_done, 1)

            def expert_step(t):
                units = units_beside(t)
                silu(t, 0)
                for u in units[0:1]:
                    round_unit(u)
                round_h(t, 0)
                for u in units[1:2]:
                    round_unit(u)
                if not (isinstance(t.pair, int) and t.at() == NT - 1):
                    affine_xs(t.plus(1))
                    round_xs(t.plus(1))
                for u in units[2:3]:
                    round_unit(u)
                silu(t, 1)
                for u in units[3:4]:
                    round_unit(u)
                round_h(t, 1)
                for u in units[4:]:
                    round_unit(u)

            affine_xs(Tile(0, 0))
            round_xs(Tile(0, 0))
            pipeline(act, expert_step, 0, NT, E - SPLIT_A, 2)

        @block.vector
        def _(dve):
            done = [0]

            def did(ins):
                done[0] += 1
                ins.then_inc(pro_v, 1)

            def after(n=None):
                dve.wait_ge(pro_v, done[0] if n is None else n)

            dve.wait_ge(s_x, 16)
            for t in range(NTOK):
                did(nc.vector.bn_stats(st6[:, t, :], x_all[:, t, :]))
            after()
            for t in range(NTOK):
                did(nc.vector.bn_aggr(mv_x[:, t, :], st6[:, t, :]))
            after()
            did(nc.vector.tensor_scalar(var_x[:], mv_x[:, :, 1], EPS, None, ALU.add))
            assert done[0] == VARX, done[0]
            did(nc.vector.memset(gates[:].bitcast(I32), 0))
            did(nc.vector.memset(shifts[:].bitcast(I32), 0))
            did(nc.vector.memset(seen[:, 0, :], 0.0))
            did(nc.vector.memset(ones[:], 1.0))
            dve.wait_ge(s_row, 32)
            dve.wait_ge(s_ids, 32)
            did(nc.vector.tensor_scalar(onehot[0:KR, :], ids[0:KR, :], row_id[0:KR, :], None, ALU.is_equal))

            def split(table, width, stacked):
                def rows(v, n):
                    return v[32 * n:32 * n + ROWS, 0:width]
                after()
                did(nc.vector.tensor_copy(rows(stacked, 0), rows(table, 0)))
                did(nc.vector.tensor_copy(t_bf[0:KR, 0:width], table[0:KR, 0:width]))
                after()
                did(nc.vector.tensor_tensor(t_rest[0:KR, 0:width], table[0:KR, 0:width], t_bf[0:KR, 0:width], ALU.subtract))
                after()
                did(nc.vector.tensor_copy(rows(stacked, 1), rows(t_rest, 1)))
                did(nc.vector.tensor_copy(t_bf[0:KR, 0:width], t_rest[0:KR, 0:width]))
                after()
                did(nc.vector.tensor_tensor(t_part[0:KR, 0:width], t_rest[0:KR, 0:width], t_bf[0:KR, 0:width], ALU.subtract))
                after()
                did(nc.vector.tensor_copy(rows(stacked, 2), rows(t_part, 2)))

            split(g_tab, 4 * D, gates)
            dve.wait_ge(pro_p, 3)
            did(nc.vector.scalar_tensor_tensor(nmr_x[:], mv_x[:, :, 0], -1.0, rstd_x[:], ALU.mult, ALU.mult))
            assert done[0] == NMX, done[0]
            dve.wait_ge(s_cond, 16 * 5)
            dve.wait_ge(pro_t, 1)
            did(nc.vector.tensor_tensor(c_sh[:], bank[0][:, 0:6 * B], c_b1[:], ALU.add))
            assert done[0] == CSH, done[0]
            dve.wait_ge(s_const, 16 * NCONST)
            did(nc.vector.tensor_reduce(aw_s[:, 0:1], aw[:], AX.X, ALU.max))
            did(nc.vector.tensor_copy(before[:], before_f[:]))
            did(nc.vector.tensor_copy(ident_h[:], ident[:]))
            did(nc.vector.tensor_copy(ident_l[:], ident[:]))
            after()
            did(nc.vector.tensor_scalar(aw[:], aw[:], aw_s[:, 0:1], None, ALU.subtract))
            assert done[0] == AWS, done[0]
            dve.wait_ge(pro_t, 2)
            did(nc.vector.tensor_tensor(c_h[:, 0:2, :].rearrange("b c d -> b (c d)"), bank[1][0:B, :], c_vec[:, 0, 0:2 * D], ALU.add))
            did(nc.vector.tensor_tensor(c_h[:, 2, :], bank[2][0:B, 0:D], c_vec[:, 0, 2 * D:3 * D], ALU.add))
            after()
            for c in range(3):
                did(nc.vector.bn_stats(c_st[:, c, 0:6], c_h[:, c, :]))
            after()
            for c in range(3):
                did(nc.vector.bn_aggr(c_st[:, c, 6:8], c_st[:, c, 0:6]))
            after()
            did(nc.vector.tensor_scalar(c_ve[:, 0:3], c_st[:, :, 7], EPS, None, ALU.add))
            assert done[0] == CVE, done[0]
            dve.wait_ge(pro_a, 2)
            did(nc.vector.tensor_reduce(aw_s[:, 1:2], aw[:], AX.X, ALU.add))
            after()
            did(nc.vector.reciprocal(aw_s[:, 2:3], aw_s[:, 1:2]))
            after()
            did(nc.vector.tensor_scalar(aw[:], aw[:], aw_s[:, 2:3], None, ALU.mult))
            after()
            dve.wait_ge(s_win, 32)
            for c in range(6):
                w2 = w_in[:, 2 * c:2 * c + 2, :]
                did(nc.vector.tensor_scalar(w2, w2, aw[:, c:c + 1], None, ALU.mult))
            dve.wait_ge(pro_p, 4)
            for c in range(3):
                did(nc.vector.tensor_scalar(c_h[:, c, :], c_h[:, c, :], c_st[:, c, 6:7], c_ve[:, 3 + c:4 + c], ALU.subtract, ALU.mult))
            after()
            ch = c_h.rearrange("b c d -> b (c d)")
            did(nc.vector.tensor_tensor(ch, ch, c_vec[:, 1, :], ALU.mult))
            after()
            did(nc.vector.tensor_tensor(ch, ch, c_vec[:, 2, :], ALU.add))
            assert done[0] == CLN, done[0]
            dve.wait_ge(pro_t, 3)
            for n in range(PARTS):
                o = 32 * n + ROWS - B
                did(nc.vector.tensor_copy(tab_t[:, 4:10, o:o + B], bank[3][:, 0:6 * B].rearrange("p (c b) -> p c b", b=B)))
            assert done[0] == CTT, done[0]

            def affine_a(i):
                def w(n):
                    dve.wait_ge(a_step, i.at(AN_, n))
                p = i.parity
                dve.wait_ge(xn_done, i.at(1, 1))
                dve.wait_ge(s_pw[p], i.pair * 16 + 16)
                if not i.is_first():
                    dve.wait_ge(an_done, i.at())
                nc.vector.tensor_tensor(an0, xn[:, p, :], pw[:, p, 0:D], ALU.mult).then_inc(a_step, 1)
                yield
                w(1)
                nc.vector.tensor_tensor(an0, an0, pw[:, p, D:2 * D], ALU.add).then_inc(a_step, 1)
                yield
                w(2)
                nc.vector.bn_stats(st_a[:, 0:6], an0).then_inc(a_step, 1)
                yield
                w(3)
                dve.sem_inc(relay_v, 1)
                nc.vector.bn_aggr(st_a[:, 6:8], st_a[:, 0:6]).then_inc(a_step, 1)
                yield
                w(4)
                nc.vector.tensor_scalar(st_a[:, 8:9], st_a[:, 7:8], EPS, None, ALU.add).then_inc(a_step, 1)

            def bias_a(i):
                dve.wait_ge(ra_done, i.at(1, 1))
                nc.vector.tensor_scalar(nm_a[:], st_a[:, 6:7], -1.0, r_a[:], ALU.mult, ALU.mult).then_inc(nma_done, 1)

            side_by_side(affine_a(Tile(0, 0)))
            bias_a(Tile(0, 0))
            dve.wait_ge(pro_t, 4)
            did(nc.vector.tensor_copy(g_tab[0:KR, 0:D], bank[4][0:KR, 0:D]))
            split(g_tab, D, shifts)
            for c in (6, 8):
                after()
                did(nc.vector.tensor_tensor(w_in[:, 4:6, :], w_in[:, 4:6, :], w_in[:, c:c + 2, :], ALU.add))
            assert done[0] == NMR, done[0]

            def gain(i):
                dve.wait_ge(flip_done, i.at(1, 1))
                dve.wait_ge(gate_done, i.at(2, 2))
                if not i.is_first(2):
                    dve.wait_ge(in_done, i.at(1, -1))
                c = cat[:, i.parity].rearrange("p c t -> p (c t)")
                nc.vector.tensor_tensor(c[:, 0:2 * D], gate_s[:, 0:2 * D], bank[0][:, :], ALU.mult).then_inc(cat_done, 1)
                nc.vector.tensor_tensor(c[:, 2 * D:3 * D], gate_s[:, 2 * D:3 * D], bank[0][:, D:2 * D], ALU.mult).then_inc(cat_done, 1)

            def stats_y(i):
                def w(n):
                    dve.wait_ge(ly_step, i.at(LYN, n))
                dve.wait_ge(out_mm, i.at(1, 1))
                dve.sem_inc(relay_v, 1)
                nc.vector.bn_stats(st_y[:, 0:6], bank[5][:, 0:D]).then_inc(ly_step, 1)
                yield
                w(1)
                dve.sem_inc(relay_v, 1)
                nc.vector.bn_aggr(st_y[:, 6:8], st_y[:, 0:6]).then_inc(ly_step, 1)
                yield
                w(2)
                nc.vector.tensor_scalar(st_y[:, 8:9], st_y[:, 7:8], EPS, None, ALU.add).then_inc(ly_step, 1)

            def bias_y(i):
                dve.wait_ge(ry_done, i.at(1, 1))
                if not i.is_first():
                    dve.wait_ge(yn_done, i.at())
                nc.vector.tensor_scalar(nm_y[:], st_y[:, 6:7], -1.0, r_y[:], ALU.mult, ALU.mult).then_inc(nmy_done, 1)

            def number_rows(i):
                if not i.is_first(2):
                    dve.wait_ge(s_scat[i.parity], i.pair * (16 * K))
                nc.vector.tensor_copy(y_rows[:, i.parity, :, D + 1],
                                      token_id[:, bass.ds(i.at(), 1)].broadcast_to([P, K])).then_inc(id_step, 1)

            def route(i):
                def w(n):
                    dve.wait_ge(top_step, i.at(TOPN, n))
                def s(ins):
                    ins.then_inc(top_step, 1)
                p = i.parity
                dve.wait_ge(logit_mm, i.at(1, 1))
                s(nc.vector.tensor_copy(lg[:], bank[7][:, 0:E]))
                yield
                w(1)
                dve.sem_inc(relay_v, 1)
                s(nc.vector.max(top[:], lg[:]))
                yield
                w(2)
                dve.sem_inc(relay_v, 1)
                s(nc.vector.max_index(top_i[:], top[:], lg[:]))
                s(nc.vector.tensor_tensor(gap[:], top[:, 1:2], top[:, 0:1], ALU.subtract))
                yield
                w(3)
                for k in range(K):
                    s(nc.vector.tensor_scalar(oh[:, k, :], iota_e, top_i[:, k:k + 1], None, ALU.is_equal))
                yield
                w(6)
                if not i.is_first(2):
                    dve.wait_ge(rank_mm, i.at(1, -1))
                s(nc.vector.tensor_tensor(oh_sum[:, p, :], oh[:, 0, :], oh[:, 1, :], ALU.add))
                yield
                w(7)
                if not i.is_first():
                    dve.wait_ge(rank_mm, i.at())
                s(nc.vector.tensor_tensor(seen[:, 1 - p, :], seen[:, p, :], oh_sum[:, p, :], ALU.add))

            def slots(i):
                def w(n):
                    dve.wait_ge(slot_step, i.at(SLOTN, n))
                def s(ins):
                    ins.then_inc(slot_step, 1)
                p = i.parity
                dve.wait_ge(rank_mm, i.at(1, 1))
                dve.wait_ge(q_done, i.at(1, 1))
                s(nc.vector.tensor_scalar(den[:], q_[:], 1.0, None, ALU.add))
                s(nc.vector.tensor_tensor(pos[:], bank[7][:, 0:E], region_e, ALU.add))
                yield
                w(1)
                s(nc.vector.reciprocal(y_rows[:, p, 0, D:D + 1], den[:]))
                w(2)
                for k in range(K):
                    s(nc.vector.tensor_tensor_reduce(out=pos_k[:, k, :], in0=pos[:], in1=oh[:, k, :], scale=1.0, scalar=0.0,
                                                     op0=ALU.mult, op1=ALU.add, accum_out=slot_f[:, k:k + 1]))
                yield
                w(3)
                s(nc.vector.tensor_tensor(y_rows[:, p, 1, D:D + 1], q_[:], y_rows[:, p, 0, D:D + 1], ALU.mult))
                yield
                w(5)
                s(nc.vector.tensor_copy(slot[p][:], slot_f[:]))

            def rest_of_unit(u):
                dve.wait_ge(split_hi, u.at(1, 1))
                nc.vector.tensor_tensor(w_lo[:, bass.ds(u.at(2 * I, I), I)], w_all[:, bass.ds(u.at(I, SHIFT * I), I)],
                                        w_hi[:, bass.ds(u.at(2 * I), I)], ALU.subtract).then_inc(split_lo, 1)

            def step(n):
                def alive(*work):
                    return [f(n.plus(lag)) for lag, f in work if n.plus(lag).inside(NTOK)]
                side_by_side(*alive((1, affine_a), (-4, slots)))
                alive((0, gain), (1, bias_a), (-3, number_rows))
                side_by_side(*alive((-2, stats_y), (-3, route)))
                alive((-2, bias_y))
                if n.plus(-3).inside(SPLIT_A * UNITS):
                    rest_of_unit(n.plus(-3))

            pipeline(dve, step, 0, NTOK + 4, HEAD, TAIL)
            rest_of_unit(Tile(SPLIT_A * UNITS // 2 - 1, 1))

            planned = [0]

            def plan(ins):
                planned[0] += 1
                ins.then_inc(plan_step, 1)
                dve.wait_ge(plan_step, planned[0])

            dve.wait_ge(rank_mm, NTOK + 1)
            plan(nc.vector.tensor_copy(cnt[:], bank[7][0:1, 0:E]))
            plan(nc.vector.tensor_scalar(cnt_i[:], cnt[:], float(P - 1), float(P), ALU.add, ALU.max))
            plan(nc.vector.tensor_scalar(cnt_i[:], cnt_i[:], 7, None, ALU.logical_shift_right))
            plan(nc.vector.tensor_copy(ntile[:], cnt_i[:]))
            plan(nc.vector.tensor_tensor_scan(t_end[:], ones[0:1, 0:E], ntile[:], 0.0, ALU.mult, ALU.add))
            plan(nc.vector.tensor_tensor(tail_i[:], cnt[:], region_e[0:1, :], ALU.add))
            plan(nc.vector.memset(t_exp[:], 0.0))
            plan(nc.vector.tensor_copy(t_loc[:], t_num[:]))
            for e in range(E):
                plan(nc.vector.tensor_scalar(t_tmp[:], t_num[:], t_end[:, e:e + 1], None, ALU.is_ge))
                plan(nc.vector.tensor_tensor(t_exp[:], t_exp[:], t_tmp[:], ALU.add))
                plan(nc.vector.tensor_scalar(t_tmp[:], t_tmp[:], ntile[:, e:e + 1], None, ALU.mult))
                plan(nc.vector.tensor_tensor(t_loc[:], t_loc[:], t_tmp[:], ALU.subtract))
            plan(nc.vector.tensor_scalar(t_loc[:], t_loc[:], float(P), None, ALU.mult))
            plan(nc.vector.tensor_scalar(t_tmp[:], t_exp[:], float(REGION), None, ALU.mult))
            plan(nc.vector.tensor_tensor(t_loc[:], t_loc[:], t_tmp[:], ALU.add))
            plan(nc.vector.tensor_scalar(t_loc[:], t_loc[:], float(E * REGION), None, ALU.min))
            plan(nc.vector.tensor_copy(tile_row[:], t_loc[:]))
            plan(nc.vector.tensor_scalar(tile_exp[:], t_exp[:], float(E - 1), None, ALU.min))
            assert planned[0] == PLAN, planned[0]

            def rest_of_xs(t):
                dve.wait_ge(xhi_done, t.at(1, 1))
                halves = xsp[:, t.parity]
                nc.vector.tensor_tensor(halves.bitcast(BF16)[:, D:2 * D], xf, halves.bitcast(F16)[:, 0:D],
                                        ALU.subtract).then_inc(xlo_done, 1)

            def hidden(t, h):
                dve.wait_ge(u_mm[h], t.at(1, 1))
                dve.wait_ge(sg_done[h], t.at(1, 1))
                if not t.is_first():
                    dve.wait_ge(lo_done[h], t.at())
                nc.vector.tensor_tensor(hh[h], sg[h], bank[2 * h + 1][:, 0:width[h]], ALU.mult).then_inc(h_done[h], 1)

            def rest_of_h(t, h):
                n = width[h]
                dve.wait_ge(hi_done[h], t.at(1, 1))
                nc.vector.tensor_tensor(hsp[h].bitcast(BF16)[:, n:2 * n], hh[h], hsp[h].bitcast(F16)[:, 0:n],
                                        ALU.subtract).then_inc(lo_done[h], 1)

            def copy_ht(t, h):
                dve.wait_ge(ht_mm[h], t.at(1, 1))
                if not t.is_first():
                    dve.wait_ge(y_mm, t.at())
                nc.vector.tensor_copy(ht[h].bitcast(I32), bank[4 + h][:, 0:width[h]].bitcast(I32)).then_inc(ht_done[h], 1)

            def meta(t):
                p = t.parity
                if not t.is_first(2):
                    dve.wait_ge(s_add, t.at(16, -16))
                nc.vector.tensor_copy(tok[p][:], xs[:, p, D + 1:D + 2]).then_inc(meta_step, 1)
                nc.vector.tensor_copy(weight[:, p:p + 1], xs[:, p, D:D + 1]).then_inc(meta_step, 1)

            def weigh(t):
                p = t.parity
                dve.wait_ge(y_mm, t.at(1, 1))
                dve.wait_ge(meta_step, t.at(2, 2))
                nc.vector.tensor_scalar(yo[:, p, :], bank[6][:, 0:D], weight[:, p:p + 1], None, ALU.mult).then_inc(yo_done, 1)

            def expert_step(t):
                units = units_beside(t)
                hidden(t, 0)
                for u in units[0:1]:
                    rest_of_unit(u)
                if not t.is_first():
                    copy_ht(t.plus(-1), 1)
                rest_of_h(t, 0)
                for u in units[1:2]:
                    rest_of_unit(u)
                if not (isinstance(t.pair, int) and t.at() == NT - 1):
                    rest_of_xs(t.plus(1))
                for u in units[2:3]:
                    rest_of_unit(u)
                meta(t)
                hidden(t, 1)
                for u in units[3:4]:
                    rest_of_unit(u)
                if not t.is_first():
                    weigh(t.plus(-1))
                rest_of_h(t, 1)
                for u in units[4:]:
                    rest_of_unit(u)
                copy_ht(t, 0)

            rest_of_xs(Tile(0, 0))
            pipeline(dve, expert_step, 0, NT, E - SPLIT_A, 2)
            t = Tile((NT - 1) // 2, (NT - 1) % 2)
            copy_ht(t, 1)
            weigh(t)

        @block.tensor
        def _(pe):
            mm = nc.tensor.matmul
            pe.wait_ge(s_cond, 16 * 5)
            for c in range(3):
                for f in range(DC):
                    o = (c * DC + f) * B
                    last = mm(bank[0][:, o:o + B], c_w1[:, c, f * P:(f + 1) * P], cond[:, c * B:(c + 1) * B],
                              start=True, stop=True)
            last.then_inc(pro_t, 1)
            pe.wait_ge(pro_a, 1)
            for c in range(3):
                for f in range(DC):
                    o = (c * DC + f) * B
                    last = mm(bank[1 + c // 2][0:B, (c % 2) * D:(c % 2 + 1) * D], c_sh[:, o:o + B],
                              c_w2[:, c * DC + f, :], start=(f == 0), stop=(f == DC - 1))
            last.then_inc(pro_t, 1)
            pe.wait_ge(pro_v, CLN)
            pe.wait_ge(s_const, 16 * NCONST)
            for c in range(3):
                for f in range(DC):
                    o = (c * DC + f) * B
                    last = nc.tensor.transpose(bank[3][:, o:o + B], c_h[:, c, f * P:(f + 1) * P], ident[0:B, 0:B])
            last.then_inc(pro_t, 1)
            pe.wait_ge(pro_v, CTT)
            for c in range(12):
                mm(bank[4][0:KR, 0:D], tab_t[:, c, :], w_in[:, c, :], start=(c == 0), stop=False)
            mm(bank[4][0:KR, 0:D], b1_sel[:], b1_row[:], start=False, stop=True).then_inc(pro_t, 1)
            def flip(i):
                p = i.parity
                pe.wait_ge(an_done, i.at(1, 1))
                pe.wait_ge(xn_done, i.at(1, 1))
                if not i.is_first():
                    pe.wait_ge(cat_done, i.at(2))
                    pe.wait_ge(gate_done, i.at(2))
                for n, src in enumerate((an, an, xn, xn)):
                    f = n % DC
                    last = nc.tensor.transpose(bank[0][:, n * P:(n + 1) * P], src[:, p, f * P:(f + 1) * P], ident[:])
                last.then_inc(flip_done, 1)
                cols = onehot[0:KR, bass.ds(i.at(P), P)]
                for n in range(6):
                    b, o = (bank[1], n) if n < 4 else (bank[2], n - 4)
                    last = mm(b[:, o * P:(o + 1) * P], gates[:, n * P:(n + 1) * P], cols, start=True, stop=True)
                last.then_inc(gate_mm, 1)

            def integrate(i):
                p = i.parity
                pe.wait_ge(cat_done, i.at(2, 2))
                if i.is_first():
                    pe.wait_ge(pro_v, NMR)
                if not i.is_first():
                    pe.wait_ge(silu_done, i.at())
                pe.wait_ge(s_xt[p], i.pair * 16 + 16)
                o = bank[3][:, 0:D]
                mm(o, onehot[0:KR, bass.ds(i.at(P), P)], shifts[:], start=True, stop=False)
                for n, c in enumerate((0, 1, 2, 3, 10, 11)):
                    mm(o, cat[:, p, n, :], w_in[:, c, :], start=False, stop=False)
                for f in range(DC):
                    last = mm(o, x_t[:, p, f, :], w_in[:, 4 + f, :], start=False, stop=(f == DC - 1))
                last.then_inc(in_done, 1)

            def flip_s(i):
                pe.wait_ge(silu_done, i.at(1, 1))
                if not i.is_first():
                    pe.wait_ge(s1t_done, i.at())
                for f in range(DC):
                    last = nc.tensor.transpose(bank[4][:, f * P:(f + 1) * P], s1[:, f * P:(f + 1) * P], ident[:])
                last.then_inc(s1t_mm, 1)

            def flip_y(i):
                pe.wait_ge(yn_done, i.at(1, 1))
                if not i.is_first():
                    pe.wait_ge(yt_done, i.at(2))
                for f in range(DC):
                    last = nc.tensor.transpose(bank[6][:, f * P:(f + 1) * P], yn[:, i.parity, f * P:(f + 1) * P], ident[:])
                last.then_inc(yt_mm, 1)

            def project(i):
                pe.wait_ge(s1t_done, i.at(1, 1))
                if not i.is_first():
                    pe.wait_ge(yn_done, i.at())
                o = bank[5][:, 0:D]
                mm(o, onehot[0:KR, bass.ds(i.at(P), P)], gates[:, 3 * D:4 * D], start=True, stop=False)
                for f in range(DC):
                    last = mm(o, s1_t[:, f, :], w_out[:, f, :], start=False, stop=(f == DC - 1))
                last.then_inc(out_mm, 1)

            def logits(i):
                pe.wait_ge(yt_done, i.at(2, 2))
                if not i.is_first():
                    pe.wait_ge(slot_step, i.at(SLOTN))
                for f in range(DC):
                    last = mm(bank[7][:, 0:E], y_t[:, f, :], wgate[:, f, :], start=(f == 0), stop=(f == DC - 1))
                last.then_inc(logit_mm, 1)

            def rank(i):
                p = i.parity
                pe.wait_ge(top_step, i.at(TOPN, TOPN))
                mm(bank[7][:, 0:E], before[:], oh_sum[:, p, :], start=True, stop=False)
                mm(bank[7][:, 0:E], ones[:], seen[:, p, :], start=False, stop=True).then_inc(rank_mm, 1)

            def step(n):
                for lag, work in ((-4, rank), (0, flip), (-2, flip_s), (-3, flip_y), (-2, project),
                                  (-3, logits), (-1, integrate)):
                    if n.plus(lag).inside(NTOK):
                        work(n.plus(lag))

            pipeline(pe, step, 0, NTOK + 4, HEAD, TAIL)
            pe.wait_ge(slot_step, SLOTN * NTOK)
            mm(bank[7][:, 0:E], ones[:], seen[:, NTOK % 2, :], start=True, stop=True).then_inc(rank_mm, 1)

            pe.wait_ge(plan_step, PLAN)

            def expert_of(t):
                return pe.value_load(tile_exp[0:1, bass.ds(t.at(), 1)], min_val=0, max_val=E - 1)

            def products(o, x_hi, x_lo, e, unit, start, n, first, last):
                def w(v, half):
                    return v[:, bass.ds(e * (2 * WEXP) + (2 * unit + half) * I + start, n)]
                mm(o, x_hi, w(w_hi, 0), start=first, stop=False)
                mm(o, x_hi, w(w_lo, 1), start=False, stop=False)
                return mm(o, x_lo, w(w_hi, 0), start=False, stop=last)

            def flip_in(t):
                pe.wait_ge(s_xs[t.parity], t.pair * 16 + 16)
                if not t.is_first():
                    pe.wait_ge(xst_done, t.at(2))
                for f in range(DC):
                    last = nc.tensor.transpose(bank[7][:, f * P:(f + 1) * P], xs[:, t.parity, f * P:(f + 1) * P], ident[:])
                last.then_inc(flip_x, 1)

            def gate_up(t, e, h):
                c0, c1 = HALF[h]
                n = (c1 - c0) * P
                halves = xsp[:, t.parity]
                if h == 0:
                    pe.wait_ge(xlo_done, t.at(1, 1))
                for m, (s_free, s_full) in enumerate(((sg_done[h], g_mm[h]), (h_done[h], u_mm[h]))):
                    if not t.is_first():
                        pe.wait_ge(s_free, t.at())
                    for f in range(DC):
                        last = products(bank[2 * h + m][:, 0:n], halves.bitcast(F16)[:, f * P:(f + 1) * P],
                                        halves.bitcast(BF16)[:, D + f * P:D + (f + 1) * P],
                                        e, f * 2 + m, c0 * P, n, f == 0, f == DC - 1)
                    last.then_inc(s_full, 1)

            def flip_h(t, h):
                c0, c1 = HALF[h]
                pe.wait_ge(hi_done[h], t.at(1, 1))
                pe.wait_ge(lo_done[h], t.at(1, 1))
                if not t.is_first():
                    pe.wait_ge(ht_done[h], t.at())
                n = c1 - c0
                for dt, unit, chunks in ((F16, ident_h, range(n)), (BF16, ident_l, range(n, 2 * n))):
                    for c in chunks:
                        cols = slice(c * P, (c + 1) * P)
                        last = nc.tensor.transpose(bank[4 + h][:, 0:width[h]].bitcast(dt)[:, cols],
                                                   hsp[h].bitcast(dt)[:, cols], unit[:])
                last.then_inc(ht_mm[h], 1)

            def down(t, e, h):
                c0, c1 = HALF[h]
                pe.wait_ge(ht_done[h], t.at(1, 1))
                if h == 0 and not t.is_first():
                    pe.wait_ge(yo_done, t.at())
                n = c1 - c0
                for c in range(c0, c1):
                    hi = ht[h].bitcast(F16)[:, (c - c0) * P:(c - c0 + 1) * P]
                    lo = ht[h].bitcast(BF16)[:, (n + c - c0) * P:(n + c - c0 + 1) * P]
                    done = 0
                    while done < D:
                        unit, start = divmod(c * D + done, I)
                        part = min(D - done, I - start)
                        last = products(bank[6][:, done:done + part], hi, lo, e, 2 * DC + unit, start, part,
                                        c == 0, c == IC - 1)
                        done += part
                if h == 1:
                    last.then_inc(y_mm, 1)

            def expert_step(t):
                before_t = t.plus(-1)
                e = expert_of(t)
                pe.wait_ge(split_lo, e * UNITS + UNITS)
                gate_up(t, e, 0)
                if not t.is_first():
                    e_b = expert_of(before_t)
                    flip_h(before_t, 1)
                    down(before_t, e_b, 0)
                if not (isinstance(t.pair, int) and t.at() == NT - 1):
                    flip_in(t.plus(1))
                gate_up(t, e, 1)
                if not t.is_first():
                    down(before_t, e_b, 1)
                flip_h(t, 0)

            flip_in(Tile(0, 0))
            pipeline(pe, expert_step, 0, NT, 3, 2)
            t = Tile((NT - 1) // 2, (NT - 1) % 2)
            e = expert_of(t)
            flip_h(t, 1)
            down(t, e, 0)
            down(t, e, 1)


VARX = 2 * NTOK + 1
NMX = VARX + 5 + 7 + 1
CSH = NMX + 1
AWS = CSH + 5
CVE = AWS + 2 + 6 + 1
CLN = CVE + 3 + 6 + 5
CTT = CLN + 3
NMR = CTT + 1 + 7 + 2
HEAD, TAIL = 6, 6
PLAN = 8 + 4 * E + 6


def kernel(**v):
    import numpy as _np
    import concourse.bacc as _bacc
    from concourse.bass_utils import run_bass_kernel_spmd as _run

    v = {k: _np.asarray(x) for k, x in v.items()}
    f = _np.float32

    def part(w):
        return w.reshape(-1, P, w.shape[-1]).transpose(1, 0, 2)

    h = {}
    x = v["x"].reshape(T, D)
    h["x"] = x
    h["x_t"] = x.reshape(NTOK, P, DC, P).transpose(0, 3, 2, 1).reshape(NTOK * P, DC * P)
    h["pw_tab"] = _np.concatenate([v["L0_cond_pw_g"], v["L0_cond_pw_b"]], axis=1)
    h["pw_ids"] = v["itok_BxS_0_999"].reshape(NTOK, P).T
    comp, scale = v["itok_BxS_0_4"].reshape(T), v["mask_BxS_ik0"].reshape(T)
    ids = _np.full((KR, T), -1, _np.int32)
    g_tab = _np.zeros((KR, 4 * D), f)
    row_id = _np.zeros((P, 1), f)
    tab_t = _np.zeros((P, 12, KR), f)
    b1_sel = _np.zeros((1, KR), f)
    for n in range(PARTS):
        o = 32 * n
        ids[o:o + NCOMP] = comp
        ids[o + NCOMP:o + NCOMP + NSCALE] = scale
        ids[o + ROWS - B:o + ROWS] = _np.repeat(_np.arange(B, dtype=_np.int32), S)
        g_tab[o:o + NCOMP, 0:D] = v["L0_cond_cp_g"]
        g_tab[o:o + NCOMP, D:2 * D] = v["L0_cond_tm_g"]
        g_tab[o + NCOMP:o + NCOMP + NSCALE, 2 * D:3 * D] = v["L0_cond_ms_g"]
        g_tab[o + ROWS - B:o + ROWS, 3 * D:4 * D] = v["L0_cond_int_b2"]
        row_id[o:o + ROWS, 0] = [*range(NCOMP), *range(NSCALE), *range(B)]
        tab_t[:, 0:2, o:o + NCOMP] = part(v["L0_cond_cp_b"].T)
        tab_t[:, 2:4, o:o + NCOMP] = part(v["L0_cond_tm_b"].T)
        tab_t[:, 10:12, o + NCOMP:o + NCOMP + NSCALE] = part(v["L0_cond_ms_b"].T)
        b1_sel[0, o + ROWS - B:o + ROWS] = 1
    h["ids"], h["g_tab"], h["tab_t"], h["b1_sel"] = ids, g_tab, tab_t, b1_sel
    h["b1_row"] = v["L0_cond_int_b1"].reshape(1, D)
    h["w_in"] = part(v["L0_cond_int_W1"])
    h["w_out"] = part(v["L0_cond_int_W2"])
    nets = ("mem", "noi", "res")
    cond, c_w1 = _np.zeros((P, 3, B), f), _np.zeros((P, 3, D), f)
    for c, (s, n) in enumerate(zip(("cond_512", "cond_64", "fside_Bx32_0"), nets)):
        w = v[f"L0_cond_{n}_W1"]
        cond[:w.shape[0], c] = v[s].T
        c_w1[:w.shape[0], c] = w
    h["cond"], h["c_w1"] = cond.reshape(P, 3 * B), c_w1
    h["c_w2"] = _np.concatenate([part(v[f"L0_cond_{n}_W2"]) for n in nets], axis=1)
    b1 = _np.stack([v[f"L0_cond_{n}_b1"] for n in nets]).reshape(3 * DC, P).T
    h["c_b1"] = _np.repeat(b1, B, axis=1)
    vec = _np.stack([_np.concatenate([v[f"L0_cond_{n}_{k}"] for n in nets]) for k in ("b2", "g", "be")])
    h["c_vec"] = _np.broadcast_to(vec, (B, 3, 3 * D))
    h["aw"] = _np.broadcast_to(v["L0_cond_aw"], (P, 6))
    h["ln_gb"] = _np.stack([v[f"L0_cond_int_{k}"].reshape(DC, P).T for k in ("g", "be")], axis=1)
    h["wgate"] = part(v["L0_ffn_w_gate"].T)
    h["ident"] = _np.eye(P, dtype=f)
    h["before"] = _np.triu(_np.ones((P, P), f), 1)
    iota = _np.broadcast_to(_np.arange(E, dtype=f), (P, E))
    tokens = _np.arange(T, dtype=f).reshape(NTOK, P).T
    h["small"] = _np.concatenate([iota, iota * REGION, _np.ones((P, 1), f), row_id, tokens], axis=1)
    h["tile_num"] = _np.arange(NT, dtype=f).reshape(1, NT)
    pad = _np.zeros((P, ROW), f)
    pad[:, D + 1] = _np.arange(T, T + P)
    h["pad_rows"] = pad
    w1, w3, w2 = v["L0_ffn_w1"], v["L0_ffn_w3"], v["L0_ffn_w2"]
    gu = _np.stack([w1, w3], axis=1).reshape(E, 2, I, DC, P).transpose(0, 4, 3, 1, 2).reshape(E, P, 2 * DC * I)
    dn = w2.reshape(E, D, IC, P).transpose(0, 3, 2, 1).reshape(E, P, IC * D)
    h["w_exp"] = _np.concatenate([gu, dn], axis=2).transpose(1, 0, 2).reshape(P, E * WEXP)

    nc = _bacc.Bacc("TRN2", target_bir_lowering=False, num_devices=1)
    arrays, aps = {}, {}
    for name, w in h.items():
        w = _np.ascontiguousarray(w)
        arrays[f"in_{name}"] = w
        aps[name] = nc.dram_tensor(f"in_{name}", w.shape, mybir.dt.from_np(w.dtype), kind="ExternalInput").ap()
    out = nc.dram_tensor("out_rows", (T + P, D), F32, kind="ExternalOutput").ap()
    routed = nc.dram_tensor("routed_rows", (E * REGION + P, ROW), F32, kind="Internal").ap()
    adaln_moe(nc, aps, out, routed)
    r = _run(nc, [arrays], core_ids=[0])
    return r.results[0]["out_rows"][0:T].reshape(B, S, D)
```

```python
import itertools
from contextlib import ExitStack

import numpy as np
import concourse.bass as bass
from concourse import mybir

ALU = mybir.AluOpType
ACT = mybir.ActivationFunctionType
AX = mybir.AxisListType
F32 = mybir.dt.float32
BF16 = mybir.dt.bfloat16
F16 = mybir.dt.float16
I32 = mybir.dt.int32
U32 = mybir.dt.uint32

P = 128
B, S, D = 2, 1024, 256
T = B * S
NTOK = T // P
DC = D // P
E, I, K = 8, 896, 2
IC = I // P
NCOMP, NSCALE = 5, 3
ROWS = NCOMP + NSCALE + B
PARTS = 3
KR = 32 * (PARTS - 1) + ROWS
EPS = 1e-5

LEAST = K * T // P
REGION = T + P
NT = (K * T + K * (P - 1) + (E - K) * P) // P
ROW = D + 2
WEXP = 2 * DC * I + IC * D
HALF = ((0, 4), (4, IC))
EARLY = 6
PIECE = EARLY * WEXP // NTOK
UNITS = WEXP // I
SHIFT = 2
SPLIT_A = 11
SPLIT_B = 20
BESIDE = E - 1


class Tile:

    def __init__(self, pair, parity):
        self.pair, self.parity = pair, parity

    def plus(self, d):
        q = self.parity + d
        return Tile(self.pair + q // 2, q % 2)

    def at(self, scale=1, offset=0):
        return self.pair * (2 * scale) + (self.parity * scale + offset)

    def inside(self, n):
        return not isinstance(self.pair, int) or 0 <= self.at() < n

    def is_first(self, n=1):
        return isinstance(self.pair, int) and self.at() < n


class Unit:

    def __init__(self, number):
        self.number = number
        self.known = isinstance(number, int)

    def plus(self, d):
        return Unit(self.number + d)

    def at(self, scale=1, offset=0):
        return self.number * scale + offset


def pipeline(engine, body, first, last, head, tail):
    lo, hi = first + head, last - tail
    for n in range(first, lo):
        body(Tile(n // 2, n % 2))
    with engine.Fori(lo // 2, lo // 2 + (hi - lo) // 2) as pair:
        body(Tile(pair, 0).plus(lo % 2))
        body(Tile(pair, 0).plus(lo % 2 + 1))
    for n in range(hi, last):
        body(Tile(n // 2, n % 2))


def tiles_needed(engine, n, body, last=NT):
    for t in range(LEAST, last):
        with engine.If(n > t):
            body(Tile(t // 2, t % 2))


def side_by_side(*chains):
    chains = list(chains)
    while chains:
        for chain in tuple(chains):
            if next(chain, done_) is done_:
                chains.remove(chain)


done_ = object()


def adaln_moe(nc, a, out, routed):
    with ExitStack() as ctx:
        def sb(name, shape, dt=F32):
            return ctx.enter_context(nc.sbuf_tensor(name, shape, dt))

        def sem(name):
            return ctx.enter_context(nc.semaphore(name))

        ident = sb("ident", [P, P])
        before = sb("before", [P, P], BF16)
        ones = sb("ones", [P, P], BF16)
        ident_h = sb("ident_h", [P, P], F16)
        ident_l = sb("ident_l", [P, P], BF16)
        small = sb("small", [P, 2 * E + 2 + NTOK])
        iota_e = small[:, 0:E]
        region_e = small[:, E:2 * E]
        row_id = small[:, 2 * E + 1:2 * E + 2]
        token_id = small[:, 2 * E + 2:2 * E + 2 + NTOK]
        pad_rows = sb("pad_rows", [P, ROW])
        ln_gb = sb("ln_gb", [P, 2, DC])
        wgate = sb("wgate", [P, DC, E])
        pw_ids = sb("pw_ids", [P, NTOK], I32)
        pw_idx = [sb(f"pw_idx{p}", [P, 1], I32) for p in range(2)]
        minus_half = sb("minus_half", [P, NTOK])
        gates = sb("gates", [KR, 4 * D], BF16)
        shifts = sb("shifts", [KR, D], BF16)

        w_all = sb("w_all", [P, E * WEXP + SHIFT * I])
        w_hi, w_lo = w_all[:].bitcast(F16), w_all[:].bitcast(BF16)
        at = [EARLY * WEXP + SHIFT * I]

        def place(n, dt=F32):
            v = w_all[:, at[0]:at[0] + n]
            at[0] += n
            return v if dt == F32 else v.bitcast(dt)

        x_all = place(NTOK * D).rearrange("p (t d) -> p t d", d=D)
        onehot = place(T // 2, BF16)
        w_in = place(12 * D).rearrange("p (c d) -> p c d", d=D)
        w_out = place(DC * D).rearrange("p (c d) -> p c d", d=D)
        gate_s = place(3 * D)
        s1 = place(D)
        s1_t = place(D).rearrange("p (c t) -> p c t", t=P)
        y_t = place(D).rearrange("p (c t) -> p c t", t=P)
        w_x = place(DC * D).rearrange("p (c d) -> p c d", d=D)
        assert at[0] <= E * WEXP + SHIFT * I
        at[0] = PIECE * NTOK // 2 + SHIFT * I
        before_f = place(P)
        ids = place(T, I32)
        c_w1 = place(3 * D).rearrange("p (c d) -> p c d", d=D)
        c_w2 = place(6 * D).rearrange("p (c d) -> p c d", d=D)
        g_tab = place(4 * D)
        t_rest = place(4 * D)
        t_part = place(4 * D)
        tab_t = place(12 * KR).rearrange("p (c k) -> p c k", k=KR)
        c_b2 = place(3 * D)[0:B]
        c_h = place(3 * D).rearrange("p (c d) -> p c d", c=3)[0:B]
        b1_row = place(D)[0:1]
        b1_sel = place(KR)[0:1]
        assert at[0] <= EARLY * WEXP + SHIFT * I

        aw = sb("aw", [P, 6])
        aw_s = sb("aw_s", [P, 4])
        cond = sb("cond", [P, 3 * B])
        c_b1 = sb("c_b1", [P, 6 * B])
        c_sh = sb("c_sh", [P, 6 * B])
        c_gb = sb("c_gb", [P, 2, 6 * B])
        c_t = sb("c_t", [P, 6 * B])
        c_st = sb("c_st", [B, 3, 8])
        c_ve = sb("c_ve", [B, 8])
        st6 = sb("st6", [P, NTOK, 6])
        mv_x = sb("mv_x", [P, NTOK, 2])
        var_x = sb("var_x", [P, NTOK])
        rstd_x = sb("rstd_x", [P, NTOK])
        nmr_x = sb("nmr_x", [P, NTOK])

        both = sb("both", [P, 13 * D + 2 * 6 * P + 2 * K * ROW])
        used = [0]

        def share(n):
            used[0] += n
            return both[:, used[0] - n:used[0]]

        x_t = share(2 * D).rearrange("p (b c t) -> p b c t", b=2, t=P)
        pw = share(4 * D).rearrange("p (b d) -> p b d", b=2)
        xn = share(2 * D).rearrange("p (b d) -> p b d", b=2)
        an0 = share(D)
        an = share(2 * D).rearrange("p (b d) -> p b d", b=2)
        cat = share(2 * 6 * P).rearrange("p (b c t) -> p b c t", b=2, t=P)
        yn = share(2 * D).rearrange("p (b d) -> p b d", b=2)
        y_rows = share(2 * K * ROW).rearrange("p (b k r) -> p b k r", b=2, k=K)
        st_a = sb("st_a", [P, 10])
        r_a = sb("r_a", [P, 1])
        st_y = sb("st_y", [P, 10])
        r_y = sb("r_y", [P, 1])
        top = sb("top", [P, 8])
        top_i = sb("top_i", [P, 8], U32)
        oh = sb("oh", [P, K, E])
        oh_sum = sb("oh_sum", [P, 2, E], BF16)
        seen = sb("seen", [P, 2, E], BF16)
        gap = sb("gap", [P, 1])
        nm_a = sb("nm_a", [P, 1])
        nm_y = sb("nm_y", [P, 1])
        euler = sb("euler", [P, 1])
        q_ = sb("q_", [P, 1])
        den = sb("den", [P, 1])
        pos = sb("pos", [P, E])
        pos_k = sb("pos_k", [P, K, E])
        slot_f = sb("slot_f", [P, K])
        slot = [sb(f"slot{p}", [P, K], I32) for p in range(2)]


        cnt = sb("cnt", [1, E])
        cnt_i = sb("cnt_i", [1, E], I32)
        ntile = sb("ntile", [1, E])
        t_end = sb("t_end", [1, E])
        tail_i = sb("tail_i", [1, E], I32)
        t_num = sb("t_num", [1, NT])
        t_exp = sb("t_exp", [1, NT])
        t_loc = sb("t_loc", [1, NT])
        t_tmp = sb("t_tmp", [1, NT])
        tile_exp = sb("tile_exp", [1, NT], I32)
        tile_row = sb("tile_row", [1, NT], I32)
        n_tiles = sb("n_tiles", [1, 1], I32)

        used[0] = 0
        xs = share(2 * ROW).rearrange("p (b r) -> p b r", b=2)
        xf = share(D)
        xsp = share(2 * D).rearrange("p (b d) -> p b d", b=2)
        width = [(c1 - c0) * P for c0, c1 in HALF]
        sg = [share(n) for n in width]
        hh = [share(n) for n in width]
        hsp = [share(n) for n in width]
        ht = [share(n) for n in width]
        yo = share(2 * D).rearrange("p (b d) -> p b d", b=2)
        weight = sb("weight", [P, 2])
        tok = [sb(f"tok{p}", [P, 1], I32) for p in range(2)]

        bank = [ctx.enter_context(nc.psum_tensor(f"bank{n}", [P, 512], F32)) for n in range(8)]

        s_row = sem("s_row")
        s_const = sem("s_const")
        s_x = sem("s_x")
        s_x2 = sem("s_x2")
        s_ids = sem("s_ids")
        s_win = sem("s_win")
        s_tab = sem("s_tab")
        s_gtab = sem("s_gtab")
        s_cond2 = sem("s_cond2")
        s_cond = sem("s_cond")
        s_out0 = sem("s_out0")
        s_early = [sem(f"s_early{p}") for p in range(2)]
        s_late = [sem(f"s_late{e}") for e in range(EARLY, E)]
        split_hi = sem("split_hi")
        split_lo = sem("split_lo")
        split_lo_p = sem("split_lo_p")
        experts_ready = sem("experts_ready")
        s_xt = [sem(f"s_xt{p}") for p in range(2)]
        s_pw = [sem(f"s_pw{p}") for p in range(2)]
        pro_v = sem("pro_v")
        pro_a = sem("pro_a")
        pro_p = sem("pro_p")
        pro_t = sem("pro_t")
        xn_done = sem("xn_done")
        a_step = sem("a_step")
        ra_done = sem("ra_done")
        an_done = sem("an_done")
        flip_done = sem("flip_done")
        gate_mm = sem("gate_mm")
        gate_done = sem("gate_done")
        cat_done = sem("cat_done")
        in_done = sem("in_done")
        silu_done = sem("silu_done")
        s1t_mm = sem("s1t_mm")
        s1t_done = sem("s1t_done")
        out_mm = sem("out_mm")
        ly_step = sem("ly_step")
        ry_done = sem("ry_done")
        nma_done = sem("nma_done")
        nmy_done = sem("nmy_done")
        yn_done = sem("yn_done")
        row_step = sem("row_step")
        id_step = sem("id_step")
        yt_mm = sem("yt_mm")
        yt_done = sem("yt_done")
        logit_mm = sem("logit_mm")
        top_step = sem("top_step")
        q_done = sem("q_done")
        rank_mm = sem("rank_mm")
        slot_step = sem("slot_step")
        s_scat = [sem(f"s_scat{p}") for p in range(2)]
        plan_step = sem("plan_step")
        s_tail = sem("s_tail")
        s_xs = [sem(f"s_xs{p}") for p in range(2)]
        flip_x = sem("flip_x")
        xst_done = sem("xst_done")
        xhi_done = sem("xhi_done")
        xlo_done = sem("xlo_done")
        g_mm = [sem(f"g_mm{h}") for h in range(2)]
        u_mm = [sem(f"u_mm{h}") for h in range(2)]
        sg_done = [sem(f"sg_done{h}") for h in range(2)]
        h_done = [sem(f"h_done{h}") for h in range(2)]
        hi_done = [sem(f"hi_done{h}") for h in range(2)]
        lo_done = [sem(f"lo_done{h}") for h in range(2)]
        ht_mm = [sem(f"ht_mm{h}") for h in range(2)]
        ht_done = [sem(f"ht_done{h}") for h in range(2)]
        y_mm = sem("y_mm")
        meta_step = sem("meta_step")
        yo_done = sem("yo_done")
        s_add = sem("s_add")
        idx_done = sem("idx_done")
        s_pwid = sem("s_pwid")
        relay_s, relay_p, relay_v = sem("relay_s"), sem("relay_p"), sem("relay_v")

        def units_in_step(n):
            lo, hi = HEAD, NTOK + 4 - TAIL
            if not isinstance(n.pair, int) or lo <= n.at() < hi:
                return [Unit(n.pair)] if n.parity == 0 else []
            if 2 <= n.at() < lo - 1:
                return [Unit(n.at() - 2)]
            if hi <= n.at() < hi + 4:
                return [Unit(hi // 2 + n.at() - hi)]
            return []

        units_left = [Unit(u) for u in range(SPLIT_A, SPLIT_B)]

        def units_beside(t):
            if not t.is_first(BESIDE):
                return []
            first, last = (SPLIT_B + -(-(E * UNITS - SPLIT_B) * n // BESIDE) for n in (t.at(), t.at() + 1))
            assert last >= min(E, t.at() + 2) * UNITS
            return [Unit(u) for u in range(first, last)]

        def of_pool(u):
            return u.known and u.at() >= SPLIT_B and u.at() % 3 == 2

        def wait_unit(engine, u):
            pools = u.at() // 3 - SPLIT_B // 3 + (u.at() % 3 == 2) if u.known and u.at() >= SPLIT_B else 0
            if of_pool(u):
                engine.wait_ge(split_lo_p, pools)
            else:
                engine.wait_ge(split_lo, u.at(1, 1 - pools))

        NCONST = 5
        TOPN, SLOTN, LYN, AN_ = 7, 7, 3, 5

        block = ctx.enter_context(nc.Block())

        def pad_regions(engine, first):
            engine.wait_ge(plan_step, TAILS)
            for e in range(first, E, 2):
                row = engine.value_load(tail_i[0:1, e:e + 1], min_val=0, max_val=E * REGION - P)
                engine.dma_start(routed[bass.ds(row, P), :], pad_rows[:]).then_inc(s_tail, 16)

        def tile_count(engine):
            return engine.value_load(n_tiles[0:1, 0:1], min_val=LEAST, max_val=NT)

        @block.sync
        def _(sp):
            for dst, src in ((cond[:], a["cond"]), (c_b1[:], a["c_b1"]), (c_w1, a["c_w1"])):
                sp.dma_start(dst, src).then_inc(s_cond, 16)
            for dst, src in ((c_w2, a["c_w2"]), (c_b2, a["c_b2"]), (c_gb[:], a["c_gb"]), (aw[:], a["aw"]),
                             (ident[:], a["ident"])):
                sp.dma_start(dst, src).then_inc(s_cond2, 16)
            sp.dma_start(g_tab[0:KR, :], a["g_tab"]).then_inc(s_gtab, 16)
            x_tiles = a["x"].rearrange("(t p) d -> p t d", p=P)
            sp.dma_start(x_all[:, 0:FIRST], x_tiles[:, 0:FIRST]).then_inc(s_x, 16)
            sp.dma_start(w_in, a["w_in"]).then_inc(s_win, 16)
            for dst, src in ((tab_t, a["tab_t"]), (b1_row, a["b1_row"]), (b1_sel, a["b1_sel"])):
                sp.dma_start(dst, src).then_inc(s_tab, 16)
            for dst, src in ((small[:], a["small"]), (pad_rows[:], a["pad_rows"])):
                sp.dma_start(dst, src).then_inc(s_row, 16)
            sp.dma_start(ids[0:KR, :], a["ids"]).then_inc(s_ids, 16)
            sp.dma_start(x_all[:, FIRST:], x_tiles[:, FIRST:]).then_inc(s_x2, 16)
            for dst, src in ((before_f[:], a["before"]), (ln_gb[:], a["ln_gb"]), (wgate[:], a["wgate"]),
                             (t_num[:], a["tile_num"]), (w_out, a["w_out"])):
                sp.dma_start(dst, src).then_inc(s_const, 16)

            def load_tile(t):
                if not t.is_first(2):
                    sp.wait_ge(in_done, t.at(1, -1))
                    sp.sem_inc(relay_s, 1)
                sp.dma_start(x_t[:, t.parity], a["x_t"][bass.ds(t.at(P), P), :]).then_inc(s_xt[t.parity], 16)
                if not t.is_first(2):
                    sp.wait_ge(s_early[t.parity], t.pair * 16)
                    sp.sem_inc(relay_s, 1)
                sp.dma_start(w_all[:, bass.ds(t.at(PIECE, SHIFT * I), PIECE)],
                             a["w_exp"][:, bass.ds(t.at(PIECE), PIECE)]).then_inc(s_early[t.parity], 16)

            pipeline(sp, load_tile, 0, NTOK, 2, 0)

            sp.dma_start(out[0:T, :], a["x"]).then_inc(s_out0, 16)
            sp.wait_ge(s_row, 32)
            sp.dma_start(out[T:T + P, :], pad_rows[:, 0:D]).then_inc(s_out0, 16)
            sp.dma_start(routed[E * REGION:E * REGION + P, :], pad_rows[:]).then_inc(s_tail, 16)
            pad_regions(sp, 0)
            sp.wait_ge(plan_step, PLAN)
            sp.wait_ge(s_tail, 16 * (E + 1))
            for p in range(2):
                sp.wait_ge(s_scat[p], 16 * K * NTOK // 2)

            def load_xs(t):
                row = sp.value_load(tile_row[0:1, bass.ds(t.at(), 1)], min_val=0, max_val=E * REGION)
                if not t.is_first(2):
                    sp.wait_ge(flip_x, t.at(1, -1))
                    sp.wait_ge(meta_step, t.at(2, -2))
                    sp.sem_inc(relay_s, 1)
                sp.dma_start(xs[:, t.parity, :], routed[bass.ds(row, P), :]).then_inc(s_xs[t.parity], 16)

            load_xs(Tile(0, 0))
            load_xs(Tile(0, 1))
            for n in range(E - EARLY):
                c = (EARLY + n) * WEXP
                sp.dma_start(w_all[:, c + SHIFT * I:c + SHIFT * I + WEXP], a["w_exp"][:, c:c + WEXP]).then_inc(s_late[n], 16)
                load_xs(Tile(1 + n // 2, n % 2))
            pipeline(sp, load_xs, 2 + E - EARLY, LEAST + 1, 0, 1)
            n = tile_count(sp)
            tiles_needed(sp, n, lambda t: load_xs(t.plus(1)), NT - 1)
            sp.wait_ge(s_add, 16 * n)
            sp.sem_inc(relay_s, 1)

        @block.gpsimd
        def _(pool):
            nc.gpsimd.memset(minus_half[:], -0.5).then_inc(pro_p, 1)
            nc.gpsimd.memset(euler[:], float(np.e)).then_inc(pro_p, 1)
            pool.dma_start(pw_ids[:], a["pw_ids"]).then_inc(s_pwid, 16)

            def gather_pw(t):
                if not t.is_first(2):
                    pool.wait_ge(a_step, t.at(AN_, -AN_))
                    pool.sem_inc(relay_p, 1)
                nc.gpsimd.tensor_copy(pw_idx[t.parity][:], pw_ids[:, bass.ds(t.at(), 1)]).then_inc(idx_done, 1)
                pool.wait_ge(idx_done, t.at(1, 1))
                pool.sem_inc(relay_p, 1)
                nc.gpsimd.indirect_dma_start(
                    pw[:, t.parity, :], None, a["pw_tab"],
                    bass.IndirectOffsetOnAxis(ap=pw_idx[t.parity][:, 0:1], axis=0)).then_inc(s_pw[t.parity], 16)

            def power(o, base, exponent, s):
                nc.gpsimd.tensor_tensor(o, base, exponent, ALU.pow).then_inc(s, 1)

            pool.wait_ge(s_pwid, 16)
            gather_pw(Tile(0, 0))
            gather_pw(Tile(0, 1))
            pool.wait_ge(pro_p, 2)
            pool.wait_ge(pro_v, VARX)
            power(rstd_x[:, 0:FIRST], var_x[:, 0:FIRST], minus_half[:, 0:FIRST], pro_p)
            pool.wait_ge(pro_v, CVE)
            power(c_ve[:, 3:6], c_ve[:, 0:3], minus_half[0:B, 0:3], pro_p)
            pool.wait_ge(pro_a, 8)
            nc.gpsimd.tensor_tensor(w_x, w_in[:, 4:6, :], w_in[:, 6:8, :], ALU.add).then_inc(pro_p, 1)
            pool.wait_ge(pro_p, 5)
            nc.gpsimd.tensor_tensor(w_x, w_x, w_in[:, 8:10, :], ALU.add).then_inc(pro_p, 1)

            def root_a(i):
                pool.wait_ge(a_step, i.at(AN_, AN_))
                power(r_a[:], st_a[:, 8:9], minus_half[:, 0:1], ra_done)

            def root_y(i):
                pool.wait_ge(ly_step, i.at(LYN, LYN))
                power(r_y[:], st_y[:, 8:9], minus_half[:, 0:1], ry_done)

            def exp_gap(i):
                pool.wait_ge(top_step, i.at(TOPN, TOPN))
                power(q_[:], euler[:], gap[:], q_done)

            def scatter(i):
                pool.wait_ge(slot_step, i.at(SLOTN, SLOTN))
                pool.wait_ge(row_step, i.at(1, 1))
                pool.wait_ge(id_step, i.at(1, 1))
                pool.sem_inc(relay_p, 1)
                for k in range(K):
                    nc.gpsimd.indirect_dma_start(
                        routed, bass.IndirectOffsetOnAxis(ap=slot[i.parity][:, k:k + 1], axis=0),
                        y_rows[:, i.parity, k, :], None).then_inc(s_scat[i.parity], 16)

            root_a(Tile(0, 0))
            pool.wait_ge(pro_v, VARX2)
            power(rstd_x[:, FIRST:], var_x[:, FIRST:], minus_half[:, FIRST:], pro_p)

            def step(n):
                for lag, work in ((2, gather_pw), (1, root_a), (-4, scatter), (-2, root_y), (-3, exp_gap)):
                    if n.plus(lag).inside(NTOK):
                        work(n.plus(lag))

            pipeline(pool, step, 0, NTOK + 4, HEAD, TAIL)

            def add_tile(t):
                if not t.is_first(1):
                    pool.wait_ge(s_add, t.at(16))
                pool.wait_ge(yo_done, t.at(1, 1))
                pool.sem_inc(relay_p, 1)
                nc.gpsimd.indirect_dma_start(
                    out, bass.IndirectOffsetOnAxis(ap=tok[t.parity][:, 0:1], axis=0),
                    yo[:, t.parity, :], None, compute_op=ALU.add).then_inc(s_add, 16)

            def rest_of_units(units):
                for u in units:
                    if of_pool(u):
                        pool.wait_ge(split_hi, u.at(1, 1))
                        nc.gpsimd.tensor_tensor(w_lo[:, bass.ds(u.at(2 * I, I), I)], w_all[:, bass.ds(u.at(I, SHIFT * I), I)],
                                                w_hi[:, bass.ds(u.at(2 * I), I)], ALU.subtract).then_inc(split_lo_p, 1)

            def expert_step(t):
                rest_of_units(units_beside(t.plus(1)))
                add_tile(t)

            pool.wait_ge(s_out0, 32)
            rest_of_units(units_beside(Tile(0, 0)))
            pipeline(pool, expert_step, 0, LEAST, BESIDE + 1, 0)
            pool.wait_ge(plan_step, PLAN)
            tiles_needed(pool, tile_count(pool), add_tile)

        @block.scalar
        def _(act):
            act.wait_ge(pro_v, CSH)
            nc.scalar.activation(c_sh[:], c_sh[:], ACT.Silu).then_inc(pro_a, 1)
            act.wait_ge(pro_v, AWS)
            nc.scalar.activation(aw[:], aw[:], ACT.Exp).then_inc(pro_a, 1)
            act.wait_ge(pro_v, AWD)
            act.wait_ge(s_win, 16)
            for c in range(6):
                w2 = w_in[:, 2 * c:2 * c + 2, :]
                nc.scalar.activation(w2, w2, ACT.Copy, scale=aw[:, c:c + 1]).then_inc(pro_a, 1)
            act.wait_ge(pro_v, NMX)

            def norm_x(i):
                if isinstance(i.pair, int) and i.at() == FIRST:
                    act.wait_ge(pro_v, NMX2)
                if not i.is_first(2):
                    act.wait_ge(flip_done, i.at(1, -1))
                    act.wait_ge(a_step, i.at(AN_, -AN_))
                c = bass.ds(i.at(), 1)
                nc.scalar.activation(xn[:, i.parity, :], x_all[:, c, :].rearrange("p o d -> p (o d)"), ACT.Identity,
                                     bias=nmr_x[:, c], scale=rstd_x[:, c]).then_inc(xn_done, 1)

            def norm_a(i):
                act.wait_ge(nma_done, i.at(1, 1))
                if not i.is_first(2):
                    act.wait_ge(flip_done, i.at(1, -1))
                nc.scalar.activation(an[:, i.parity, :], an0, ACT.Identity, bias=nm_a[:], scale=r_a[:]).then_inc(an_done, 1)

            def copy_s1(i):
                act.wait_ge(s1t_mm, i.at(1, 1))
                nc.scalar.copy(s1_t.rearrange("p c t -> p (c t)"), bank[4][:, 0:D]).then_inc(s1t_done, 1)

            def copy_gates(i):
                act.wait_ge(gate_mm, i.at(1, 1))
                if not i.is_first():
                    act.wait_ge(cat_done, i.at(2))
                nc.scalar.copy(gate_s[:, 0:2 * D], bank[1][:, :]).then_inc(gate_done, 1)
                nc.scalar.copy(gate_s[:, 2 * D:3 * D], bank[2][:, 0:D]).then_inc(gate_done, 1)

            def affine_y(i):
                act.wait_ge(yt_mm, i.at(1, 1))
                if not i.is_first():
                    act.wait_ge(logit_mm, i.at())
                for f in range(DC):
                    nc.scalar.activation(y_t[:, f, :], bank[6][:, f * P:(f + 1) * P], ACT.Identity,
                                         bias=ln_gb[:, 1, f:f + 1], scale=ln_gb[:, 0, f:f + 1]).then_inc(yt_done, 1)

            def silu_1(i):
                act.wait_ge(in_done, i.at(1, 1))
                if not i.is_first():
                    act.wait_ge(s1t_mm, i.at())
                nc.scalar.activation(s1, bank[3][:, 0:D], ACT.Silu).then_inc(silu_done, 1)

            def norm_y(i):
                act.wait_ge(nmy_done, i.at(1, 1))
                if not i.is_first(2):
                    act.wait_ge(yt_mm, i.at(1, -1))
                nc.scalar.activation(yn[:, i.parity, :], bank[5][:, 0:D], ACT.Identity, bias=nm_y[:], scale=r_y[:]).then_inc(yn_done, 1)

            def copy_rows(i):
                act.wait_ge(yn_done, i.at(1, 1))
                if not i.is_first(2):
                    act.wait_ge(s_scat[i.parity], i.pair * (16 * K))
                for k in range(K):
                    last = nc.scalar.copy(y_rows[:, i.parity, k, 0:D], yn[:, i.parity, :])
                last.then_inc(row_step, 1)

            norm_x(Tile(0, 0))
            norm_x(Tile(0, 1))
            norm_a(Tile(0, 0))

            def round_unit(u):
                if u.known and u.at() >= EARLY * UNITS:
                    act.wait_ge(s_late[u.at() // UNITS - EARLY], 16)
                elif u.known and u.at() >= SPLIT_A:
                    for p in range(2):
                        act.wait_ge(s_early[p], 16 * NTOK // 2)
                elif u.known:
                    piece = ((u.at() + 1) * I - 1) // PIECE
                    for p in range(2):
                        if piece >= p:
                            act.wait_ge(s_early[p], 16 * ((piece - p) // 2 + 1))
                else:
                    act.wait_ge(s_early[0], u.at(16))
                    act.wait_ge(s_early[1], u.at(16, -16))
                if not (u.known and u.at() < SHIFT):
                    wait_unit(act, u.plus(-SHIFT))
                nc.scalar.copy(w_hi[:, bass.ds(u.at(2 * I), I)],
                               w_all[:, bass.ds(u.at(I, SHIFT * I), I)]).then_inc(split_hi, 1)

            def step(n):
                def alive(*works):
                    for lag, work in works:
                        if n.plus(lag).inside(NTOK):
                            work(n.plus(lag))
                alive((0, copy_gates), (-2, copy_s1), (-3, affine_y), (2, norm_x))
                for u in units_in_step(n):
                    round_unit(u)
                alive((1, norm_a), (-3, copy_rows), (-1, silu_1), (-2, norm_y))

            pipeline(act, step, 0, NTOK + 4, HEAD, TAIL)

            def silu(t, h):
                n = (HALF[h][1] - HALF[h][0]) * P
                act.wait_ge(g_mm[h], t.at(1, 1))
                if not t.is_first():
                    act.wait_ge(h_done[h], t.at())
                nc.scalar.activation(sg[h], bank[2 * h][:, 0:n], ACT.Silu).then_inc(sg_done[h], 1)

            def round_h(t, h):
                n = width[h]
                act.wait_ge(h_done[h], t.at(1, 1))
                if not t.is_first():
                    act.wait_ge(ht_mm[h], t.at())
                nc.scalar.copy(hsp[h].bitcast(F16)[:, 0:n], hh[h]).then_inc(hi_done[h], 1)

            def affine_xs(t):
                act.wait_ge(flip_x, t.at(1, 1))
                if not t.is_first():
                    act.wait_ge(xlo_done, t.at())
                for f in range(DC):
                    cols = slice(f * P, (f + 1) * P)
                    nc.scalar.activation(xf[:, cols], bank[7][:, cols], ACT.Identity, bias=ln_gb[:, 1, f:f + 1],
                                         scale=ln_gb[:, 0, f:f + 1]).then_inc(xst_done, 1)

            def round_xs(t):
                act.wait_ge(xst_done, t.at(2, 2))
                if not t.is_first(2):
                    act.wait_ge(u_mm[1], t.at(1, -1))
                nc.scalar.copy(xsp[:, t.parity].bitcast(F16)[:, 0:D], xf).then_inc(xhi_done, 1)

            def expert_step(t):
                units = iter(units_beside(t))

                def round_next(n=1):
                    for u in itertools.islice(units, n):
                        round_unit(u)

                silu(t, 0)
                round_next()
                round_h(t, 0)
                round_next()
                if not (isinstance(t.pair, int) and t.at() == NT - 1):
                    affine_xs(t.plus(1))
                    round_xs(t.plus(1))
                round_next()
                silu(t, 1)
                round_next()
                round_h(t, 1)
                round_next()

            for u in units_left[:SHIFT]:
                round_unit(u)
            pad_regions(act, 1)
            for u in units_left[SHIFT:-4]:
                round_unit(u)
            affine_xs(Tile(0, 0))
            round_xs(Tile(0, 0))
            for u in units_left[-4:]:
                round_unit(u)
            pipeline(act, expert_step, 0, LEAST, BESIDE + 1, 0)
            tiles_needed(act, tile_count(act), expert_step)

        @block.vector
        def _(dve):
            done = [0]

            def did(ins):
                done[0] += 1
                ins.then_inc(pro_v, 1)

            def after(n=None):
                dve.wait_ge(pro_v, done[0] if n is None else n)

            dve.wait_ge(s_cond, 16 * 3)
            dve.wait_ge(pro_t, 1)
            did(nc.vector.tensor_tensor(c_sh[:], bank[0][:, 0:6 * B], c_b1[:], ALU.add))
            assert done[0] == CSH, done[0]
            dve.wait_ge(s_cond2, 16 * 5)
            did(nc.vector.tensor_reduce(aw_s[:, 0:1], aw[:], AX.X, ALU.max))
            after()
            did(nc.vector.tensor_scalar(aw[:], aw[:], aw_s[:, 0:1], None, ALU.subtract))
            assert done[0] == AWS, done[0]
            did(nc.vector.memset(seen[:, 0, :], 0.0))
            did(nc.vector.memset(ones[:], 1.0))
            did(nc.vector.tensor_copy(ident_h[:], ident[:]))
            did(nc.vector.tensor_copy(ident_l[:], ident[:]))
            dve.wait_ge(pro_a, 2)
            did(nc.vector.tensor_reduce(aw_s[:, 1:2], aw[:], AX.X, ALU.add))
            after()
            did(nc.vector.reciprocal(aw_s[:, 2:3], aw_s[:, 1:2]))
            after()
            did(nc.vector.tensor_scalar(aw[:], aw[:], aw_s[:, 2:3], None, ALU.mult))
            assert done[0] == AWD, done[0]

            def stats_x(t0, t1):
                for t in range(t0, t1):
                    did(nc.vector.bn_stats(st6[:, t, :], x_all[:, t, :]))
                    if t % 3 == 0:
                        yield
                after()
                for t in range(t0, t1):
                    did(nc.vector.bn_aggr(mv_x[:, t, :], st6[:, t, :]))
                after()
                did(nc.vector.tensor_scalar(var_x[:, t0:t1], mv_x[:, t0:t1, 1], EPS, None, ALU.add))

            def bias_x(t0, t1):
                did(nc.vector.scalar_tensor_tensor(nmr_x[:, t0:t1], mv_x[:, t0:t1, 0], -1.0, rstd_x[:, t0:t1], ALU.mult, ALU.mult))

            dve.wait_ge(s_x, 16)
            side_by_side(stats_x(0, FIRST))
            assert done[0] == VARX, done[0]
            dve.wait_ge(pro_p, 3)
            bias_x(0, FIRST)
            assert done[0] == NMX, done[0]
            dve.wait_ge(pro_t, 2)
            did(nc.vector.tensor_tensor(c_h[:, 0:2, :].rearrange("b c d -> b (c d)"), bank[1][0:B, :], c_b2[:, 0:2 * D], ALU.add))
            did(nc.vector.tensor_tensor(c_h[:, 2, :], bank[2][0:B, 0:D], c_b2[:, 2 * D:3 * D], ALU.add))
            after()
            for c in range(3):
                did(nc.vector.bn_stats(c_st[:, c, 0:6], c_h[:, c, :]))
            after()
            for c in range(3):
                did(nc.vector.bn_aggr(c_st[:, c, 6:8], c_st[:, c, 0:6]))
            after()
            did(nc.vector.tensor_scalar(c_ve[:, 0:3], c_st[:, :, 7], EPS, None, ALU.add))
            assert done[0] == CVE, done[0]

            def split(table, width, stacked):
                st, rest = stacked[:, 0:width], t_rest[0:KR, 0:width]
                did(nc.vector.tensor_copy(st, table))
                yield
                after()
                did(nc.vector.tensor_tensor(rest, table, st, ALU.subtract))
                yield
                after()
                did(nc.vector.tensor_copy(st[32:64], rest[32:64]))
                did(nc.vector.tensor_copy(st[64:KR], rest[64:KR]))
                yield
                after()
                did(nc.vector.tensor_tensor(t_part[64:KR, 0:width], rest[64:KR], st[64:KR], ALU.subtract))
                yield
                after()
                did(nc.vector.tensor_copy(st[64:KR], t_part[64:KR, 0:width]))

            def conditions():
                yield
                dve.wait_ge(pro_p, 4)
                for c in range(3):
                    did(nc.vector.tensor_scalar(c_h[:, c, :], c_h[:, c, :], c_st[:, c, 6:7], c_ve[:, 3 + c:4 + c], ALU.subtract, ALU.mult))
                assert done[0] == CLN, done[0]
                yield
                yield
                dve.wait_ge(pro_t, 3)
                dve.wait_ge(s_tab, 48)
                did(nc.vector.tensor_tensor(c_t[:], bank[3][:, 0:6 * B], c_gb[:, 0, :], ALU.mult))
                yield
                after()
                for n in range(PARTS):
                    o = 32 * n + ROWS - B
                    did(nc.vector.tensor_tensor(tab_t[:, 4:10, o:o + B], c_t[:].rearrange("p (c b) -> p c b", b=B),
                                                c_gb[:, 1, :].rearrange("p (c b) -> p c b", b=B), ALU.add))
                assert done[0] == CTT, done[0]

            dve.wait_ge(s_gtab, 16)
            side_by_side(split(g_tab[0:KR, :], 4 * D, gates), conditions())
            dve.wait_ge(s_row, 32)
            dve.wait_ge(s_ids, 16)
            did(nc.vector.tensor_scalar(onehot[0:KR, :], ids[0:KR, :], row_id[0:KR, :], None, ALU.is_equal))

            def affine_a(i):
                def w(n):
                    dve.wait_ge(a_step, i.at(AN_, n))
                p = i.parity
                dve.wait_ge(xn_done, i.at(1, 1))
                dve.wait_ge(s_pw[p], i.pair * 16 + 16)
                if not i.is_first():
                    dve.wait_ge(an_done, i.at())
                nc.vector.tensor_tensor(an0, xn[:, p, :], pw[:, p, 0:D], ALU.mult).then_inc(a_step, 1)
                yield
                w(1)
                nc.vector.tensor_tensor(an0, an0, pw[:, p, D:2 * D], ALU.add).then_inc(a_step, 1)
                yield
                w(2)
                nc.vector.bn_stats(st_a[:, 0:6], an0).then_inc(a_step, 1)
                yield
                w(3)
                dve.sem_inc(relay_v, 1)
                nc.vector.bn_aggr(st_a[:, 6:8], st_a[:, 0:6]).then_inc(a_step, 1)
                yield
                w(4)
                nc.vector.tensor_scalar(st_a[:, 8:9], st_a[:, 7:8], EPS, None, ALU.add).then_inc(a_step, 1)

            def bias_a(i):
                dve.wait_ge(ra_done, i.at(1, 1))
                nc.vector.tensor_scalar(nm_a[:], st_a[:, 6:7], -1.0, r_a[:], ALU.mult, ALU.mult).then_inc(nma_done, 1)

            dve.wait_ge(s_x2, 16)
            side_by_side(affine_a(Tile(0, 0)), stats_x(FIRST, NTOK))
            assert done[0] == VARX2, done[0]
            bias_a(Tile(0, 0))
            dve.wait_ge(pro_t, 4)
            side_by_side(split(bank[4][0:KR, 0:D], D, shifts))
            assert done[0] == NMR, done[0]

            def gain(i):
                dve.wait_ge(flip_done, i.at(1, 1))
                dve.wait_ge(gate_done, i.at(2, 2))
                if not i.is_first(2):
                    dve.wait_ge(in_done, i.at(1, -1))
                c = cat[:, i.parity].rearrange("p c t -> p (c t)")
                nc.vector.tensor_tensor(c[:, 0:2 * D], gate_s[:, 0:2 * D], bank[0][:, :], ALU.mult).then_inc(cat_done, 1)
                nc.vector.tensor_tensor(c[:, 2 * D:3 * D], gate_s[:, 2 * D:3 * D], bank[0][:, D:2 * D], ALU.mult).then_inc(cat_done, 1)

            def stats_y(i):
                def w(n):
                    dve.wait_ge(ly_step, i.at(LYN, n))
                dve.wait_ge(out_mm, i.at(1, 1))
                dve.sem_inc(relay_v, 1)
                nc.vector.bn_stats(st_y[:, 0:6], bank[5][:, 0:D]).then_inc(ly_step, 1)
                yield
                w(1)
                dve.sem_inc(relay_v, 1)
                nc.vector.bn_aggr(st_y[:, 6:8], st_y[:, 0:6]).then_inc(ly_step, 1)
                yield
                w(2)
                nc.vector.tensor_scalar(st_y[:, 8:9], st_y[:, 7:8], EPS, None, ALU.add).then_inc(ly_step, 1)

            def bias_y(i):
                dve.wait_ge(ry_done, i.at(1, 1))
                if not i.is_first():
                    dve.wait_ge(yn_done, i.at())
                nc.vector.tensor_scalar(nm_y[:], st_y[:, 6:7], -1.0, r_y[:], ALU.mult, ALU.mult).then_inc(nmy_done, 1)

            def number_rows(i):
                if not i.is_first(2):
                    dve.wait_ge(s_scat[i.parity], i.pair * (16 * K))
                nc.vector.tensor_copy(y_rows[:, i.parity, :, D + 1],
                                      token_id[:, bass.ds(i.at(), 1)].broadcast_to([P, K])).then_inc(id_step, 1)

            def route(i):
                def w(n):
                    dve.wait_ge(top_step, i.at(TOPN, n))
                def s(ins):
                    ins.then_inc(top_step, 1)
                p = i.parity
                dve.wait_ge(logit_mm, i.at(1, 1))
                dve.sem_inc(relay_v, 1)
                s(nc.vector.max(top[:], bank[7][:, 0:E]))
                yield
                w(1)
                dve.sem_inc(relay_v, 1)
                s(nc.vector.max_index(top_i[:], top[:], bank[7][:, 0:E]))
                s(nc.vector.tensor_tensor(gap[:], top[:, 1:2], top[:, 0:1], ALU.subtract))
                yield
                w(2)
                for k in range(K):
                    s(nc.vector.tensor_scalar(oh[:, k, :], iota_e, top_i[:, k:k + 1], None, ALU.is_equal))
                yield
                w(5)
                if not i.is_first(2):
                    dve.wait_ge(rank_mm, i.at(1, -1))
                s(nc.vector.tensor_tensor(oh_sum[:, p, :], oh[:, 0, :], oh[:, 1, :], ALU.add))
                yield
                w(6)
                if not i.is_first():
                    dve.wait_ge(rank_mm, i.at())
                s(nc.vector.tensor_tensor(seen[:, 1 - p, :], seen[:, p, :], oh_sum[:, p, :], ALU.add))

            def slots(i):
                def w(n):
                    dve.wait_ge(slot_step, i.at(SLOTN, n))
                def s(ins):
                    ins.then_inc(slot_step, 1)
                p = i.parity
                dve.wait_ge(rank_mm, i.at(1, 1))
                dve.wait_ge(q_done, i.at(1, 1))
                s(nc.vector.tensor_scalar(den[:], q_[:], 1.0, None, ALU.add))
                s(nc.vector.tensor_tensor(pos[:], bank[7][:, 0:E], region_e, ALU.add))
                yield
                w(1)
                s(nc.vector.reciprocal(y_rows[:, p, 0, D:D + 1], den[:]))
                w(2)
                for k in range(K):
                    s(nc.vector.tensor_tensor_reduce(out=pos_k[:, k, :], in0=pos[:], in1=oh[:, k, :], scale=1.0, scalar=0.0,
                                                     op0=ALU.mult, op1=ALU.add, accum_out=slot_f[:, k:k + 1]))
                yield
                w(3)
                s(nc.vector.tensor_tensor(y_rows[:, p, 1, D:D + 1], q_[:], y_rows[:, p, 0, D:D + 1], ALU.mult))
                yield
                w(5)
                s(nc.vector.tensor_copy(slot[p][:], slot_f[:]))

            def rest_of_unit(u):
                if of_pool(u):
                    return
                dve.wait_ge(split_hi, u.at(1, 1))
                nc.vector.tensor_tensor(w_lo[:, bass.ds(u.at(2 * I, I), I)], w_all[:, bass.ds(u.at(I, SHIFT * I), I)],
                                        w_hi[:, bass.ds(u.at(2 * I), I)], ALU.subtract).then_inc(split_lo, 1)

            def step(n):
                def alive(*work):
                    return [f(n.plus(lag)) for lag, f in work if n.plus(lag).inside(NTOK)]
                side_by_side(*alive((1, affine_a), (-4, slots)))
                alive((0, gain), (1, bias_a), (-3, number_rows))
                side_by_side(*alive((-2, stats_y), (-3, route)))
                alive((-2, bias_y))
                for u in units_in_step(n.plus(-1)):
                    rest_of_unit(u)
                if n.is_first():
                    dve.wait_ge(s_const, 16 * NCONST)
                    did(nc.vector.tensor_copy(before[:], before_f[:]))
                    dve.wait_ge(pro_p, 7)
                    bias_x(FIRST, NTOK)
                    assert done[0] == NMX2, done[0]

            pipeline(dve, step, 0, NTOK + 4, HEAD, TAIL)
            planned = [0]

            def plan(ins):
                planned[0] += 1
                ins.then_inc(plan_step, 1)
                dve.wait_ge(plan_step, planned[0])

            dve.wait_ge(rank_mm, NTOK + 1)
            plan(nc.vector.tensor_copy(cnt[:], bank[7][0:1, 0:E]))
            plan(nc.vector.tensor_tensor(tail_i[:], cnt[:], region_e[0:1, :], ALU.add))
            assert planned[0] == TAILS
            plan(nc.vector.tensor_scalar(cnt_i[:], cnt[:], float(P - 1), float(P), ALU.add, ALU.max))
            plan(nc.vector.tensor_scalar(cnt_i[:], cnt_i[:], 7, None, ALU.logical_shift_right))
            plan(nc.vector.tensor_copy(ntile[:], cnt_i[:]))
            plan(nc.vector.tensor_tensor_scan(t_end[:], ones[0:1, 0:E], ntile[:], 0.0, ALU.mult, ALU.add))
            ended, tiles = (gate_s[0:1, n * E * NT:(n + 1) * E * NT].rearrange("o (t e) -> o t e", e=E) for n in range(2))
            plan(nc.vector.tensor_tensor(ended, t_num[:, :, None].broadcast_to([1, NT, E]),
                                         t_end[:, None, :].broadcast_to([1, NT, E]), ALU.is_ge))
            plan(nc.vector.tensor_tensor(tiles, ended, ntile[:, None, :].broadcast_to([1, NT, E]), ALU.mult))
            plan(nc.vector.tensor_reduce(t_exp[:], ended, AX.X, ALU.add))
            plan(nc.vector.tensor_reduce(t_loc[:], tiles, AX.X, ALU.add))
            plan(nc.vector.tensor_tensor(t_loc[:], t_num[:], t_loc[:], ALU.subtract))
            plan(nc.vector.tensor_scalar(t_tmp[:], t_exp[:], float(REGION), None, ALU.mult))
            plan(nc.vector.scalar_tensor_tensor(t_loc[:], t_loc[:], float(P), t_tmp[:], ALU.mult, ALU.add))
            plan(nc.vector.tensor_scalar(tile_row[:], t_loc[:], float(E * REGION), None, ALU.min))
            plan(nc.vector.tensor_scalar(tile_exp[:], t_exp[:], float(E - 1), None, ALU.min))
            plan(nc.vector.tensor_copy(n_tiles[:], t_end[:, E - 1:E]))
            assert planned[0] == PLAN, planned[0]
            dve.wait_ge(split_lo, UNITS)
            dve.sem_inc(experts_ready, 1)
            for u in units_left[:-4]:
                rest_of_unit(u)

            def rest_of_xs(t):
                dve.wait_ge(xhi_done, t.at(1, 1))
                halves = xsp[:, t.parity]
                nc.vector.tensor_tensor(halves.bitcast(BF16)[:, D:2 * D], xf, halves.bitcast(F16)[:, 0:D],
                                        ALU.subtract).then_inc(xlo_done, 1)

            def hidden(t, h):
                dve.wait_ge(u_mm[h], t.at(1, 1))
                dve.wait_ge(sg_done[h], t.at(1, 1))
                if not t.is_first():
                    dve.wait_ge(lo_done[h], t.at())
                nc.vector.tensor_tensor(hh[h], sg[h], bank[2 * h + 1][:, 0:width[h]], ALU.mult).then_inc(h_done[h], 1)

            def rest_of_h(t, h):
                n = width[h]
                dve.wait_ge(hi_done[h], t.at(1, 1))
                nc.vector.tensor_tensor(hsp[h].bitcast(BF16)[:, n:2 * n], hh[h], hsp[h].bitcast(F16)[:, 0:n],
                                        ALU.subtract).then_inc(lo_done[h], 1)

            def copy_ht(t, h):
                dve.wait_ge(ht_mm[h], t.at(1, 1))
                if not t.is_first():
                    dve.wait_ge(y_mm, t.at())
                nc.vector.tensor_copy(ht[h].bitcast(I32), bank[4 + h][:, 0:width[h]].bitcast(I32)).then_inc(ht_done[h], 1)

            def meta(t):
                p = t.parity
                if not t.is_first(2):
                    dve.wait_ge(s_add, t.at(16, -16))
                nc.vector.tensor_copy(tok[p][:], xs[:, p, D + 1:D + 2]).then_inc(meta_step, 1)
                nc.vector.tensor_copy(weight[:, p:p + 1], xs[:, p, D:D + 1]).then_inc(meta_step, 1)

            def weigh(t):
                p = t.parity
                dve.wait_ge(y_mm, t.at(1, 1))
                dve.wait_ge(meta_step, t.at(2, 2))
                nc.vector.tensor_scalar(yo[:, p, :], bank[6][:, 0:D], weight[:, p:p + 1], None, ALU.mult).then_inc(yo_done, 1)

            def expert_step(t):
                units = units_beside(t)
                hidden(t, 0)
                for u in units[0:1]:
                    rest_of_unit(u)
                if not t.is_first():
                    copy_ht(t.plus(-1), 1)
                rest_of_h(t, 0)
                for u in units[1:2]:
                    rest_of_unit(u)
                if not (isinstance(t.pair, int) and t.at() == NT - 1):
                    rest_of_xs(t.plus(1))
                for u in units[2:3]:
                    rest_of_unit(u)
                meta(t)
                hidden(t, 1)
                for u in units[3:4]:
                    rest_of_unit(u)
                if not t.is_first():
                    weigh(t.plus(-1))
                rest_of_h(t, 1)
                for u in units[4:]:
                    rest_of_unit(u)
                copy_ht(t, 0)
                for u in units:
                    if u.at() % UNITS == UNITS - 1:
                        wait_unit(dve, u.plus(-1))
                        wait_unit(dve, u)
                        dve.sem_inc(experts_ready, 1)

            rest_of_xs(Tile(0, 0))
            for u in units_left[-4:]:
                rest_of_unit(u)
            ready = SPLIT_B // UNITS
            for u in range(ready * UNITS - 2, ready * UNITS):
                wait_unit(dve, Unit(u))
            dve.sem_inc(experts_ready, ready - 1)
            pipeline(dve, expert_step, 0, LEAST, BESIDE + 1, 0)
            n = tile_count(dve)
            tiles_needed(dve, n, expert_step)
            for t in range(LEAST - 1, NT):
                with dve.If(n == t + 1):
                    copy_ht(Tile(t // 2, t % 2), 1)
                    weigh(Tile(t // 2, t % 2))

        @block.tensor
        def _(pe):
            mm = nc.tensor.matmul
            pe.wait_ge(s_cond, 16 * 3)
            for c in range(3):
                for f in range(DC):
                    o = (c * DC + f) * B
                    last = mm(bank[0][:, o:o + B], c_w1[:, c, f * P:(f + 1) * P], cond[:, c * B:(c + 1) * B],
                              start=True, stop=True)
            last.then_inc(pro_t, 1)
            pe.wait_ge(pro_a, 1)
            pe.wait_ge(s_cond2, 16 * 5)
            for c in range(3):
                for f in range(DC):
                    o = (c * DC + f) * B
                    last = mm(bank[1 + c // 2][0:B, (c % 2) * D:(c % 2 + 1) * D], c_sh[:, o:o + B],
                              c_w2[:, c * DC + f, :], start=(f == 0), stop=(f == DC - 1))
            last.then_inc(pro_t, 1)
            pe.wait_ge(pro_v, CLN)
            for c in range(3):
                for f in range(DC):
                    o = (c * DC + f) * B
                    last = nc.tensor.transpose(bank[3][:, o:o + B], c_h[:, c, f * P:(f + 1) * P], ident[0:B, 0:B])
            last.then_inc(pro_t, 1)
            pe.wait_ge(s_tab, 48)
            pe.wait_ge(pro_a, 8)
            shift = bank[4][0:KR, 0:D]
            mm(shift, b1_sel[:], b1_row[:], start=True, stop=False)
            for c in (0, 1, 2, 3, 10, 11):
                mm(shift, tab_t[:, c, :], w_in[:, c, :], start=False, stop=False)
            pe.wait_ge(pro_v, CTT)
            for c in range(4, 10):
                last = mm(shift, tab_t[:, c, :], w_in[:, c, :], start=False, stop=(c == 9))
            last.then_inc(pro_t, 1)

            def flip(i):
                p = i.parity
                pe.wait_ge(an_done, i.at(1, 1))
                pe.wait_ge(xn_done, i.at(1, 1))
                if not i.is_first():
                    pe.wait_ge(cat_done, i.at(2))
                    pe.wait_ge(gate_done, i.at(2))
                for n, src in enumerate((an, an, xn, xn)):
                    f = n % DC
                    last = nc.tensor.transpose(bank[0][:, n * P:(n + 1) * P], src[:, p, f * P:(f + 1) * P], ident[:])
                last.then_inc(flip_done, 1)
                cols = onehot[0:KR, bass.ds(i.at(P), P)]
                for n in range(6):
                    b, o = (bank[1], n) if n < 4 else (bank[2], n - 4)
                    last = mm(b[:, o * P:(o + 1) * P], gates[:, n * P:(n + 1) * P], cols, start=True, stop=True)
                last.then_inc(gate_mm, 1)

            def integrate(i):
                p = i.parity
                pe.wait_ge(cat_done, i.at(2, 2))
                if i.is_first():
                    pe.wait_ge(pro_v, NMR)
                    pe.wait_ge(pro_p, 6)
                    pe.wait_ge(s_const, 16 * NCONST)
                if not i.is_first():
                    pe.wait_ge(silu_done, i.at())
                pe.wait_ge(s_xt[p], i.pair * 16 + 16)
                o = bank[3][:, 0:D]
                mm(o, onehot[0:KR, bass.ds(i.at(P), P)], shifts[:], start=True, stop=False)
                for f in range(DC):
                    mm(o, x_t[:, p, f, :], w_x[:, f, :], start=False, stop=False)
                yield
                for n, c in enumerate((0, 1, 2, 3, 10, 11)):
                    last = mm(o, cat[:, p, n, :], w_in[:, c, :], start=False, stop=(n == 5))
                    if n == 1:
                        yield
                last.then_inc(in_done, 1)

            def flip_s(i):
                pe.wait_ge(silu_done, i.at(1, 1))
                if not i.is_first():
                    pe.wait_ge(s1t_done, i.at())
                for f in range(DC):
                    last = nc.tensor.transpose(bank[4][:, f * P:(f + 1) * P], s1[:, f * P:(f + 1) * P], ident[:])
                last.then_inc(s1t_mm, 1)

            def flip_y(i):
                pe.wait_ge(yn_done, i.at(1, 1))
                if not i.is_first():
                    pe.wait_ge(yt_done, i.at(2))
                for f in range(DC):
                    last = nc.tensor.transpose(bank[6][:, f * P:(f + 1) * P], yn[:, i.parity, f * P:(f + 1) * P], ident[:])
                last.then_inc(yt_mm, 1)

            def project(i):
                pe.wait_ge(s1t_done, i.at(1, 1))
                if not i.is_first():
                    pe.wait_ge(yn_done, i.at())
                o = bank[5][:, 0:D]
                mm(o, onehot[0:KR, bass.ds(i.at(P), P)], gates[:, 3 * D:4 * D], start=True, stop=False)
                for f in range(DC):
                    last = mm(o, s1_t[:, f, :], w_out[:, f, :], start=False, stop=(f == DC - 1))
                last.then_inc(out_mm, 1)

            def logits(i):
                pe.wait_ge(yt_done, i.at(2, 2))
                if not i.is_first():
                    pe.wait_ge(slot_step, i.at(SLOTN))
                for f in range(DC):
                    last = mm(bank[7][:, 0:E], y_t[:, f, :], wgate[:, f, :], start=(f == 0), stop=(f == DC - 1))
                last.then_inc(logit_mm, 1)

            def rank(i):
                p = i.parity
                pe.wait_ge(top_step, i.at(TOPN, TOPN))
                mm(bank[7][:, 0:E], before[:], oh_sum[:, p, :], start=True, stop=False)
                mm(bank[7][:, 0:E], ones[:], seen[:, p, :], start=False, stop=True).then_inc(rank_mm, 1)

            def step(n):
                def alive(*works):
                    for lag, work in works:
                        if n.plus(lag).inside(NTOK):
                            work(n.plus(lag))
                alive((0, flip), (-4, rank), (-2, flip_s), (-3, flip_y))
                inner = integrate(n.plus(-1)) if n.plus(-1).inside(NTOK) else iter(())
                next(inner, done_)
                alive((-2, project))
                next(inner, done_)
                alive((-3, logits))
                next(inner, done_)

            pipeline(pe, step, 0, NTOK + 4, HEAD, TAIL)
            pe.wait_ge(slot_step, SLOTN * NTOK)
            mm(bank[7][:, 0:E], ones[:], seen[:, NTOK % 2, :], start=True, stop=True).then_inc(rank_mm, 1)

            pe.wait_ge(plan_step, PLAN)

            def expert_of(t):
                return pe.value_load(tile_exp[0:1, bass.ds(t.at(), 1)], min_val=0, max_val=E - 1)

            def products(o, x_hi, x_lo, e, unit, start, n, first, last):
                def w(v, half):
                    return v[:, bass.ds(e * (2 * WEXP) + (2 * unit + half) * I + start, n)]
                mm(o, x_hi, w(w_hi, 0), start=first, stop=False)
                mm(o, x_hi, w(w_lo, 1), start=False, stop=False)
                return mm(o, x_lo, w(w_hi, 0), start=False, stop=last)

            def flip_in(t):
                pe.wait_ge(s_xs[t.parity], t.pair * 16 + 16)
                if not t.is_first():
                    pe.wait_ge(xst_done, t.at(2))
                for f in range(DC):
                    last = nc.tensor.transpose(bank[7][:, f * P:(f + 1) * P], xs[:, t.parity, f * P:(f + 1) * P], ident[:])
                last.then_inc(flip_x, 1)

            def gate_up(t, e, h):
                c0, c1 = HALF[h]
                n = (c1 - c0) * P
                halves = xsp[:, t.parity]
                if h == 0:
                    pe.wait_ge(xlo_done, t.at(1, 1))
                for m, (s_free, s_full) in enumerate(((sg_done[h], g_mm[h]), (h_done[h], u_mm[h]))):
                    if not t.is_first():
                        pe.wait_ge(s_free, t.at())
                    for f in range(DC):
                        last = products(bank[2 * h + m][:, 0:n], halves.bitcast(F16)[:, f * P:(f + 1) * P],
                                        halves.bitcast(BF16)[:, D + f * P:D + (f + 1) * P],
                                        e, f * 2 + m, c0 * P, n, f == 0, f == DC - 1)
                    last.then_inc(s_full, 1)

            def flip_h(t, h):
                c0, c1 = HALF[h]
                pe.wait_ge(hi_done[h], t.at(1, 1))
                pe.wait_ge(lo_done[h], t.at(1, 1))
                if not t.is_first():
                    pe.wait_ge(ht_done[h], t.at())
                n = c1 - c0
                for dt, unit, chunks in ((F16, ident_h, range(n)), (BF16, ident_l, range(n, 2 * n))):
                    for c in chunks:
                        cols = slice(c * P, (c + 1) * P)
                        last = nc.tensor.transpose(bank[4 + h][:, 0:width[h]].bitcast(dt)[:, cols],
                                                   hsp[h].bitcast(dt)[:, cols], unit[:])
                last.then_inc(ht_mm[h], 1)

            def down(t, e, h):
                c0, c1 = HALF[h]
                pe.wait_ge(ht_done[h], t.at(1, 1))
                if h == 0 and not t.is_first():
                    pe.wait_ge(yo_done, t.at())
                n = c1 - c0
                for c in range(c0, c1):
                    hi = ht[h].bitcast(F16)[:, (c - c0) * P:(c - c0 + 1) * P]
                    lo = ht[h].bitcast(BF16)[:, (n + c - c0) * P:(n + c - c0 + 1) * P]
                    done = 0
                    while done < D:
                        unit, start = divmod(c * D + done, I)
                        part = min(D - done, I - start)
                        last = products(bank[6][:, done:done + part], hi, lo, e, 2 * DC + unit, start, part,
                                        c == 0, c == IC - 1)
                        done += part
                if h == 1:
                    last.then_inc(y_mm, 1)

            def expert_step(t):
                before_t = t.plus(-1)
                e = expert_of(t)
                pe.wait_ge(experts_ready, e + 1)
                gate_up(t, e, 0)
                if not t.is_first():
                    e_b = expert_of(before_t)
                    flip_h(before_t, 1)
                    down(before_t, e_b, 0)
                if not (isinstance(t.pair, int) and t.at() == NT - 1):
                    flip_in(t.plus(1))
                gate_up(t, e, 1)
                if not t.is_first():
                    down(before_t, e_b, 1)
                flip_h(t, 0)

            flip_in(Tile(0, 0))
            pipeline(pe, expert_step, 0, LEAST, 2, 0)
            n = tile_count(pe)
            tiles_needed(pe, n, expert_step)
            for i in range(LEAST - 1, NT):
                with pe.If(n == i + 1):
                    t = Tile(i // 2, i % 2)
                    e = expert_of(t)
                    flip_h(t, 1)
                    down(t, e, 0)
                    down(t, e, 1)


FIRST = 4
CSH = 1
AWS = CSH + 2
AWD = AWS + 4 + 3
VARX = AWD + 2 * FIRST + 1
NMX = VARX + 1
CVE = NMX + 2 + 3 + 3 + 1
CLN = CVE + 2 + 3
CTT = CLN + 3 + 1 + 1 + PARTS
VARX2 = CTT + 1 + 2 * (NTOK - FIRST) + 1
NMR = VARX2 + 6
NMX2 = NMR + 1 + 1
HEAD, TAIL = 6, 6
TAILS = 2
PLAN = TAILS + 14


def kernel(**v):
    import numpy as _np
    import concourse.bacc as _bacc
    from concourse.bass_utils import run_bass_kernel_spmd as _run

    v = {k: _np.asarray(x) for k, x in v.items()}
    f = _np.float32

    def part(w):
        return w.reshape(-1, P, w.shape[-1]).transpose(1, 0, 2)

    h = {}
    x = v["x"].reshape(T, D)
    h["x"] = x
    h["x_t"] = x.reshape(NTOK, P, DC, P).transpose(0, 3, 2, 1).reshape(NTOK * P, DC * P)
    h["pw_tab"] = _np.concatenate([v["L0_cond_pw_g"], v["L0_cond_pw_b"]], axis=1)
    h["pw_ids"] = v["itok_BxS_0_999"].reshape(NTOK, P).T
    comp, scale = v["itok_BxS_0_4"].reshape(T), v["mask_BxS_ik0"].reshape(T)
    ids = _np.full((KR, T), -1, _np.int32)
    g_tab = _np.zeros((KR, 4 * D), f)
    row_id = _np.zeros((P, 1), f)
    tab_t = _np.zeros((P, 12, KR), f)
    b1_sel = _np.zeros((1, KR), f)
    for n in range(PARTS):
        o = 32 * n
        ids[o:o + NCOMP] = comp
        ids[o + NCOMP:o + NCOMP + NSCALE] = scale
        ids[o + ROWS - B:o + ROWS] = _np.repeat(_np.arange(B, dtype=_np.int32), S)
        g_tab[o:o + NCOMP, 0:D] = v["L0_cond_cp_g"]
        g_tab[o:o + NCOMP, D:2 * D] = v["L0_cond_tm_g"]
        g_tab[o + NCOMP:o + NCOMP + NSCALE, 2 * D:3 * D] = v["L0_cond_ms_g"]
        g_tab[o + ROWS - B:o + ROWS, 3 * D:4 * D] = v["L0_cond_int_b2"]
        row_id[o:o + ROWS, 0] = [*range(NCOMP), *range(NSCALE), *range(B)]
        tab_t[:, 0:2, o:o + NCOMP] = part(v["L0_cond_cp_b"].T)
        tab_t[:, 2:4, o:o + NCOMP] = part(v["L0_cond_tm_b"].T)
        tab_t[:, 10:12, o + NCOMP:o + NCOMP + NSCALE] = part(v["L0_cond_ms_b"].T)
        b1_sel[0, o + ROWS - B:o + ROWS] = 1
    h["ids"], h["g_tab"], h["tab_t"], h["b1_sel"] = ids, g_tab, tab_t, b1_sel
    h["b1_row"] = v["L0_cond_int_b1"].reshape(1, D)
    h["w_in"] = part(v["L0_cond_int_W1"])
    h["w_out"] = part(v["L0_cond_int_W2"])
    nets = ("mem", "noi", "res")
    cond, c_w1 = _np.zeros((P, 3, B), f), _np.zeros((P, 3, D), f)
    for c, (s, n) in enumerate(zip(("cond_512", "cond_64", "fside_Bx32_0"), nets)):
        w = v[f"L0_cond_{n}_W1"]
        cond[:w.shape[0], c] = v[s].T
        c_w1[:w.shape[0], c] = w
    h["cond"], h["c_w1"] = cond.reshape(P, 3 * B), c_w1
    h["c_w2"] = _np.concatenate([part(v[f"L0_cond_{n}_W2"]) for n in nets], axis=1)
    b1 = _np.stack([v[f"L0_cond_{n}_b1"] for n in nets]).reshape(3 * DC, P).T
    h["c_b1"] = _np.repeat(b1, B, axis=1)
    h["c_b2"] = _np.broadcast_to(_np.concatenate([v[f"L0_cond_{n}_b2"] for n in nets]), (B, 3 * D))
    gb = [_np.stack([v[f"L0_cond_{n}_{k}"] for n in nets]).reshape(3 * DC, P).T for k in ("g", "be")]
    h["c_gb"] = _np.repeat(_np.stack(gb, axis=1), B, axis=2)
    h["aw"] = _np.broadcast_to(v["L0_cond_aw"], (P, 6))
    h["ln_gb"] = _np.stack([v[f"L0_cond_int_{k}"].reshape(DC, P).T for k in ("g", "be")], axis=1)
    h["wgate"] = part(v["L0_ffn_w_gate"].T)
    h["ident"] = _np.eye(P, dtype=f)
    h["before"] = _np.triu(_np.ones((P, P), f), 1)
    iota = _np.broadcast_to(_np.arange(E, dtype=f), (P, E))
    tokens = _np.arange(T, dtype=f).reshape(NTOK, P).T
    h["small"] = _np.concatenate([iota, iota * REGION, _np.ones((P, 1), f), row_id, tokens], axis=1)
    h["tile_num"] = _np.arange(NT, dtype=f).reshape(1, NT)
    pad = _np.zeros((P, ROW), f)
    pad[:, D + 1] = _np.arange(T, T + P)
    h["pad_rows"] = pad
    w1, w3, w2 = v["L0_ffn_w1"], v["L0_ffn_w3"], v["L0_ffn_w2"]
    gu = _np.stack([w1, w3], axis=1).reshape(E, 2, I, DC, P).transpose(0, 4, 3, 1, 2).reshape(E, P, 2 * DC * I)
    dn = w2.reshape(E, D, IC, P).transpose(0, 3, 2, 1).reshape(E, P, IC * D)
    h["w_exp"] = _np.concatenate([gu, dn], axis=2).transpose(1, 0, 2).reshape(P, E * WEXP)

    nc = _bacc.Bacc("TRN2", target_bir_lowering=False, num_devices=1)
    arrays, aps = {}, {}
    for name, w in h.items():
        w = _np.ascontiguousarray(w)
        arrays[f"in_{name}"] = w
        aps[name] = nc.dram_tensor(f"in_{name}", w.shape, mybir.dt.from_np(w.dtype), kind="ExternalInput").ap()
    out = nc.dram_tensor("out_rows", (T + P, D), F32, kind="ExternalOutput").ap()
    routed = nc.dram_tensor("routed_rows", (E * REGION + P, ROW), F32, kind="Internal").ap()
    adaln_moe(nc, aps, out, routed)
    r = _run(nc, [arrays], core_ids=[0])
    return r.results[0]["out_rows"][0:T].reshape(B, S, D)
```
